# Optimizing a Trainium2 kernel written in Bass

```python
import numpy as np
import jax
import jax.numpy as jnp

def _softmax(x, axis=-1):
    return jax.nn.softmax(x, axis=axis)

def _gelu(x):
    return jax.nn.gelu(x, approximate=True)

def _silu(x):
    return jax.nn.silu(x)

def _sigmoid(x):
    return jax.nn.sigmoid(x)

def _layernorm(x, axis=-1, eps=1e-05):
    m = jnp.mean(x, axis=axis, keepdims=True)
    v = jnp.var(x, axis=axis, keepdims=True)
    return (x - m) / jnp.sqrt(v + eps)

def _scatter_add(tgt, idx, src, axis=0):
    return tgt.at[idx].add(src)

def _segment_sum(src, seg, n):
    return jax.ops.segment_sum(src, seg, n)
kernel_name = 'mk_decoder_preln_d2_seqx_r8_66e777'

def setup_inputs(seed: int=0):
    np.random.seed(seed)
    _w = jnp.asarray

    def _rec_inputs():
        import jax
        import jax.numpy as jnp
        _rk = jax.random.key(seed)
        x = -0.0002928 + 1 * jax.random.normal(jax.random.fold_in(_rk, 1), (16, 128, 128), jnp.float32)
        _lenS = 128 - jax.random.randint(jax.random.fold_in(_rk, 7), (16,), 0, max(1, 128 // 4) + 1, jnp.int32)
        _lenS2 = 128 - jax.random.randint(jax.random.fold_in(_rk, 8), (16,), 0, max(1, 128 // 4) + 1, jnp.int32)
        _ctx_1024P = jax.random.normal(jax.random.fold_in(_rk, 11), (16, 16, 128), jnp.float32)
        _ctx_1024c = jax.random.dirichlet(jax.random.fold_in(_rk, 511), 0.3 * jnp.ones((16,), jnp.float32), (16, 128))
        _ctx_1024t = jnp.einsum('bsk,bkd->bsd', _ctx_1024c, _ctx_1024P)
        _ctx_1024t = _ctx_1024t * jax.lax.rsqrt(jnp.mean(jnp.square(_ctx_1024t)) + 1e-12) * 0.953939
        ctx_1024 = -1.39393e-06 + 0.999914 * (_ctx_1024t + 0.3 * jax.random.normal(jax.random.fold_in(_rk, 611), (16, 128, 128), jnp.float32))
        return (x, ctx_1024)
    x, ctx_1024 = _rec_inputs()

    def _L0_attn_setup():
        import jax, jax.numpy as jnp
        import numpy as np
        import math
        DIM = 128
        key = jax.random.key(seed)
        ks = jax.random.split(key, 9)
        s = 1.0 / math.sqrt(DIM)
        x = jax.random.normal(ks[0], (4, 256, DIM), dtype=jnp.float32)

        def lin(kw, kb):
            W = jax.random.uniform(kw, (DIM, DIM), minval=-s, maxval=s, dtype=jnp.float32)
            b = jax.random.uniform(kb, (DIM,), minval=-s, maxval=s, dtype=jnp.float32)
            return (W, b)
        Wq, bq = lin(ks[1], ks[2])
        Wk, bk = lin(ks[3], ks[4])
        Wv, bv = lin(ks[5], ks[6])
        Wo, bo = lin(ks[7], ks[8])
        return {'x': x, 'Wq': Wq, 'bq': bq, 'Wk': Wk, 'bk': bk, 'Wv': Wv, 'bv': bv, 'Wo': Wo, 'bo': bo}
    _L0_attn_all = _L0_attn_setup()
    _L0_attn_in = {k: v for k, v in _L0_attn_all.items() if k in ('Wq', 'bq', 'Wk', 'bk', 'Wv', 'bv', 'Wo', 'bo')}
    del _L0_attn_all

    def _L0_xattn_setup():
        import math
        import jax, jax.numpy as jnp
        import numpy as np
        B, T, D, H = (2, 256, 128, 16)
        HD = D // H
        key = jax.random.key(seed)
        ks = jax.random.split(key, 7)
        s = 1.0 / math.sqrt(D)
        return {'q': jax.random.normal(ks[0], (B, T, D), jnp.float32), 'k': jax.random.normal(ks[1], (B, T, D), jnp.float32), 'v': jax.random.normal(ks[2], (B, T, D), jnp.float32), 'Wq': jax.random.normal(ks[3], (D, D), jnp.float32) * s, 'Wk': jax.random.normal(ks[4], (D, D), jnp.float32) * s, 'Wv': jax.random.normal(ks[5], (D, D), jnp.float32) * s, 'Wo': jax.random.normal(ks[6], (D, D), jnp.float32) * s}
    _L0_xattn_all = _L0_xattn_setup()
    _L0_xattn_in = {k: v for k, v in _L0_xattn_all.items() if k in ('Wq', 'Wk', 'Wv', 'Wo')}
    del _L0_xattn_all

    def _L0_ffn_setup():
        import jax, jax.numpy as jnp
        import numpy as np
        D_MODEL = 128
        N_HEADS = 16
        HEAD_DIM = D_MODEL // N_HEADS
        FFN_DIM = 512
        N_EXPERTS = 8
        TOP_K = 2
        BATCH = 4
        SEQ = 128

        def _layernorm(x, w, b, eps=1e-05):
            mu = jnp.mean(x, axis=-1, keepdims=True)
            var = jnp.mean(jnp.square(x - mu), axis=-1, keepdims=True)
            return (x - mu) * jax.lax.rsqrt(var + eps) * w + b

        def _causal_attention(nx, Wqkv, bqkv, Wo, bo):
            B, S, D = nx.shape
            qkv = nx @ Wqkv + bqkv
            q, k, v = jnp.split(qkv, 3, axis=-1)
            q = q.reshape(B, S, N_HEADS, HEAD_DIM)
            k = k.reshape(B, S, N_HEADS, HEAD_DIM)
            v = v.reshape(B, S, N_HEADS, HEAD_DIM)
            scores = jnp.einsum('bqhd,bkhd->bhqk', q, k) / jnp.sqrt(jnp.float32(HEAD_DIM))
            causal = jnp.tril(jnp.ones((S, S), bool))
            scores = jnp.where(causal, scores, jnp.finfo(scores.dtype).min)
            attn = jax.nn.softmax(scores, axis=-1)
            out = jnp.einsum('bhqk,bkhd->bqhd', attn, v).reshape(B, S, D)
            return out @ Wo + bo

        def _moe_ffn(nx, gate_W, fc1_w, fc1_b, fc2_w, fc2_b):
            gate_logits = nx @ gate_W
            topk_vals, topk_idx = jax.lax.top_k(gate_logits, TOP_K)
            gate_w = jax.nn.softmax(topk_vals, axis=-1)
            dense_gates = jnp.sum(jax.nn.one_hot(topk_idx, N_EXPERTS, dtype=nx.dtype) * gate_w[..., None], axis=-2)
            moe_out = jnp.zeros_like(nx)
            for e in range(N_EXPERTS):
                h = jax.nn.gelu(jnp.einsum('bsd,fd->bsf', nx, fc1_w[e]) + fc1_b[e], approximate=False)
                y = jnp.einsum('bsf,df->bsd', h, fc2_w[e]) + fc2_b[e]
                moe_out = moe_out + y * dense_gates[..., e:e + 1]
            return moe_out
        key = jax.random.key(seed)
        ks = jax.random.split(key, 12)
        s = lambda k, shape, scale: jax.random.normal(k, shape, dtype=jnp.float32) * scale
        inp = {'x': s(ks[0], (BATCH, SEQ, D_MODEL), 1.0), 'ln1_w': jnp.ones((D_MODEL,), jnp.float32), 'ln1_b': jnp.zeros((D_MODEL,), jnp.float32), 'ln2_w': jnp.ones((D_MODEL,), jnp.float32), 'ln2_b': jnp.zeros((D_MODEL,), jnp.float32), 'Wqkv': s(ks[1], (D_MODEL, 3 * D_MODEL), 0.02), 'bqkv': jnp.zeros((3 * D_MODEL,), jnp.float32), 'Wo': s(ks[2], (D_MODEL, D_MODEL), 0.02), 'bo': jnp.zeros((D_MODEL,), jnp.float32), 'gate_W': s(ks[3], (D_MODEL, N_EXPERTS), 0.02), 'fc1_w': s(ks[4], (N_EXPERTS, FFN_DIM, D_MODEL), (2.0 / D_MODEL) ** 0.5), 'fc1_b': jnp.zeros((N_EXPERTS, FFN_DIM), jnp.float32), 'fc2_w': s(ks[5], (N_EXPERTS, D_MODEL, FFN_DIM), (1.0 / FFN_DIM) ** 0.5), 'fc2_b': jnp.zeros((N_EXPERTS, D_MODEL), jnp.float32)}
        return inp
    _L0_ffn_all = _L0_ffn_setup()
    _L0_ffn_in = {k: v for k, v in _L0_ffn_all.items() if k in ('ln1_w', 'ln1_b', 'ln2_w', 'ln2_b', 'Wqkv', 'bqkv', 'Wo', 'bo', 'gate_W', 'fc1_w', 'fc1_b', 'fc2_w', 'fc2_b')}
    del _L0_ffn_all

    def _L1_attn_setup():
        import jax, jax.numpy as jnp
        import numpy as np
        DIM = 128
        HEADS = 16
        HEAD_DIM = DIM // HEADS

        def _feature_map(t):
            return jax.nn.elu(t) + 1.0
        key = jax.random.key(seed)
        k1, k2, k3 = jax.random.split(key, 3)
        x = jax.random.normal(k1, (4, 512, DIM), dtype=jnp.float32)
        w_qkv = jax.random.normal(k2, (3 * DIM, DIM), dtype=jnp.float32) * (1.0 / np.sqrt(DIM))
        w_out = jax.random.normal(k3, (DIM, DIM), dtype=jnp.float32) * (1.0 / np.sqrt(DIM))
        return {'x': x, 'w_qkv': w_qkv, 'w_out': w_out}
    _L1_attn_all = _L1_attn_setup()
    _L1_attn_in = {k: v for k, v in _L1_attn_all.items() if k in ('w_qkv', 'w_out')}
    del _L1_attn_all

    def _L1_xattn_setup():
        import jax, jax.numpy as jnp
        import numpy as np
        DIM = 128
        H = 16
        DH = 64
        INNER = H * DH
        SCALE = DH ** (-0.5)
        key = jax.random.key(seed)
        ks = jax.random.split(key, 6)
        B, L, R = (4, 512, 64)
        x = jax.random.normal(ks[0], (B, L, DIM), dtype=jnp.float32)
        context = jax.random.normal(ks[1], (B, R, DIM), dtype=jnp.float32)
        s = DIM ** (-0.5)
        Wq = jax.random.normal(ks[2], (DIM, INNER), dtype=jnp.float32) * s
        Wk = jax.random.normal(ks[3], (DIM, INNER), dtype=jnp.float32) * s
        Wv = jax.random.normal(ks[4], (DIM, INNER), dtype=jnp.float32) * s
        Wo = jax.random.normal(ks[5], (INNER, DIM), dtype=jnp.float32) * INNER ** (-0.5)
        return {'x': x, 'context': context, 'Wq': Wq, 'Wk': Wk, 'Wv': Wv, 'Wo': Wo}
    _L1_xattn_all = _L1_xattn_setup()
    _L1_xattn_in = {k: v for k, v in _L1_xattn_all.items() if k in ('Wq', 'Wk', 'Wv', 'Wo')}
    del _L1_xattn_all

    def _L1_ffn_setup():
        import jax, jax.numpy as jnp
        import numpy as np
        B, S, D = (2, 256, 128)
        E, K, DFF = (8, 2, 4 * 128)
        EPS_GATE = 1e-08
        EPS_LN = 1e-05
        key = jax.random.key(seed)
        ks = jax.random.split(key, 4)
        scaled = lambda k, shape, fan: jax.random.normal(k, shape, jnp.float32) / np.sqrt(fan).astype(np.float32)
        return {'x': jax.random.normal(ks[0], (B, S, D), jnp.float32), 'Wg': scaled(ks[1], (D, E), D), 'bg': jnp.zeros((E,), jnp.float32), 'W1': scaled(ks[2], (E, D, DFF), D), 'b1': jnp.zeros((E, DFF), jnp.float32), 'W2': scaled(ks[3], (E, DFF, D), DFF), 'b2': jnp.zeros((E, D), jnp.float32), 'gamma': jnp.ones((D,), jnp.float32), 'beta': jnp.zeros((D,), jnp.float32)}
    _L1_ffn_all = _L1_ffn_setup()
    _L1_ffn_in = {k: v for k, v in _L1_ffn_all.items() if k in ('Wg', 'bg', 'W1', 'b1', 'W2', 'b2', 'gamma', 'beta')}
    del _L1_ffn_all
    return {'x': x, 'ctx_1024': ctx_1024, 'L0_attn_Wq': _L0_attn_in['Wq'], 'L0_attn_bq': _L0_attn_in['bq'], 'L0_attn_Wk': _L0_attn_in['Wk'], 'L0_attn_bk': _L0_attn_in['bk'], 'L0_attn_Wv': _L0_attn_in['Wv'], 'L0_attn_bv': _L0_attn_in['bv'], 'L0_attn_Wo': _L0_attn_in['Wo'], 'L0_attn_bo': _L0_attn_in['bo'], 'L0_xattn_Wq': _L0_xattn_in['Wq'], 'L0_xattn_Wk': _L0_xattn_in['Wk'], 'L0_xattn_Wv': _L0_xattn_in['Wv'], 'L0_xattn_Wo': _L0_xattn_in['Wo'], 'L0_ffn_ln1_w': _L0_ffn_in['ln1_w'], 'L0_ffn_ln1_b': _L0_ffn_in['ln1_b'], 'L0_ffn_ln2_w': _L0_ffn_in['ln2_w'], 'L0_ffn_ln2_b': _L0_ffn_in['ln2_b'], 'L0_ffn_Wqkv': _L0_ffn_in['Wqkv'], 'L0_ffn_bqkv': _L0_ffn_in['bqkv'], 'L0_ffn_Wo': _L0_ffn_in['Wo'], 'L0_ffn_bo': _L0_ffn_in['bo'], 'L0_ffn_gate_W': _L0_ffn_in['gate_W'], 'L0_ffn_fc1_w': _L0_ffn_in['fc1_w'], 'L0_ffn_fc1_b': _L0_ffn_in['fc1_b'], 'L0_ffn_fc2_w': _L0_ffn_in['fc2_w'], 'L0_ffn_fc2_b': _L0_ffn_in['fc2_b'], 'L1_attn_w_qkv': _L1_attn_in['w_qkv'], 'L1_attn_w_out': _L1_attn_in['w_out'], 'L1_xattn_Wq': _L1_xattn_in['Wq'], 'L1_xattn_Wk': _L1_xattn_in['Wk'], 'L1_xattn_Wv': _L1_xattn_in['Wv'], 'L1_xattn_Wo': _L1_xattn_in['Wo'], 'L1_ffn_Wg': _L1_ffn_in['Wg'], 'L1_ffn_bg': _L1_ffn_in['bg'], 'L1_ffn_W1': _L1_ffn_in['W1'], 'L1_ffn_b1': _L1_ffn_in['b1'], 'L1_ffn_W2': _L1_ffn_in['W2'], 'L1_ffn_b2': _L1_ffn_in['b2'], 'L1_ffn_gamma': _L1_ffn_in['gamma'], 'L1_ffn_beta': _L1_ffn_in['beta']}

def reference(x, ctx_1024, L0_attn_Wq, L0_attn_bq, L0_attn_Wk, L0_attn_bk, L0_attn_Wv, L0_attn_bv, L0_attn_Wo, L0_attn_bo, L0_xattn_Wq, L0_xattn_Wk, L0_xattn_Wv, L0_xattn_Wo, L0_ffn_ln1_w, L0_ffn_ln1_b, L0_ffn_ln2_w, L0_ffn_ln2_b, L0_ffn_Wqkv, L0_ffn_bqkv, L0_ffn_Wo, L0_ffn_bo, L0_ffn_gate_W, L0_ffn_fc1_w, L0_ffn_fc1_b, L0_ffn_fc2_w, L0_ffn_fc2_b, L1_attn_w_qkv, L1_attn_w_out, L1_xattn_Wq, L1_xattn_Wk, L1_xattn_Wv, L1_xattn_Wo, L1_ffn_Wg, L1_ffn_bg, L1_ffn_W1, L1_ffn_b1, L1_ffn_W2, L1_ffn_b2, L1_ffn_gamma, L1_ffn_beta):
    import jax
    import jax.numpy as jnp

    def _L0_attn_ref(x, Wq, bq, Wk, bk, Wv, bv, Wo, bo):
        import jax, jax.numpy as jnp
        import numpy as np
        import math
        DIM = 128
        scale = 1.0 / math.sqrt(DIM)
        Q = x @ Wq.T + bq
        K = x @ Wk.T + bk
        V = x @ Wv.T + bv
        Qn = Q / (jnp.linalg.norm(Q, axis=-1, keepdims=True) + 1e-08)
        Kn = K / (jnp.linalg.norm(K, axis=-1, keepdims=True) + 1e-08)
        phase = jnp.cos(jnp.einsum('bqd,bkd->bqk', Qn, Kn) * jnp.pi)
        amplitude = jnp.einsum('bqd,bkd->bqk', Q, K) * scale
        weight = jax.nn.softmax(phase * amplitude, axis=-1)
        out = jnp.einsum('bqk,bkd->bqd', weight, V)
        return out @ Wo.T + bo

    def _L0_xattn_ref(q, k, v, Wq, Wk, Wv, Wo):
        import math
        import jax, jax.numpy as jnp
        import numpy as np
        B, T, D, H = (2, 256, 128, 16)
        HD = D // H
        b, t, d = q.shape
        qp = (q @ Wq.T).reshape(b, t, H, HD).transpose(0, 2, 1, 3)
        kp = (k @ Wk.T).reshape(b, t, H, HD).transpose(0, 2, 1, 3)
        vp = (v @ Wv.T).reshape(b, t, H, HD).transpose(0, 2, 1, 3)
        scores = jnp.einsum('bhqd,bhkd->bhqk', qp, kp)
        scores = scores / math.sqrt(HD)
        scores = scores * math.log(b)
        scores = scores - jnp.max(scores, axis=-1, keepdims=True)
        causal = jnp.triu(jnp.ones((t, t), bool), k=1)
        scores = jnp.where(causal, -jnp.inf, scores)
        num = jnp.exp(scores)
        den = jnp.sum(num, axis=-1, keepdims=True) + 1.0
        attn = num / den
        out = jnp.einsum('bhqk,bhkd->bhqd', attn, vp)
        out = out.transpose(0, 2, 1, 3).reshape(b, t, d)
        return out @ Wo.T

    def _L0_ffn_ref(x, ln1_w, ln1_b, ln2_w, ln2_b, Wqkv, bqkv, Wo, bo, gate_W, fc1_w, fc1_b, fc2_w, fc2_b):
        import jax, jax.numpy as jnp
        import numpy as np
        D_MODEL = 128
        N_HEADS = 16
        HEAD_DIM = D_MODEL // N_HEADS
        FFN_DIM = 512
        N_EXPERTS = 8
        TOP_K = 2
        BATCH = 4
        SEQ = 128

        def _layernorm(x, w, b, eps=1e-05):
            mu = jnp.mean(x, axis=-1, keepdims=True)
            var = jnp.mean(jnp.square(x - mu), axis=-1, keepdims=True)
            return (x - mu) * jax.lax.rsqrt(var + eps) * w + b

        def _causal_attention(nx, Wqkv, bqkv, Wo, bo):
            B, S, D = nx.shape
            qkv = nx @ Wqkv + bqkv
            q, k, v = jnp.split(qkv, 3, axis=-1)
            q = q.reshape(B, S, N_HEADS, HEAD_DIM)
            k = k.reshape(B, S, N_HEADS, HEAD_DIM)
            v = v.reshape(B, S, N_HEADS, HEAD_DIM)
            scores = jnp.einsum('bqhd,bkhd->bhqk', q, k) / jnp.sqrt(jnp.float32(HEAD_DIM))
            causal = jnp.tril(jnp.ones((S, S), bool))
            scores = jnp.where(causal, scores, jnp.finfo(scores.dtype).min)
            attn = jax.nn.softmax(scores, axis=-1)
            out = jnp.einsum('bhqk,bkhd->bqhd', attn, v).reshape(B, S, D)
            return out @ Wo + bo

        def _moe_ffn(nx, gate_W, fc1_w, fc1_b, fc2_w, fc2_b):
            gate_logits = nx @ gate_W
            topk_vals, topk_idx = jax.lax.top_k(gate_logits, TOP_K)
            gate_w = jax.nn.softmax(topk_vals, axis=-1)
            dense_gates = jnp.sum(jax.nn.one_hot(topk_idx, N_EXPERTS, dtype=nx.dtype) * gate_w[..., None], axis=-2)
            moe_out = jnp.zeros_like(nx)
            for e in range(N_EXPERTS):
                h = jax.nn.gelu(jnp.einsum('bsd,fd->bsf', nx, fc1_w[e]) + fc1_b[e], approximate=False)
                y = jnp.einsum('bsf,df->bsd', h, fc2_w[e]) + fc2_b[e]
                moe_out = moe_out + y * dense_gates[..., e:e + 1]
            return moe_out
        nx = _layernorm(x, ln1_w, ln1_b)
        attn_out = _causal_attention(nx, Wqkv, bqkv, Wo, bo)
        x = x + attn_out
        nx2 = _layernorm(x, ln2_w, ln2_b)
        moe_out = _moe_ffn(nx2, gate_W, fc1_w, fc1_b, fc2_w, fc2_b)
        return x + moe_out

    def _L1_attn_ref(x, w_qkv, w_out):
        import jax, jax.numpy as jnp
        import numpy as np
        DIM = 128
        HEADS = 16
        HEAD_DIM = DIM // HEADS

        def _feature_map(t):
            return jax.nn.elu(t) + 1.0
        b, n, _ = x.shape
        qkv = x @ w_qkv.T
        q, k, v = jnp.split(qkv, 3, axis=-1)

        def to_heads(t):
            return t.reshape(b, n, HEADS, HEAD_DIM).transpose(0, 2, 1, 3)
        q, k, v = (to_heads(q), to_heads(k), to_heads(v))
        q = _feature_map(q)
        k = _feature_map(k)
        kv = jnp.einsum('bhnd,bhne->bhde', k, v)
        out = jnp.einsum('bhnd,bhde->bhne', q, kv)
        k_sum = k.sum(axis=2)
        normalizer = jnp.einsum('bhnd,bhd->bhn', q, k_sum)
        out = out / (normalizer[..., None] + 1e-06)
        out = out.transpose(0, 2, 1, 3).reshape(b, n, DIM)
        return out @ w_out.T

    def _L1_xattn_ref(x, context, Wq, Wk, Wv, Wo):
        import jax, jax.numpy as jnp
        import numpy as np
        DIM = 128
        H = 16
        DH = 64
        INNER = H * DH
        SCALE = DH ** (-0.5)
        B, L, _ = x.shape
        R = context.shape[1]
        q = (x @ Wq).reshape(B, L, H, DH).transpose(0, 2, 1, 3)
        k = (context @ Wk).reshape(B, R, H, DH).transpose(0, 2, 1, 3)
        v = (context @ Wv).reshape(B, R, H, DH).transpose(0, 2, 1, 3)
        scores = jnp.einsum('bhld,bhrd->bhlr', q, k) * SCALE
        attn = jax.nn.softmax(scores, axis=-1)
        out = jnp.einsum('bhlr,bhrd->bhld', attn, v)
        out = out.transpose(0, 2, 1, 3).reshape(B, L, INNER)
        return out @ Wo

    def _L1_ffn_ref(x, Wg, bg, W1, b1, W2, b2, gamma, beta):
        import jax, jax.numpy as jnp
        import numpy as np
        B, S, D = (2, 256, 128)
        E, K, DFF = (8, 2, 4 * 128)
        EPS_GATE = 1e-08
        EPS_LN = 1e-05
        b, s, d = x.shape
        xf = x.reshape(-1, d)
        T = xf.shape[0]
        num_experts = Wg.shape[1]
        logits = xf @ Wg + bg
        w = jax.nn.softmax(logits, axis=-1)
        top_w, top_idx = jax.lax.top_k(w, K)
        top_w = top_w / (top_w.sum(axis=-1, keepdims=True) + EPS_GATE)
        cw = jnp.zeros((T, num_experts), xf.dtype).at[jnp.arange(T)[:, None], top_idx].add(top_w)
        out = jnp.zeros_like(xf)
        for e in range(num_experts):
            h = jax.nn.gelu(xf @ W1[e] + b1[e], approximate=False)
            y = h @ W2[e] + b2[e]
            out = out + cw[:, e:e + 1] * y
        mu = out.mean(axis=-1, keepdims=True)
        var = out.var(axis=-1, keepdims=True)
        out = (out - mu) / jnp.sqrt(var + EPS_LN) * gamma + beta
        return out.reshape(b, s, d)
    x = x + _L0_attn_ref(_layernorm(x, axis=-1), L0_attn_Wq, L0_attn_bq, L0_attn_Wk, L0_attn_bk, L0_attn_Wv, L0_attn_bv, L0_attn_Wo, L0_attn_bo)
    x = x + _L0_xattn_ref(_layernorm(x, axis=-1), ctx_1024, ctx_1024, L0_xattn_Wq, L0_xattn_Wk, L0_xattn_Wv, L0_xattn_Wo)
    x = x + _L0_ffn_ref(_layernorm(x, axis=-1), L0_ffn_ln1_w, L0_ffn_ln1_b, L0_ffn_ln2_w, L0_ffn_ln2_b, L0_ffn_Wqkv, L0_ffn_bqkv, L0_ffn_Wo, L0_ffn_bo, L0_ffn_gate_W, L0_ffn_fc1_w, L0_ffn_fc1_b, L0_ffn_fc2_w, L0_ffn_fc2_b)
    x = x + _L1_attn_ref(_layernorm(x, axis=-1), L1_attn_w_qkv, L1_attn_w_out)
    x = x + _L1_xattn_ref(_layernorm(x, axis=-1), ctx_1024, L1_xattn_Wq, L1_xattn_Wk, L1_xattn_Wv, L1_xattn_Wo)
    x = x + _L1_ffn_ref(_layernorm(x, axis=-1), L1_ffn_Wg, L1_ffn_bg, L1_ffn_W1, L1_ffn_b1, L1_ffn_W2, L1_ffn_b2, L1_ffn_gamma, L1_ffn_beta)
    return x

_drawn_inputs = setup_inputs


def setup_inputs(seed=0):
    import zlib

    import numpy as np

    out = dict(_drawn_inputs(seed))
    spreads = {'L0_ffn_ln1_w': (1.0, 0.6),
     'L0_ffn_ln1_b': (0.0, 0.282),
     'L0_ffn_ln2_w': (1.0, 0.2),
     'L0_ffn_ln2_b': (0.0, 0.1),
     'L0_ffn_bqkv': (0.0, 0.1),
     'L0_ffn_bo': (0.0, 0.1),
     'L0_ffn_fc1_b': (0.0, 0.1),
     'L0_ffn_fc2_b': (0.0, 0.1),
     'L1_ffn_bg': (0.0, 0.1),
     'L1_ffn_b1': (0.0, 0.1),
     'L1_ffn_b2': (0.0, 0.1),
     'L1_ffn_gamma': (1.0, 0.2),
     'L1_ffn_beta': (0.0, 0.1)}
    factors = {'L0_attn_bq': 4.207, 'L0_attn_bk': 182.534}
    for name, (base, spread) in spreads.items():
        noise = np.random.default_rng([zlib.crc32(name.encode()), seed]).standard_normal(out[name].shape)
        drawn = base * np.exp(spread * noise) if base else spread * noise
        out[name] = jnp.asarray(drawn.astype(out[name].dtype))
    for name, factor in factors.items():
        out[name] = (out[name] * factor).astype(out[name].dtype)
    return out
```

```python
from contextlib import ExitStack

import concourse.bass as bass
from concourse import mybir

F32 = mybir.dt.float32
BF16 = mybir.dt.bfloat16
ALU = mybir.AluOpType
ACT = mybir.ActivationFunctionType
AX = mybir.AxisListType

P = 128
NB = 16
CH = 4
NC = NB // CH
H = 16
HD = P // H
WH = 64
WB = H * WH // P
E = 8
FF = 512
FB = FF // P
HG = 4
G = H // HG
EPS = 1e-5
NEG = -3.0e38
PI = 3.141592653589793
LN_B = 2.772588722239781


def skewed(eng, iteration, first, lo, hi, last):
    for i in range(first, lo):
        iteration(i, i % 2)
    with eng.Fori(0, (hi - lo) // 2) as pair:
        iteration(2 * pair + lo, lo % 2)
        iteration(2 * pair + (lo + 1), (lo + 1) % 2)
    for i in range(hi, last + 1):
        iteration(i, i % 2)


def there(b):
    return not isinstance(b, int) or 0 <= b < NB


def later(b, n):
    return not isinstance(b, int) or b >= n


def take(eng, passed):
    eng.sem_inc(passed, 1)


class Stage:

    def __init__(self, sems, past):
        self.sems, self.past = dict(sems), past

    def __getitem__(self, name):
        return self.sems[name]


class Chain:

    def __init__(self, per, past=0):
        self.per, self.past, self.at = per, past, 0

    def begin(self, b):
        self.base, self.at = self.per * b + self.past, 0

    def next(self):
        self.at += 1
        return self.base + self.at

    def end(self):
        assert self.at == self.per, (self.at, self.per)


def decoder(nc, a, out):
    with ExitStack() as ctx:
        def sb(name, shape, dt=F32):
            return ctx.enter_context(nc.sbuf_tensor(name, shape, dt))

        early = ctx.enter_context(ExitStack())

        def eb(name, shape, dt=F32):
            return early.enter_context(nc.sbuf_tensor(name, shape, dt))

        def sems(prefix, names):
            return {n: ctx.enter_context(nc.semaphore(f"{prefix}_{n}")) for n in names.split()}

        bank = ctx.enter_context(nc.psum_tensor("bank", [P, 8, 512], F32))

        def quarters(k):
            return bank[:, k, :].rearrange("p (n c) -> p n c", n=4)

        NT = 28
        NCOL = 2 * E * FB + 6
        x = sb("x", [P, NB, P])
        y = sb("y", [P, NB, P])
        tokensT = sb("tokensT", [P, NB * P])

        ident = sb("ident", [P, P])
        ident16 = sb("ident16", [P, P], BF16)
        head_of = sb("head_of", [P, H])
        future = sb("future", [P, HG, P], BF16)
        expert_of = sb("expert_of", [E, P])
        countdown = sb("countdown", [P, E])
        ones_row = sb("ones_row", [1, P])
        minus_half = sb("minus_half", [P, 2 * E])
        plus_half = sb("plus_half", [P, 2 * E])

        turned = sb("turned", [P, NT, P])
        A0_QKV, A0_O, X0_Q, X0_K, X0_V, X0_O, A1_QKV, A1_O, X1_Q, X1_K = 0, 3, 4, 5, 6, 7, 8, 11, 12, 20
        cols = sb("cols", [P, NCOL])
        C_B1, C_LN1W, C_LN1B, C_LN2W, C_LN2B, C_BQ, C_BK = (0, E * FB), 64, 65, 66, 67, 68, 69
        c0_qkv = sb("c0_qkv", [P, 3 * P])
        c0_o = sb("c0_o", [P, P])
        x1_v = sb("x1_v", [P, WB * P])
        x1_o = sb("x1_o", [P, WB, P])
        x1_m = sb("x1_m", [P, H, P])
        gate_w = sb("gate_w", [P, 2, E])
        b2_rows = sb("b2_rows", [E, 2, P])
        b2_rep = sb("b2_rep", [P, 2, P])
        a0_bqkv = sb("a0_bqkv", [P, 3 * P])
        a0_bo = sb("a0_bo", [P, P])
        c0_bv = sb("c0_bv", [P, P])
        c0_bo = sb("c0_bo", [P, P])
        gate_b = sb("gate_b", [P, E])
        gamma = sb("gamma", [P, P])
        beta = sb("beta", [P, P])

        all_done = []

        def after_previous(eng, n):
            if n:
                eng.wait_ge(*all_done[n - 1])

        rows = eb("rows", [P, NT, P])
        col_rows = eb("col_rows", [NCOL, P])
        L = sems("load", "x w vec const turned_ps turned_a turned_b cols_ps cols b2_ps b2 wide_ps m_done passed")
        w_loads = [
            (rows[:, A0_QKV, :], a["L0_attn_Wq"]), (rows[:, A0_QKV + 1, :], a["L0_attn_Wk"]),
            (rows[:, A0_QKV + 2, :], a["L0_attn_Wv"]), (rows[:, A0_O, :], a["L0_attn_Wo"]),
            (rows[:, X0_Q, :], a["L0_xattn_Wq"]), (rows[:, X0_K, :], a["L0_xattn_Wk"]),
            (rows[:, X0_V, :], a["L0_xattn_Wv"]), (rows[:, X0_O, :], a["L0_xattn_Wo"]),
            (rows[:, A1_QKV:A1_QKV + 3, :], a["L1_attn_w_qkv"].rearrange("(c p) d -> p c d", p=P)),
            (rows[:, A1_O, :], a["L1_attn_w_out"]),
            (rows[:, X1_Q:X1_Q + WB, :], a["L1_xattn_Wq"].rearrange("p (c d) -> p c d", d=P)),
            (rows[:, X1_K:X1_K + WB, :], a["L1_xattn_Wk"].rearrange("p (c d) -> p c d", d=P)),
            (col_rows[0:32, :], a["L0_ffn_fc1_b"].rearrange("e (c p) -> (e c) p", p=P)),
            (col_rows[32:64, :], a["L1_ffn_b1"].rearrange("e (c p) -> (e c) p", p=P)),
            (col_rows[64:65, :], a["L0_ffn_ln1_w"].unsqueeze(0)), (col_rows[65:66, :], a["L0_ffn_ln1_b"].unsqueeze(0)),
            (col_rows[66:67, :], a["L0_ffn_ln2_w"].unsqueeze(0)), (col_rows[67:68, :], a["L0_ffn_ln2_b"].unsqueeze(0)),
            (col_rows[68:70, :], a["L0_ffn_bqkv"][0:2 * P].rearrange("(c p) -> c p", p=P)),
            (b2_rows[:, 0, :], a["L0_ffn_fc2_b"]), (b2_rows[:, 1, :], a["L1_ffn_b2"]),
        ]
        vec_loads = [
            (a0_bqkv[:, 0:P], a["L0_attn_bq"].partition_broadcast(P)),
            (a0_bqkv[:, P:2 * P], a["L0_attn_bk"].partition_broadcast(P)),
            (a0_bqkv[:, 2 * P:3 * P], a["L0_attn_bv"].partition_broadcast(P)),
            (a0_bo[:, :], a["L0_attn_bo"].partition_broadcast(P)),
            (c0_bv[:, :], a["L0_ffn_bqkv"][2 * P:3 * P].partition_broadcast(P)),
            (c0_bo[:, :], a["L0_ffn_bo"].partition_broadcast(P)),
            (gate_b[:, :], a["L1_ffn_bg"].partition_broadcast(P)),
            (gamma[:, :], a["L1_ffn_gamma"].partition_broadcast(P)),
            (beta[:, :], a["L1_ffn_beta"].partition_broadcast(P)),
            (c0_qkv[:, :], a["L0_ffn_Wqkv"]), (c0_o[:, :], a["L0_ffn_Wo"]),
            (x1_v[:, :], a["L1_xattn_Wv"]), (x1_o[:, :, :], a["L1_xattn_Wo"].rearrange("(c p) d -> p c d", p=P)),
            (gate_w[:, 0, :], a["L0_ffn_gate_W"]), (gate_w[:, 1, :], a["L1_ffn_Wg"]),
        ]

        def sp_load(sp):
            sp.dma_start(x[:, :, :], a["x"].rearrange("b t d -> t b d")).then_inc(L["x"], 16)
            for dst, src in vec_loads:
                sp.dma_start(dst, src).then_inc(L["vec"], 16)

        def act_load(act):
            for dst, src in w_loads:
                act.dma_start(dst, src).then_inc(L["w"], 16)
            for n in range(1, NT // 4, 2):
                act.wait_ge(L["turned_ps"], n + 1)
                nc.scalar.activation(turned[:, 4 * n:4 * n + 4, :], quarters(n), ACT.Copy).then_inc(L["turned_a"], 1)

        def pool_load(pool):
            made = []

            def make(instruction):
                made.append(1)
                instruction.then_inc(L["const"], 1)
                pool.wait_ge(L["const"], len(made))

            make(nc.gpsimd.memset(ident[:, :], 0.0))
            make(nc.gpsimd.affine_select(out=ident[:, :], in_=ident[:, :], compare_op=ALU.not_equal, fill=1.0,
                                         base=0, pattern=[[-1, P]], channel_multiplier=1))
            make(nc.gpsimd.tensor_copy(ident16[:, :], ident[:, :]))
            make(nc.gpsimd.memset(head_of[:, :], 1.0))
            make(nc.gpsimd.affine_select(out=head_of[:, :], in_=head_of[:, :], compare_op=ALU.is_ge, fill=0.0,
                                         base=0, pattern=[[-HD, H]], channel_multiplier=1))
            make(nc.gpsimd.affine_select(out=head_of[:, :], in_=head_of[:, :], compare_op=ALU.is_ge, fill=0.0,
                                         base=HD - 1, pattern=[[HD, H]], channel_multiplier=-1))
            make(nc.gpsimd.memset(future[:, :, :], 0.0))
            make(nc.gpsimd.affine_select(out=future[:, :, :], in_=future[:, :, :], compare_op=ALU.is_ge, fill=NEG,
                                         base=0, pattern=[[0, HG], [-1, P]], channel_multiplier=1))
            make(nc.gpsimd.memset(expert_of[:, :], 0.0))
            eo = expert_of[:, :].rearrange("p (b e) -> p b e", e=E)
            make(nc.gpsimd.affine_select(out=eo, in_=eo, compare_op=ALU.not_equal, fill=1.0,
                                         base=0, pattern=[[0, P // E], [-1, E]], channel_multiplier=1))
            make(nc.gpsimd.iota(countdown[:, :], pattern=[[-1, E]], base=E, channel_multiplier=0,
                                allow_small_or_imprecise_dtypes=True))
            make(nc.gpsimd.memset(minus_half[:, :], -0.5))
            make(nc.gpsimd.memset(plus_half[:, :], 0.5))
            make(nc.gpsimd.memset(ones_row[:, :], 1.0))
            assert len(made) == CONSTS

        CONSTS = 14

        def pe_load(pe):
            pe.wait_ge(L["const"], CONSTS)
            pe.wait_ge(L["w"], 16 * len(w_loads))
            for n in range(NT // 4):
                for j in range(4):
                    mm = nc.tensor.transpose(quarters(n)[:, j, :], rows[:, 4 * n + j, :], ident[:, :])
                mm.then_inc(L["turned_ps"], 1)
            nc.tensor.transpose(bank[:, 7, 0:NCOL], col_rows[:, :], ident[0:NCOL, 0:NCOL]).then_inc(L["cols_ps"], 1)
            pe.wait_ge(L["turned_a"], 3)
            pe.wait_ge(L["turned_b"], 4)
            pe.wait_ge(L["cols"], 1)
            for odd in range(2):
                for n in range(WB):
                    r = slice(WH * odd, WH * odd + WH)
                    mm = nc.tensor.matmul(quarters(2 * odd + n // 4)[:, n % 4, :], turned[r, X1_Q + n, :],
                                          turned[r, X1_K + n, :], start=True, stop=True)
            mm.then_inc(L["wide_ps"], 1)
            for l in range(2):
                mm = nc.tensor.matmul(bank[:, 4, l * P:(l + 1) * P], expert_of[:, :], b2_rows[:, l, :],
                                      start=True, stop=True)
            mm.then_inc(L["b2_ps"], 1)

        def dve_load(dve):
            for n in range(0, NT // 4, 2):
                dve.wait_ge(L["turned_ps"], n + 1)
                nc.vector.tensor_copy(turned[:, 4 * n:4 * n + 4, :], quarters(n)).then_inc(L["turned_b"], 1)
            dve.wait_ge(L["cols_ps"], 1)
            nc.vector.tensor_copy(cols[:, :], bank[:, 7, 0:NCOL]).then_inc(L["cols"], 1)
            dve.wait_ge(L["wide_ps"], 1)
            for n in range(4):
                odd, half = n // 2, n % 2
                nc.vector.tensor_copy(x1_m[:, odd + 8 * half:odd + 8 * half + 7:2, :], quarters(n)).then_inc(L["m_done"], 1)
            dve.wait_ge(L["b2_ps"], 1)
            nc.vector.tensor_copy(b2_rep[:, :, :], bank[:, 4, 0:2 * P].rearrange("p (l c) -> p l c", l=2)).then_inc(L["b2"], 1)

        all_loaded = (L["b2"], 1)

        A = sems("phase", """var rstd normed turned_ps turned qkv_ps qkv square root inv scaled sides_ps sides
                             score_ps sine shift probs probsT_ps probsT merged_ps merged out_ps chain done""")
        a_stats = eb("a_stats", [P, CH, 6])
        a_moments = eb("a_moments", [P, CH, 2])
        a_var = eb("a_var", [P, CH])
        a_rstd = eb("a_rstd", [P, CH])
        a_normed = eb("a_normed", [P, CH, P])
        a_T = eb("a_T", [P, CH, P])
        a_qkv = eb("a_qkv", [P, CH, 3, P])
        a_squares = eb("a_squares", [P, CH, 2, P])
        a_sums = eb("a_sums", [P, CH, 2])
        a_norms = eb("a_norms", [P, CH * 2])
        a_norms1 = eb("a_norms1", [P, CH * 2])
        a_inv = eb("a_inv", [P, CH, 2])
        a_unit = eb("a_unit", [P, CH, 2, P])
        a_sides = eb("a_sides", [P, 4, CH, P])
        a_sine = eb("a_sine", [P, CH, P])
        a_phase = eb("a_phase", [P, CH, P])
        a_scores = eb("a_scores", [P, CH, P])
        a_peak = eb("a_peak", [P, CH])
        a_shift = eb("a_shift", [P, CH, P])
        a_probs = eb("a_probs", [P, CH, P])
        a_den = eb("a_den", [P, CH])
        a_rden = eb("a_rden", [P, CH])
        a_probsT = eb("a_probsT", [P, CH, P])
        a_merged = eb("a_merged", [P, CH, P])
        a_out = eb("a_out", [P, CH, P])
        a_out1 = eb("a_out1", [P, CH, P])
        V = 2
        early.close()

        heads_end = ctx.enter_context(ExitStack())

        def hb(name, shape, dt=F32):
            return heads_end.enter_context(nc.sbuf_tensor(name, shape, dt))

        stats = hb("stats", [P, 2, 6])
        moments = hb("moments", [P, 2, 2])
        var_eps = hb("var_eps", [P, 2, 1])
        rstd = hb("rstd", [P, 2, 1])
        stats2 = hb("stats2", [P, 2, 6])
        moments2 = hb("moments2", [P, 2, 2])
        rstd2 = hb("rstd2", [P, 2, 1])
        normed = [hb(f"normed{p}", [P, P]) for p in range(2)]
        ctx_rows = [hb(f"ctx_rows{p}", [P, P]) for p in range(2)]
        bothT = [hb(f"bothT{p}", [P, 2, P]) for p in range(2)]
        qT = [hb(f"qT{p}", [P, P]) for p in range(2)]
        kT = [hb(f"kT{p}", [P, P]) for p in range(2)]
        wide = [hb(f"wide{p}", [P, H, P]) for p in range(2)]
        probs = [hb(f"probs{p}", [P, H, P]) for p in range(2)]
        probsT = hb("probsT", [P, H, P])
        peak = [hb(f"peak{p}", [P, H]) for p in range(2)]
        values = [hb(f"values{p}", [P, H, 32]) for p in range(2)]
        headsT = [hb(f"headsT{p}", [P, 4, P]) for p in range(2)]
        den = [hb(f"den{p}", [P, H]) for p in range(2)]
        den1 = [hb(f"den1{p}", [P, H]) for p in range(2)]
        merged = [hb(f"merged{p}", [P, P]) for p in range(2)]
        mergedT = [hb(f"mergedT{p}", [P, P]) for p in range(2)]
        v_wide = [hb(f"v_wide{p}", [P, WB * P]) for p in range(2)]
        wideT = hb("wideT", [P, WB, P])
        lin_raw = [hb(f"lin_raw{p}", [P, 2, P]) for p in range(2)]
        lin_neg = [hb(f"lin_neg{p}", [P, 2, P]) for p in range(2)]
        lin_exp = [hb(f"lin_exp{p}", [P, 2, P]) for p in range(2)]
        lin_qk = [hb(f"lin_qk{p}", [P, 2, P]) for p in range(2)]
        lin_v = [hb(f"lin_v{p}", [P, 2, P]) for p in range(2)]
        lin_kv = [hb(f"lin_kv{p}", [P, 2 * P]) for p in range(2)]
        block_of = hb("block_of", [P, P])

        all_done.append((A["done"], NC))

        def pe_phase(pe):
            pe.wait_ge(*all_loaded)
            pe.wait_ge(L["m_done"], 4)
            pe.wait_ge(L["vec"], 16 * len(vec_loads))

            def chunk(c):
                pe.wait_ge(A["normed"], CH * c + CH)
                if later(c, 1):
                    pe.wait_ge(A["done"], c)
                for j in range(CH):
                    mm = nc.tensor.transpose(quarters(0)[:, j, :], a_normed[:, j, :], ident[:, :])
                mm.then_inc(A["turned_ps"], 1)
                pe.wait_ge(A["turned"], c + 1)
                for j in range(CH):
                    nc.tensor.matmul(bank[:, 1 + j, 0:3 * P], a_T[:, j, :], turned[:, A0_QKV:A0_QKV + 3, :],
                                     start=True, stop=True).then_inc(A["qkv_ps"], 1)
                pe.wait_ge(A["qkv"], CH * c + CH)
                for side in range(4):
                    if side == 2:
                        pe.wait_ge(A["scaled"], c + 1)
                    for j in range(CH):
                        src = a_qkv[:, j, side, :] if side < 2 else a_unit[:, j, side - 2, :]
                        mm = nc.tensor.transpose(quarters(1 + side)[:, j, :], src, ident[:, :])
                    mm.then_inc(A["sides_ps"], 1)
                pe.wait_ge(A["sides"], 4 * c + 4)
                for j in range(CH):
                    mm = nc.tensor.matmul(quarters(5)[:, j, :], a_sides[:, 2, j, :], a_sides[:, 3, j, :],
                                          start=True, stop=True)
                mm.then_inc(A["score_ps"], 1)
                for j in range(CH):
                    mm = nc.tensor.matmul(quarters(6)[:, j, :], a_sides[:, 0, j, :], a_sides[:, 1, j, :],
                                          start=True, stop=True)
                mm.then_inc(A["score_ps"], 1)
                pe.wait_ge(A["probs"], c + 1)
                for j in range(CH):
                    mm = nc.tensor.transpose(quarters(7)[:, j, :], a_probs[:, j, :], ident[:, :])
                mm.then_inc(A["probsT_ps"], 1)
                pe.wait_ge(A["probsT"], c + 1)
                for j in range(CH):
                    mm = nc.tensor.matmul(quarters(0)[:, j, :], a_qkv[:, j, V, :], a_probsT[:, j, :],
                                          start=True, stop=True)
                mm.then_inc(A["merged_ps"], 1)
                pe.wait_ge(A["merged"], c + 1)
                for j in range(CH):
                    mm = nc.tensor.matmul(quarters(1)[:, j, :], a_merged[:, j, :], turned[:, A0_O, :],
                                          start=True, stop=True)
                mm.then_inc(A["out_ps"], 1)

            chunk(0)
            with pe.Fori(1, NC) as c:
                chunk(c)

        def act_phase(act):
            def chunk(c):
                act.wait_ge(A["turned_ps"], c + 1)
                nc.scalar.activation(a_T[:, :, :], quarters(0), ACT.Copy).then_inc(A["turned"], 1)
                act.wait_ge(A["qkv"], CH * c + CH)
                nc.scalar.activation(a_squares[:, :, :, :], a_qkv[:, :, 0:2, :], ACT.Square).then_inc(A["square"], 1)
                for side in range(4):
                    act.wait_ge(A["sides_ps"], 4 * c + side + 1)
                    nc.scalar.activation(a_sides[:, side, :, :], quarters(1 + side), ACT.Copy).then_inc(A["sides"], 1)
                act.wait_ge(A["score_ps"], 2 * c + 1)
                nc.scalar.activation(a_sine[:, :, :], quarters(5), ACT.Sin, scale=PI / 2).then_inc(A["sine"], 1)
                act.wait_ge(A["shift"], c + 1)
                nc.scalar.activation(a_probs[:, :, :], a_shift[:, :, :], ACT.Exp, scale=P ** -0.5).then_inc(A["probs"], 1)
                act.wait_ge(A["probsT_ps"], c + 1)
                nc.scalar.activation(a_probsT[:, :, :], quarters(7), ACT.Copy).then_inc(A["probsT"], 1)
                act.wait_ge(A["merged_ps"], c + 1)
                nc.scalar.activation(a_merged[:, :, :], quarters(0), ACT.Copy).then_inc(A["merged"], 1)

            chunk(0)
            with act.Fori(1, NC) as c:
                chunk(c)

        def pool_phase(pool):
            def chunk(c):
                pool.wait_ge(A["var"], c + 1)
                nc.gpsimd.tensor_tensor(a_rstd[:, :], a_var[:, :], minus_half[:, 0:CH], ALU.pow).then_inc(A["rstd"], 1)
                pool.wait_ge(A["square"], 2 * c + 2)
                nc.gpsimd.tensor_tensor(a_norms[:, :], a_sums[:, :, :].rearrange("p c s -> p (c s)"),
                                        plus_half[:, 0:2 * CH], ALU.pow).then_inc(A["root"], 1)

            chunk(0)
            with pool.Fori(1, NC) as c:
                chunk(c)

        def dve_phase(dve):
            chain = Chain(11)
            dve.wait_ge(L["x"], 16)
            dve.wait_ge(L["const"], CONSTS)
            dve.wait_ge(L["vec"], 16 * len(vec_loads))

            def chunk(c):
                chain.begin(c)
                for j in range(CH):
                    ins = nc.vector.bn_stats(a_stats[:, j, :], x[:, CH * c + j, :])
                ins.then_inc(A["chain"], 1)
                dve.wait_ge(A["chain"], chain.next())
                take(dve, L["passed"])
                for j in range(CH):
                    ins = nc.vector.bn_aggr(a_moments[:, j, :], a_stats[:, j, :])
                ins.then_inc(A["chain"], 1)
                dve.wait_ge(A["chain"], chain.next())
                nc.vector.tensor_scalar(a_var[:, :], a_moments[:, :, 1], EPS, None, ALU.add).then_inc(A["var"], 1)
                dve.wait_ge(A["rstd"], c + 1)
                for j in range(CH):
                    nc.vector.tensor_scalar(a_normed[:, j, :], x[:, CH * c + j, :], a_moments[:, j, 0:1],
                                            a_rstd[:, j:j + 1], ALU.subtract, ALU.mult).then_inc(A["normed"], 1)
                for j in range(CH):
                    dve.wait_ge(A["qkv_ps"], CH * c + j + 1)
                    nc.vector.tensor_tensor(a_qkv[:, j, :, :], bank[:, 1 + j, 0:3 * P].rearrange("p (s d) -> p s d", s=3),
                                            a0_bqkv[:, :].rearrange("p (s d) -> p s d", s=3), ALU.add).then_inc(A["qkv"], 1)
                dve.wait_ge(A["square"], 2 * c + 1)
                nc.vector.tensor_reduce(a_sums[:, :, :], a_squares[:, :, :, :], AX.X, ALU.add).then_inc(A["square"], 1)
                dve.wait_ge(A["root"], c + 1)
                nc.vector.tensor_scalar(a_norms1[:, :], a_norms[:, :], 1e-8, None, ALU.add).then_inc(A["chain"], 1)
                dve.wait_ge(A["chain"], chain.next())
                nc.vector.reciprocal(a_inv[:, :, :].rearrange("p c s -> p (c s)"), a_norms1[:, :]).then_inc(A["chain"], 1)
                dve.wait_ge(A["chain"], chain.next())
                for j in range(CH):
                    for s in range(2):
                        ins = nc.vector.tensor_scalar(a_unit[:, j, s, :], a_qkv[:, j, s, :], a_inv[:, j, s:s + 1],
                                                      None, ALU.mult)
                ins.then_inc(A["scaled"], 1)
                dve.wait_ge(A["sine"], c + 1)
                nc.vector.scalar_tensor_tensor(out=a_phase[:, :, :], in0=a_sine[:, :, :], scalar=-2.0,
                                               in1=a_sine[:, :, :], op0=ALU.mult, op1=ALU.mult).then_inc(A["chain"], 1)
                dve.wait_ge(A["chain"], chain.next())
                dve.wait_ge(A["score_ps"], 2 * c + 2)
                nc.vector.scalar_tensor_tensor(out=a_scores[:, :, :], in0=a_phase[:, :, :], scalar=1.0,
                                               in1=quarters(6), op0=ALU.add, op1=ALU.mult).then_inc(A["chain"], 1)
                dve.wait_ge(A["chain"], chain.next())
                nc.vector.tensor_reduce(a_peak[:, :], a_scores[:, :, :], AX.X, ALU.max).then_inc(A["chain"], 1)
                dve.wait_ge(A["chain"], chain.next())
                nc.vector.tensor_tensor(a_shift[:, :, :], a_scores[:, :, :],
                                        a_peak[:, :].unsqueeze(2).to_broadcast([P, CH, P]), ALU.subtract).then_inc(A["shift"], 1)
                dve.wait_ge(A["probs"], c + 1)
                nc.vector.tensor_reduce(a_den[:, :], a_probs[:, :, :], AX.X, ALU.add).then_inc(A["chain"], 1)
                dve.wait_ge(A["chain"], chain.next())
                nc.vector.reciprocal(a_rden[:, :], a_den[:, :]).then_inc(A["chain"], 1)
                dve.wait_ge(A["chain"], chain.next())
                dve.wait_ge(A["out_ps"], c + 1)
                nc.vector.tensor_tensor(a_out[:, :, :], quarters(1),
                                        a_rden[:, :].unsqueeze(2).to_broadcast([P, CH, P]), ALU.mult).then_inc(A["chain"], 1)
                dve.wait_ge(A["chain"], chain.next())
                nc.vector.tensor_tensor(a_out1[:, :, :], a_out[:, :, :],
                                        a0_bo[:, :].unsqueeze(1).to_broadcast([P, CH, P]), ALU.add).then_inc(A["chain"], 1)
                dve.wait_ge(A["chain"], chain.next())
                xc = x[:, bass.ts(c, CH), :]
                nc.vector.tensor_tensor(xc, xc, a_out1[:, :, :], ALU.add).then_inc(A["done"], 1)
                chain.end()

            chunk(0)
            with dve.Fori(1, NC) as c:
                dve.wait_ge(A["done"], c)
                chunk(c)

        NARROW_SEMS = sems("narrow", """ctx stat rstd zed stat2 rstd2 normed both_ps both qk_ps q k masked score_ps
            shifted probs clean turn_ps probsT av_ps headsT back_ps merged mT_ps mT out_ps done v_ps values cleared
            chain norm_chain stat_chain pool_chain""")

        def run_twice(sem_set, before, second):
            return Stage(sem_set, {k: before(k) if second else 0 for k in sem_set})

        def narrow(n, cross):
            def before(k):
                if k in ("masked", "score_ps", "shifted", "probs", "clean", "turn_ps", "probsT", "chain"):
                    return G * NB
                if k in ("zed", "stat2", "rstd2"):
                    return 0
                return {"ctx": 16 * NB, "norm_chain": 2 * NB, "cleared": 4}.get(k, NB)

            s = run_twice(NARROW_SEMS, before, not cross)
            s.n, s.cross = n, cross
            s.scale = LN_B * HD ** -0.5 if cross else HD ** -0.5
            s.wq, s.wk, s.wv, s.wo = ([turned[:, X0_Q, :], turned[:, X0_K, :], turned[:, X0_V, :], turned[:, X0_O, :]] if cross
                                      else [c0_qkv[:, 0:P], c0_qkv[:, P:2 * P], c0_qkv[:, 2 * P:3 * P], c0_o[:, :]])
            s.kv = 1 if cross else 0
            s.sems["ready"] = s["clean"] if cross else s["probs"]
            s.past["ready"] = s.past["clean"] if cross else s.past["probs"]
            all_done.append((s["done"], NB + s.past["done"]))
            return s

        X0, C0 = narrow(1, True), narrow(2, False)
        NARROW = (-3, 3, 13, 16)

        def sp_narrow(sp, s):
            after_previous(sp, s.n)
            if s.cross:
                def load(b, p):
                    if later(b, 2):
                        sp.wait_ge(s["both_ps"], b - 1 + s.past["both_ps"])
                        take(sp, L["passed"])
                    if later(b, 1):
                        sp.wait_ge(s["ctx"], 16 * b + s.past["ctx"])
                    sp.dma_start(ctx_rows[p][:, :], a["ctx_1024"][b, :, :]).then_inc(s["ctx"], 16)

                load(0, 0)
                load(1, 1)
                with sp.Fori(1, NB // 2) as pair:
                    load(2 * pair, 0)
                    load(2 * pair + 1, 1)

        def pe_narrow(pe, s):
            after_previous(pe, s.n)

            def iteration(i, par):
                p0, p1 = par, 1 - par
                if there(i + 1):
                    b = i + 1
                    pe.wait_ge(s["q"], b + 1 + s.past["q"])
                    for g in range(G):
                        pe.wait_ge(s["masked"], G * b + g + 1 + s.past["masked"])
                        if later(b, 1):
                            pe.wait_ge(s["shifted"], G * (b - 1) + g + 1 + s.past["shifted"])
                        mm = nc.tensor.matmul(bank[:, g, :], qT[p1][:, :], wide[p1][:, HG * g:HG * g + HG, :],
                                              start=True, stop=s.cross)
                        if not s.cross:
                            mm = nc.tensor.matmul(bank[:, g, :], ident16[:, :], future[:, :, :], start=False, stop=True)
                        mm.then_inc(s["score_ps"], 1)
                if there(i + 2):
                    b = i + 2
                    pe.wait_ge(s["both"], b + 1 + s.past["both"])
                    if later(b, 3):
                        pe.wait_ge(s["headsT"], b - 2 + s.past["headsT"])
                    elif b >= 1:
                        pe.wait_ge(s["k"], b + s.past["k"])
                        pe.wait_ge(s["q"], b + s.past["q"])
                    nc.tensor.matmul(bank[:, 6, 0:P], s.wq, bothT[p0][:, 0, :], start=True, stop=True)
                    nc.tensor.matmul(bank[:, 6, P:2 * P], s.wk, bothT[p0][:, s.kv, :],
                                     start=True, stop=True).then_inc(s["qk_ps"], 1)
                if there(i - 1):
                    b = i - 1
                    pe.wait_ge(s["merged"], b + 1 + s.past["merged"])
                    if later(b, 1):
                        pe.wait_ge(s["done"], b + s.past["done"])
                    nc.tensor.transpose(bank[:, 7, 0:P], merged[p1][:, :], ident[:, :]).then_inc(s["mT_ps"], 1)
                if there(i):
                    b = i
                    for g in range(G):
                        pe.wait_ge(s["ready"], G * b + g + 1 + s.past["ready"])
                        if g >= 2:
                            pe.wait_ge(s["probsT"], G * b + g - 1 + s.past["probsT"])
                        elif g == 0 and later(b, 1):
                            pe.wait_ge(s["merged"], b + s.past["merged"])
                        elif g == 1 and (not isinstance(b, int) or b + 2 < NB):
                            pe.wait_ge(s["both"], b + 3 + s.past["both"])
                        elif g == 1:
                            pe.wait_ge(s["both"], NB + s.past["both"])
                            pe.wait_ge(s["values"], min(b + 2, NB) + s.past["values"])
                        for j in range(HG):
                            mm = nc.tensor.transpose(quarters(4 + g % 2)[:, j, :], probs[p0][:, HG * g + j, :], ident[:, :])
                        mm.then_inc(s["turn_ps"], 1)
                if there(i - 1):
                    b = i - 1
                    pe.wait_ge(s["mT"], b + 1 + s.past["mT"])
                    mm = nc.tensor.matmul(bank[:, 7, 0:P], mergedT[p1][:, :], s.wo, start=True, stop=s.cross)
                    if not s.cross:
                        mm = nc.tensor.matmul(bank[:, 7, 0:P], ones_row[:, :], c0_bo[0:1, :], start=False, stop=True)
                    mm.then_inc(s["out_ps"], 1)
                if there(i):
                    b = i
                    pe.wait_ge(s["values"], b + 1 + s.past["values"])
                    if s.cross and isinstance(b, int) and b == 0:
                        pe.wait_ge(s["cleared"], 4 + s.past["cleared"])
                    pe.wait_ge(s["probsT"], G * b + G + s.past["probsT"])
                    if not isinstance(b, int) or b + 2 < NB:
                        pe.wait_ge(s["k"], b + 3 + s.past["k"])
                        pe.wait_ge(s["q"], b + 3 + s.past["q"])
                    for h in range(H):
                        j = 32 * (h % 4)
                        mm = nc.tensor.matmul(quarters(6)[j:j + 32, h // 4, :], values[p0][:, h, :], probsT[:, h, :],
                                              start=True, stop=True)
                    mm.then_inc(s["av_ps"], 1)
                if there(i + 2):
                    b = i + 2
                    pe.wait_ge(s["both"], b + 1 + s.past["both"])
                    if there(i):
                        pe.wait_ge(s["probsT"], G * i + G + s.past["probsT"])
                    mm = nc.tensor.matmul(bank[:, 5, 0:P], bothT[p0][:, s.kv, :], s.wv, start=True, stop=s.cross)
                    if not s.cross:
                        mm = nc.tensor.matmul(bank[:, 5, 0:P], ones_row[:, :], c0_bv[0:1, :], start=False, stop=True)
                    mm.then_inc(s["v_ps"], 1)
                if there(i + 3):
                    b = i + 3
                    pe.wait_ge(s["normed"], b + 1 + s.past["normed"])
                    if s.cross:
                        pe.wait_ge(s["ctx"], 16 * (b + 1) + s.past["ctx"])
                    if s.cross:
                        nc.tensor.transpose(quarters(5)[:, 2, :], ctx_rows[p1][:, :], ident[:, :])
                    nc.tensor.transpose(quarters(5)[:, 1, :], normed[p1][:, :], ident[:, :]).then_inc(s["both_ps"], 1)
                if there(i):
                    b = i
                    pe.wait_ge(s["headsT"], b + 1 + s.past["headsT"])
                    for g in range(G):
                        mm = nc.tensor.transpose(quarters(4)[:, g, :], headsT[p0][:, g, :], ident[:, :])
                    mm.then_inc(s["back_ps"], 1)

            skewed(pe, iteration, *NARROW)

        def act_narrow(act, s):
            after_previous(act, s.n)

            def iteration(i, par):
                p0, p1 = par, 1 - par
                if there(i + 2):
                    b = i + 2
                    act.wait_ge(s["qk_ps"], b + 1 + s.past["qk_ps"])
                    if later(b, 2):
                        act.wait_ge(s["score_ps"], G * (b - 1) + s.past["score_ps"])
                    if s.cross:
                        nc.scalar.activation(kT[p0][:, :], bank[:, 6, P:2 * P], ACT.Copy).then_inc(s["k"], 1)
                        nc.scalar.activation(qT[p0][:, :], bank[:, 6, 0:P], ACT.Copy).then_inc(s["q"], 1)
                    else:
                        nc.scalar.activation(kT[p0][:, :], bank[:, 6, P:2 * P], ACT.Identity,
                                             bias=cols[:, C_BK:C_BK + 1]).then_inc(s["k"], 1)
                        nc.scalar.activation(qT[p0][:, :], bank[:, 6, 0:P], ACT.Identity,
                                             bias=cols[:, C_BQ:C_BQ + 1]).then_inc(s["q"], 1)
                if there(i - 1):
                    b = i - 1
                    act.wait_ge(s["mT_ps"], b + 1 + s.past["mT_ps"])
                    if later(b, 2):
                        act.wait_ge(s["out_ps"], b - 1 + s.past["out_ps"])
                    nc.scalar.activation(mergedT[p1][:, :], bank[:, 7, 0:P], ACT.Copy).then_inc(s["mT"], 1)

                def exps(g):
                    if there(i + 1):
                        act.wait_ge(s["shifted"], G * (i + 1) + g + 1 + s.past["shifted"])
                        pr = probs[p1][:, HG * g:HG * g + HG, :]
                        nc.scalar.activation(pr, pr, ACT.Exp, scale=s.scale).then_inc(s["probs"], 1)

                def turned_probs(g):
                    if there(i):
                        act.wait_ge(s["turn_ps"], G * i + g + 1 + s.past["turn_ps"])
                        if g == 0 and later(i, 1):
                            act.wait_ge(s["av_ps"], i + s.past["av_ps"])
                        nc.scalar.activation(probsT[:, HG * g:HG * g + HG, :], quarters(4 + g % 2),
                                             ACT.Copy).then_inc(s["probsT"], 1)

                exps(0)
                turned_probs(0)
                turned_probs(1)
                exps(1)
                turned_probs(2)
                turned_probs(3)
                exps(2)
                if there(i):
                    act.wait_ge(s["av_ps"], i + 1 + s.past["av_ps"])
                    if later(i, 2):
                        act.wait_ge(s["back_ps"], i - 1 + s.past["back_ps"])
                    nc.scalar.activation(headsT[p0][:, :, :], quarters(6), ACT.Copy).then_inc(s["headsT"], 1)
                if there(i + 2):
                    b = i + 2
                    act.wait_ge(s["v_ps"], b + 1 + s.past["v_ps"])
                    if there(i + 3):
                        act.wait_ge(s["both_ps"], i + 4 + s.past["both_ps"])
                    v8 = values[p0][:, :, 0:HD]
                    src = bank[:, 5, 0:P].rearrange("p (h d) -> p h d", d=HD)
                    nc.scalar.activation(v8, src, ACT.Copy).then_inc(s["values"], 1)
                if there(i + 3):
                    b = i + 3
                    act.wait_ge(s["both_ps"], b + 1 + s.past["both_ps"])
                    if later(b, 2):
                        act.wait_ge(s["v_ps"], b - 1 + s.past["v_ps"])
                    if s.cross:
                        nc.scalar.activation(bothT[p1][:, :, :], quarters(5)[:, 1:3, :], ACT.Copy).then_inc(s["both"], 1)
                    else:
                        nc.scalar.activation(bothT[p1][:, 0, :], quarters(5)[:, 1, :], ACT.Identity,
                                             scale=cols[:, C_LN1W:C_LN1W + 1],
                                             bias=cols[:, C_LN1B:C_LN1B + 1]).then_inc(s["both"], 1)
                exps(3)

            skewed(act, iteration, *NARROW)

        def pool_narrow(pool, s):
            after_previous(pool, s.n)
            chain = Chain(1 if s.cross else 2, s.past["pool_chain"])
            if s.cross:
                for p in range(2):
                    nc.gpsimd.memset(values[p][:, :, HD:32], 0.0).then_inc(s["cleared"], 1)
                pool.wait_ge(s["cleared"], 2 + s.past["cleared"])
                for p in range(2):
                    nc.gpsimd.memset(values[p][:, :, HD:HD + 1], 1.0).then_inc(s["cleared"], 1)

            def iteration(i, par):
                p0, p1 = par, 1 - par
                if there(i + 3):
                    b = i + 3
                    chain.begin(b)
                    pool.wait_ge(s["stat"], b + 1 + s.past["stat"])
                    take(pool, L["passed"])
                    nc.gpsimd.tensor_scalar(var_eps[:, p1, :], moments[:, p1, 1:2], EPS, None, ALU.add).then_inc(s["pool_chain"], 1)
                    pool.wait_ge(s["pool_chain"], chain.next())
                    nc.gpsimd.tensor_tensor(rstd[:, p1, :], var_eps[:, p1, :], minus_half[:, 0:1], ALU.pow).then_inc(s["rstd"], 1)
                    if not s.cross:
                        pool.wait_ge(s["stat2"], b + 1 + s.past["stat2"])
                        take(pool, L["passed"])
                        nc.gpsimd.tensor_scalar(var_eps[:, p1, :], moments2[:, p1, 1:2], EPS, None, ALU.add).then_inc(s["pool_chain"], 1)
                        pool.wait_ge(s["pool_chain"], chain.next())
                        nc.gpsimd.tensor_tensor(rstd2[:, p1, :], var_eps[:, p1, :], minus_half[:, 0:1],
                                                ALU.pow).then_inc(s["rstd2"], 1)
                    chain.end()
                if there(i + 2):
                    b = i + 2
                    pool.wait_ge(s["k"], b + 1 + s.past["k"])
                    for g in range(G):
                        if later(b, 2):
                            pool.wait_ge(s["score_ps"], G * (b - 2) + g + 1 + s.past["score_ps"])
                        nc.gpsimd.tensor_tensor(
                            wide[p0][:, HG * g:HG * g + HG, :], kT[p0][:, :].unsqueeze(1).to_broadcast([P, HG, P]),
                            head_of[:, HG * g:HG * g + HG].unsqueeze(2).to_broadcast([P, HG, P]),
                            ALU.mult).then_inc(s["masked"], 1)
                if s.cross and there(i + 1):
                    b = i + 1
                    for g in range(G):
                        pool.wait_ge(s["probs"], G * b + g + 1 + s.past["probs"])
                        pr = probs[p1][:, HG * g:HG * g + HG, :]
                        take(pool, L["passed"])
                        nc.gpsimd.affine_select(out=pr, in_=pr, compare_op=ALU.is_ge, fill=0.0, base=0,
                                                pattern=[[0, HG], [-1, P]], channel_multiplier=1).then_inc(s["clean"], 1)

            skewed(pool, iteration, *NARROW)

        def dve_narrow(dve, s):
            after_previous(dve, s.n)
            stat_chain = Chain(1 if s.cross else 2, s.past["stat_chain"])
            norm_chain = Chain(2 if s.cross else 1, s.past["norm_chain"])
            soft_chain = Chain(G, s.past["chain"])

            def iteration(i, par):
                p0, p1 = par, 1 - par
                if there(i + 3):
                    b = i + 3
                    stat_chain.begin(b)
                    nc.vector.bn_stats(stats[:, p1, :], x[:, b, :]).then_inc(s["stat_chain"], 1)
                    dve.wait_ge(s["stat_chain"], stat_chain.next())
                    take(dve, L["passed"])
                    nc.vector.bn_aggr(moments[:, p1, :], stats[:, p1, :]).then_inc(s["stat"], 1)
                if there(i - 1):
                    b = i - 1
                    norm_chain.begin(b)
                    dve.wait_ge(s["back_ps"], b + 1 + s.past["back_ps"])
                    heads = bank[:, 4, :].rearrange("p (h w) -> p h w", w=32)
                    src = heads[:, :, HD]
                    if s.cross:
                        nc.vector.tensor_scalar(den1[p1][:, :], src, 1.0, None, ALU.add).then_inc(s["norm_chain"], 1)
                        dve.wait_ge(s["norm_chain"], norm_chain.next())
                        src = den1[p1][:, :]
                    nc.vector.reciprocal(den[p1][:, :], src).then_inc(s["norm_chain"], 1)
                    dve.wait_ge(s["norm_chain"], norm_chain.next())
                    norm_chain.end()
                    if later(b, 2):
                        dve.wait_ge(s["mT_ps"], b - 1 + s.past["mT_ps"])
                    nc.vector.tensor_tensor(merged[p1][:, :].rearrange("p (h d) -> p h d", d=HD), heads[:, :, 0:HD],
                                            den[p1][:, :].unsqueeze(2).to_broadcast([P, H, HD]),
                                            ALU.mult).then_inc(s["merged"], 1)

                def soften(g):
                    b = i + 1
                    if there(b):
                        if g == 0:
                            soft_chain.begin(b)
                        hs = slice(HG * g, HG * g + HG)
                        dve.wait_ge(s["score_ps"], G * b + g + 1 + s.past["score_ps"])
                        nc.vector.tensor_reduce(peak[p1][:, hs], quarters(g), AX.X, ALU.max).then_inc(s["chain"], 1)
                        dve.wait_ge(s["chain"], soft_chain.next())
                        if later(b, 2):
                            dve.wait_ge(s["turn_ps"], G * (b - 2) + g + 1 + s.past["turn_ps"])
                        nc.vector.tensor_tensor(probs[p1][:, hs, :], quarters(g),
                                                peak[p1][:, hs].unsqueeze(2).to_broadcast([P, HG, P]),
                                                ALU.subtract).then_inc(s["shifted"], 1)

                def normalise(mom, r, src, dst):
                    return nc.vector.tensor_scalar(dst, src, mom[:, p1, 0:1], r[:, p1, :], ALU.subtract, ALU.mult)

                soften(0)
                if not s.cross and there(i + 3):
                    b = i + 3
                    dve.wait_ge(s["rstd"], b + 1 + s.past["rstd"])
                    normalise(moments, rstd, x[:, b, :], y[:, b, :]).then_inc(s["zed"], 1)
                    dve.wait_ge(s["zed"], b + 1 + s.past["zed"])
                    take(dve, L["passed"])
                    nc.vector.bn_stats(stats2[:, p1, :], y[:, b, :]).then_inc(s["stat_chain"], 1)
                    dve.wait_ge(s["stat_chain"], stat_chain.next())
                    take(dve, L["passed"])
                    nc.vector.bn_aggr(moments2[:, p1, :], stats2[:, p1, :]).then_inc(s["stat2"], 1)
                soften(1)
                if there(i - 1):
                    b = i - 1
                    dve.wait_ge(s["out_ps"], b + 1 + s.past["out_ps"])
                    if s.cross:
                        nc.vector.tensor_tensor(x[:, b, :], bank[:, 7, 0:P], x[:, b, :], ALU.add).then_inc(s["done"], 1)
                    else:
                        nc.vector.tensor_tensor(y[:, b, :], bank[:, 7, 0:P], y[:, b, :], ALU.add).then_inc(s["done"], 1)
                soften(2)
                if there(i + 3):
                    b = i + 3
                    if later(b, 2):
                        dve.wait_ge(s["both_ps"], b - 1 + s.past["both_ps"])
                    if s.cross:
                        dve.wait_ge(s["rstd"], b + 1 + s.past["rstd"])
                        normalise(moments, rstd, x[:, b, :], normed[p1][:, :]).then_inc(s["normed"], 1)
                    else:
                        dve.wait_ge(s["rstd2"], b + 1 + s.past["rstd2"])
                        normalise(moments2, rstd2, y[:, b, :], normed[p1][:, :]).then_inc(s["normed"], 1)
                soften(3)

            skewed(dve, iteration, *NARROW)

        LA = sems("linear", """stat rstd normed turned_ps turned qkv_ps raw v negative exps mapped kv_ps kv qT_ps qT att_ps
                               merged mT_ps mT out_ps done chain pool_chain map_chain""")
        LINEAR = (-3, 4, 12, 17)
        N_LINEAR = 4

        def pe_linear(pe):
            after_previous(pe, N_LINEAR)

            def iteration(i, par):
                p0, p1 = par, 1 - par
                if there(i + 2):
                    b = i + 2
                    pe.wait_ge(LA["turned"], b + 1)
                    if later(b, 1):
                        pe.wait_ge(LA["v"], b)
                    nc.tensor.matmul(bank[:, 1, 0:3 * P], bothT[p0][:, 0, :], turned[:, A1_QKV:A1_QKV + 3, :],
                                     start=True, stop=True).then_inc(LA["qkv_ps"], 1)
                if there(i + 1):
                    b = i + 1
                    pe.wait_ge(LA["mapped"], b + 1)
                    pe.wait_ge(LA["v"], b + 1)
                    if later(b, 1):
                        pe.wait_ge(LA["kv"], b)
                        pe.wait_ge(LA["qT"], b)
                    nc.tensor.matmul(bank[:, 2, 0:2 * P], lin_qk[p1][:, 1, :], lin_v[p1][:, :, :],
                                     start=True, stop=True).then_inc(LA["kv_ps"], 1)
                    nc.tensor.transpose(bank[:, 3, 0:P], lin_qk[p1][:, 0, :], ident[:, :]).then_inc(LA["qT_ps"], 1)
                if there(i):
                    b = i
                    pe.wait_ge(LA["kv"], b + 1)
                    pe.wait_ge(LA["qT"], b + 1)
                    if later(b, 1):
                        pe.wait_ge(LA["merged"], b)
                    nc.tensor.matmul(bank[:, 4, 0:2 * P], qT[p0][:, :], lin_kv[p0][:, :], start=True,
                                     stop=True).then_inc(LA["att_ps"], 1)
                if there(i - 1):
                    b = i - 1
                    pe.wait_ge(LA["merged"], b + 1)
                    if later(b, 1):
                        pe.wait_ge(LA["mT"], b)
                    nc.tensor.transpose(bank[:, 5, 0:P], merged[p1][:, :], ident[:, :]).then_inc(LA["mT_ps"], 1)
                if there(i - 2):
                    b = i - 2
                    pe.wait_ge(LA["mT"], b + 1)
                    if later(b, 1):
                        pe.wait_ge(LA["done"], b)
                    nc.tensor.matmul(bank[:, 6, 0:P], mergedT[p0][:, :], turned[:, A1_O, :], start=True,
                                     stop=True).then_inc(LA["out_ps"], 1)
                if there(i + 3):
                    b = i + 3
                    pe.wait_ge(LA["normed"], b + 1)
                    if later(b, 1):
                        pe.wait_ge(LA["turned"], b)
                    nc.tensor.transpose(bank[:, 0, 0:P], normed[p1][:, :], ident[:, :]).then_inc(LA["turned_ps"], 1)

            skewed(pe, iteration, *LINEAR)

        def act_linear(act):
            after_previous(act, N_LINEAR)

            def iteration(i, par):
                p0, p1 = par, 1 - par
                if there(i + 2):
                    b = i + 2
                    act.wait_ge(LA["qkv_ps"], b + 1)
                    if later(b, 2):
                        act.wait_ge(LA["mapped"], b - 1)
                        act.wait_ge(LA["kv_ps"], b - 1)
                    nc.scalar.activation(lin_raw[p0][:, :, :], bank[:, 1, 0:2 * P].rearrange("p (s d) -> p s d", s=2),
                                         ACT.Copy).then_inc(LA["raw"], 1)
                    nc.scalar.activation(lin_v[p0][:, 0, :], bank[:, 1, 2 * P:3 * P], ACT.Copy).then_inc(LA["v"], 1)
                if there(i + 1):
                    b = i + 1
                    act.wait_ge(LA["qT_ps"], b + 1)
                    if later(b, 2):
                        act.wait_ge(LA["att_ps"], b - 1)
                    nc.scalar.activation(qT[p1][:, :], bank[:, 3, 0:P], ACT.Copy).then_inc(LA["qT"], 1)
                if there(i - 1):
                    b = i - 1
                    act.wait_ge(LA["mT_ps"], b + 1)
                    if later(b, 2):
                        act.wait_ge(LA["out_ps"], b - 1)
                    nc.scalar.activation(mergedT[p1][:, :], bank[:, 5, 0:P], ACT.Copy).then_inc(LA["mT"], 1)
                if there(i + 2):
                    b = i + 2
                    act.wait_ge(LA["negative"], b + 1)
                    nc.scalar.activation(lin_exp[p0][:, :, :], lin_neg[p0][:, :, :], ACT.Exp).then_inc(LA["exps"], 1)
                if there(i + 3):
                    b = i + 3
                    act.wait_ge(LA["turned_ps"], b + 1)
                    if later(b, 2):
                        act.wait_ge(LA["qkv_ps"], b - 1)
                    nc.scalar.activation(bothT[p1][:, 0, :], bank[:, 0, 0:P], ACT.Copy).then_inc(LA["turned"], 1)

            skewed(act, iteration, *LINEAR)

        def pool_linear(pool):
            after_previous(pool, N_LINEAR)
            chain = Chain(1)
            nc.gpsimd.memset(lin_v[0][:, 1, :], 1.0)
            nc.gpsimd.memset(lin_v[1][:, 1, :], 1.0)
            nc.gpsimd.tensor_copy(block_of[:, :].rearrange("p (h d) -> p h d", d=HD),
                                  head_of[:, :].unsqueeze(2).to_broadcast([P, H, HD])).then_inc(LA["map_chain"], 1)

            def iteration(i, par):
                p1 = 1 - par
                if there(i + 3):
                    b = i + 3
                    chain.begin(b)
                    pool.wait_ge(LA["stat"], b + 1)
                    take(pool, L["passed"])
                    nc.gpsimd.tensor_scalar(var_eps[:, p1, :], moments[:, p1, 1:2], EPS, None, ALU.add).then_inc(LA["pool_chain"], 1)
                    pool.wait_ge(LA["pool_chain"], chain.next())
                    nc.gpsimd.tensor_tensor(rstd[:, p1, :], var_eps[:, p1, :], minus_half[:, 0:1], ALU.pow).then_inc(LA["rstd"], 1)

            skewed(pool, iteration, *LINEAR)

        def dve_linear(dve):
            after_previous(dve, N_LINEAR)
            dve.wait_ge(LA["map_chain"], 1)
            chain = Chain(2)

            def iteration(i, par):
                p0, p1 = par, 1 - par
                if there(i + 3):
                    b = i + 3
                    nc.vector.bn_stats(stats[:, p1, :], x[:, b, :]).then_inc(LA["map_chain"], 1)
                    dve.wait_ge(LA["map_chain"], b + 2)
                    take(dve, L["passed"])
                    nc.vector.bn_aggr(moments[:, p1, :], stats[:, p1, :]).then_inc(LA["stat"], 1)
                if there(i):
                    b = i
                    chain.begin(b)
                    dve.wait_ge(LA["att_ps"], b + 1)
                    nc.vector.tensor_scalar(den1[p0][:, :], bank[:, 4, P:2 * P:HD], 1e-6, None, ALU.add).then_inc(LA["chain"], 1)
                    dve.wait_ge(LA["chain"], chain.next())
                    nc.vector.reciprocal(den[p0][:, :], den1[p0][:, :]).then_inc(LA["chain"], 1)
                    dve.wait_ge(LA["chain"], chain.next())
                    if later(b, 2):
                        dve.wait_ge(LA["mT_ps"], b - 1)
                    nc.vector.tensor_tensor(merged[p0][:, :].rearrange("p (h d) -> p h d", d=HD),
                                            bank[:, 4, 0:P].rearrange("p (h d) -> p h d", d=HD),
                                            den[p0][:, :].unsqueeze(2).to_broadcast([P, H, HD]),
                                            ALU.mult).then_inc(LA["merged"], 1)
                if there(i + 2):
                    b = i + 2
                    dve.wait_ge(LA["raw"], b + 1)
                    if later(b, 2):
                        dve.wait_ge(LA["exps"], b - 1)
                    nc.vector.tensor_scalar(lin_neg[p0][:, :, :], lin_raw[p0][:, :, :], 0.0, None, ALU.min).then_inc(LA["negative"], 1)
                if there(i + 1):
                    b = i + 1
                    dve.wait_ge(LA["kv_ps"], b + 1)
                    if later(b, 2):
                        dve.wait_ge(LA["att_ps"], b - 1)
                    nc.vector.tensor_tensor(lin_kv[p1][:, :].rearrange("p (s d) -> p s d", s=2),
                                            bank[:, 2, 0:2 * P].rearrange("p (s d) -> p s d", s=2),
                                            block_of[:, :].unsqueeze(1).to_broadcast([P, 2, P]), ALU.mult).then_inc(LA["kv"], 1)
                if there(i - 2):
                    b = i - 2
                    dve.wait_ge(LA["out_ps"], b + 1)
                    nc.vector.tensor_tensor(x[:, b, :], bank[:, 6, 0:P], x[:, b, :], ALU.add).then_inc(LA["done"], 1)
                if there(i + 2):
                    b = i + 2
                    dve.wait_ge(LA["exps"], b + 1)
                    if later(b, 2):
                        dve.wait_ge(LA["kv_ps"], b - 1)
                        dve.wait_ge(LA["qT_ps"], b - 1)
                    nc.vector.scalar_tensor_tensor(out=lin_qk[p0][:, :, :], in0=lin_raw[p0][:, :, :], scalar=0.0,
                                                   in1=lin_exp[p0][:, :, :], op0=ALU.max, op1=ALU.add).then_inc(LA["mapped"], 1)
                if there(i + 3):
                    b = i + 3
                    dve.wait_ge(LA["rstd"], b + 1)
                    if later(b, 2):
                        dve.wait_ge(LA["turned_ps"], b - 1)
                    nc.vector.tensor_scalar(normed[p1][:, :], x[:, b, :], moments[:, p1, 0:1], rstd[:, p1, :],
                                            ALU.subtract, ALU.mult).then_inc(LA["normed"], 1)

            skewed(dve, iteration, *LINEAR)

        W = sems("wide", """ctx stat rstd normed both_ps both through_ps through score_ps shifted probs sums clean
                            turn_ps probsT av_ps wideT v_ps v out_ps done chain sum_chain stat_chain pool_chain""")
        WIDE = (-3, 3, 13, 15)
        N_WIDE = 5

        def sp_wide(sp):
            after_previous(sp, N_WIDE)

            def load(b, p):
                if later(b, 2):
                    sp.wait_ge(W["both_ps"], b - 1)
                    take(sp, L["passed"])
                if later(b, 1):
                    sp.wait_ge(W["ctx"], 16 * b)
                sp.dma_start(ctx_rows[p][:, :], a["ctx_1024"][b, :, :]).then_inc(W["ctx"], 16)

            load(0, 0)
            load(1, 1)
            with sp.Fori(1, NB // 2) as pair:
                load(2 * pair, 0)
                load(2 * pair + 1, 1)

        def pe_wide(pe):
            after_previous(pe, N_WIDE)

            def iteration(i, par):
                p0, p1 = par, 1 - par
                if there(i + 1):
                    b = i + 1
                    pe.wait_ge(W["both"], b + 1)
                    for g in range(G):
                        pe.wait_ge(W["through"], G * b + g + 1)
                        if later(b, 1):
                            pe.wait_ge(W["shifted"], G * (b - 1) + g + 1)
                        for j in range(HG):
                            mm = nc.tensor.matmul(quarters(g)[:, j, :], wide[p1][:, HG * g + j, :], bothT[p1][:, 1, :],
                                                  start=True, stop=True)
                        mm.then_inc(W["score_ps"], 1)
                if there(i):
                    b = i
                    for g in range(G):
                        pe.wait_ge(W["clean"], G * b + g + 1)
                        if g >= 2:
                            pe.wait_ge(W["probsT"], G * b + g - 1)
                        elif not isinstance(b, int) or b + 1 < NB:
                            pe.wait_ge(W["v"], 2 * (b + 1) + g + 1)
                        for j in range(HG):
                            mm = nc.tensor.transpose(quarters(4 + g % 2)[:, j, :], probs[p0][:, HG * g + j, :], ident[:, :])
                        mm.then_inc(W["turn_ps"], 1)
                if there(i + 2):
                    b = i + 2
                    pe.wait_ge(W["both"], b + 1)
                    for g in range(G):
                        if g >= 2:
                            pe.wait_ge(W["through"], G * b + g - 1)
                        elif there(i):
                            pe.wait_ge(W["probsT"], G * i + g + 3)
                        elif b >= 1:
                            pe.wait_ge(W["v"], 2 * (b - 1) + g + 1)
                        for j in range(HG):
                            mm = nc.tensor.matmul(quarters(4 + g % 2)[:, j, :], x1_m[:, HG * g + j, :], bothT[p0][:, 0, :],
                                                  start=True, stop=True)
                        mm.then_inc(W["through_ps"], 1)
                if there(i):
                    b = i
                    for half in range(2):
                        pe.wait_ge(W["v"], 2 * b + half + 1)
                        pe.wait_ge(W["probsT"], G * b + 2 * half + 2)
                        if half == 0 and (not isinstance(b, int) or b + 2 < NB):
                            pe.wait_ge(W["both"], b + 3)
                        if half == 1 and later(b, 1):
                            pe.wait_ge(W["done"], b)
                        for h in range(8 * half, 8 * half + 8):
                            r = WH * (h % 2)
                            mm = nc.tensor.matmul(quarters(6 + half)[r:r + WH, (h // 2) % 4, :],
                                                  v_wide[p0][:, WH * h:WH * h + WH], probsT[:, h, :], start=True, stop=True)
                        mm.then_inc(W["av_ps"], 1)
                if there(i + 2):
                    b = i + 2
                    for half in range(2):
                        pe.wait_ge(W["through"], G * b + half + 3)
                        nc.tensor.matmul(bank[:, 4 + half, :], bothT[p0][:, 1, :], x1_v[:, 512 * half:512 * half + 512],
                                         start=True, stop=True).then_inc(W["v_ps"], 1)
                if there(i + 3):
                    b = i + 3
                    pe.wait_ge(W["normed"], b + 1)
                    pe.wait_ge(W["ctx"], 16 * (b + 1))
                    if there(i):
                        pe.wait_ge(W["wideT"], 2 * i + 1)
                    elif b >= 1:
                        pe.wait_ge(W["both"], b)
                    nc.tensor.transpose(quarters(6)[:, 0, :], normed[p1][:, :], ident[:, :])
                    nc.tensor.transpose(quarters(6)[:, 1, :], ctx_rows[p1][:, :], ident[:, :]).then_inc(W["both_ps"], 1)
                if there(i):
                    b = i
                    pe.wait_ge(W["wideT"], 2 * b + 2)
                    for c in range(WB):
                        mm = nc.tensor.matmul(bank[:, 7, 0:P], wideT[:, c, :], x1_o[:, c, :], start=(c == 0),
                                              stop=(c == WB - 1))
                    mm.then_inc(W["out_ps"], 1)

            skewed(pe, iteration, *WIDE)

        def act_wide(act):
            after_previous(act, N_WIDE)

            def iteration(i, par):
                p0, p1 = par, 1 - par

                def exps(g):
                    if there(i + 1):
                        act.wait_ge(W["shifted"], G * (i + 1) + g + 1)
                        pr = probs[p1][:, HG * g:HG * g + HG, :]
                        nc.scalar.activation(pr, pr, ACT.Exp, scale=WH ** -0.5).then_inc(W["probs"], 1)

                def turned_probs(g):
                    if there(i):
                        act.wait_ge(W["turn_ps"], G * i + g + 1)
                        if g == 0 and later(i, 1):
                            act.wait_ge(W["av_ps"], 2 * i)
                        nc.scalar.activation(probsT[:, HG * g:HG * g + HG, :], quarters(4 + g % 2),
                                             ACT.Copy).then_inc(W["probsT"], 1)

                def through(g):
                    if there(i + 2):
                        b = i + 2
                        act.wait_ge(W["through_ps"], G * b + g + 1)
                        if g == 0 and later(b, 2):
                            act.wait_ge(W["score_ps"], G * (b - 1))
                        nc.scalar.activation(wide[p0][:, HG * g:HG * g + HG, :], quarters(4 + g % 2),
                                             ACT.Copy).then_inc(W["through"], 1)

                exps(0)
                turned_probs(0)
                turned_probs(1)
                exps(1)
                turned_probs(2)
                turned_probs(3)
                exps(2)
                through(0)
                through(1)
                exps(3)
                through(2)
                through(3)
                if there(i):
                    for half in range(2):
                        act.wait_ge(W["av_ps"], 2 * i + half + 1)
                        if half == 0 and later(i, 1):
                            act.wait_ge(W["out_ps"], i)
                        nc.scalar.activation(wideT[:, 4 * half:4 * half + 4, :], quarters(6 + half),
                                             ACT.Copy).then_inc(W["wideT"], 1)
                if there(i + 2):
                    b = i + 2
                    for half in range(2):
                        act.wait_ge(W["v_ps"], 2 * b + half + 1)
                        nc.scalar.activation(v_wide[p0][:, 512 * half:512 * half + 512], bank[:, 4 + half, :],
                                             ACT.Copy).then_inc(W["v"], 1)
                if there(i + 3):
                    b = i + 3
                    act.wait_ge(W["both_ps"], b + 1)
                    if later(b, 2):
                        act.wait_ge(W["score_ps"], G * (b - 1))
                        act.wait_ge(W["v_ps"], 2 * (b - 1))
                    nc.scalar.activation(bothT[p1][:, :, :], quarters(6)[:, 0:2, :], ACT.Copy).then_inc(W["both"], 1)

            skewed(act, iteration, *WIDE)

        def pool_wide(pool):
            after_previous(pool, N_WIDE)
            chain = Chain(1)

            def iteration(i, par):
                p1 = 1 - par
                if there(i + 3):
                    b = i + 3
                    chain.begin(b)
                    pool.wait_ge(W["stat"], b + 1)
                    take(pool, L["passed"])
                    nc.gpsimd.tensor_scalar(var_eps[:, p1, :], moments[:, p1, 1:2], EPS, None, ALU.add).then_inc(W["pool_chain"], 1)
                    pool.wait_ge(W["pool_chain"], chain.next())
                    nc.gpsimd.tensor_tensor(rstd[:, p1, :], var_eps[:, p1, :], minus_half[:, 0:1], ALU.pow).then_inc(W["rstd"], 1)
                if there(i + 1):
                    b = i + 1
                    for g in range(G):
                        pool.wait_ge(W["sums"], G * b + g + 1)
                        hs = slice(HG * g, HG * g + HG)
                        nc.gpsimd.tensor_tensor(probs[p1][:, hs, :], probs[p1][:, hs, :],
                                                den[p1][:, hs].unsqueeze(2).to_broadcast([P, HG, P]),
                                                ALU.mult).then_inc(W["clean"], 1)

            skewed(pool, iteration, *WIDE)

        def dve_wide(dve):
            after_previous(dve, N_WIDE)
            stat_chain = Chain(1)
            soft_chain = Chain(G)
            sum_chain = Chain(G)

            def iteration(i, par):
                p0, p1 = par, 1 - par
                if there(i + 3):
                    b = i + 3
                    stat_chain.begin(b)
                    nc.vector.bn_stats(stats[:, p1, :], x[:, b, :]).then_inc(W["stat_chain"], 1)
                    dve.wait_ge(W["stat_chain"], stat_chain.next())
                    take(dve, L["passed"])
                    nc.vector.bn_aggr(moments[:, p1, :], stats[:, p1, :]).then_inc(W["stat"], 1)

                def soften(g):
                    b = i + 1
                    if there(b):
                        if g == 0:
                            soft_chain.begin(b)
                            sum_chain.begin(b)
                        hs = slice(HG * g, HG * g + HG)
                        dve.wait_ge(W["score_ps"], G * b + g + 1)
                        nc.vector.tensor_reduce(peak[p1][:, hs], quarters(g), AX.X, ALU.max).then_inc(W["chain"], 1)
                        dve.wait_ge(W["chain"], soft_chain.next())
                        if later(b, 2):
                            dve.wait_ge(W["turn_ps"], G * (b - 2) + g + 1)
                        nc.vector.tensor_tensor(probs[p1][:, hs, :], quarters(g),
                                                peak[p1][:, hs].unsqueeze(2).to_broadcast([P, HG, P]),
                                                ALU.subtract).then_inc(W["shifted"], 1)

                def total(g):
                    b = i + 1
                    if there(b):
                        hs = slice(HG * g, HG * g + HG)
                        dve.wait_ge(W["probs"], G * b + g + 1)
                        nc.vector.tensor_reduce(den1[p1][:, hs], probs[p1][:, hs, :], AX.X, ALU.add).then_inc(W["sum_chain"], 1)
                        dve.wait_ge(W["sum_chain"], sum_chain.next())
                        nc.vector.reciprocal(den[p1][:, hs], den1[p1][:, hs]).then_inc(W["sums"], 1)

                soften(0)
                soften(1)
                total(0)
                soften(2)
                total(1)
                soften(3)
                if there(i + 3):
                    b = i + 3
                    dve.wait_ge(W["rstd"], b + 1)
                    if later(b, 2):
                        dve.wait_ge(W["both_ps"], b - 1)
                    nc.vector.tensor_scalar(normed[p1][:, :], x[:, b, :], moments[:, p1, 0:1], rstd[:, p1, :],
                                            ALU.subtract, ALU.mult).then_inc(W["normed"], 1)
                total(2)
                total(3)
                if there(i):
                    b = i
                    dve.wait_ge(W["out_ps"], b + 1)
                    nc.vector.tensor_tensor(x[:, b, :], bank[:, 7, 0:P], x[:, b, :], ALU.add).then_inc(W["done"], 1)

            skewed(dve, iteration, *WIDE)

        heads_end.close()
        m_normT = [sb(f"m_normT{p}", [P, P]) for p in range(2)]
        m_normed = [sb(f"m_normed{p}", [P, P]) for p in range(2)]
        m_stats = sb("m_stats", [P, 2, 6])
        m_moments = sb("m_moments", [P, 2, 2])
        m_var = sb("m_var", [P, 2, 1])
        m_rstd = sb("m_rstd", [P, 2, 1])
        logits = sb("logits", [P, NB, E])
        gate_tmp = [sb(f"gate_tmp{n}", [P, NB, E]) for n in range(4)]
        gate_col = [sb(f"gate_col{n}", [P, NB]) for n in range(6)]
        first_hot = sb("first_hot", [P, NB, E])
        second_hot = sb("second_hot", [P, NB, E])
        gates = sb("gates", [P, NB, E])
        gatesT = sb("gatesT", [P, P])
        b2_spread = sb("b2_spread", [P, NB, P])
        w1_rows = [sb(f"w1_rows{p}", [P, FB, P]) for p in range(2)]
        w2_rows = [sb(f"w2_rows{p}", [P, FF]) for p in range(2)]
        w1 = [sb(f"w1_{p}", [P, FF]) for p in range(2)]
        w2 = [sb(f"w2_{p}", [P, FB, P]) for p in range(2)]
        hidden = [sb(f"hidden{p}", [P, FB, CH * P]) for p in range(2)]
        m_out = [sb(f"m_out{p}", [P, P]) for p in range(2)]
        TOKENS = (-2, 2, 14, 15)
        STEPS = E * NC

        EXPERT_SEMS = sems("experts", """stat rstd normed turned_ps turned turned2 logit_ps logits chain pool_chain
            gate_exp gate_in turned_gates_ps turned_gates spread bias_ps bias rows_in0 rows_in1 rows_ps rows h_ps
            hidden y_ps added stat_chain fin_stat fin_rstd done""")

        def mixture(n, layer):
            def before(k):
                return {"chain": 17, "gate_exp": 1, "gate_in": 1, "turned_gates_ps": 1, "turned_gates": 1, "spread": 1,
                        "bias_ps": NC, "bias": NC, "rows_in0": 16 * E, "rows_in1": 16 * E, "rows_ps": 4 + 2 * E,
                        "rows": 2 + 2 * E, "h_ps": FB * STEPS, "hidden": FB + FB * STEPS, "y_ps": 6 + STEPS,
                        "added": 2 + STEPS, "fin_stat": 0, "fin_rstd": 0, "done": 0}.get(k, NB)

            s = run_twice(EXPERT_SEMS, before, layer == 1)
            s.n, s.layer = n, layer
            s.src = x if layer else y
            s.acc = y if layer else x
            return s

        def pe_mixture(pe, s):
            after_previous(pe, s.n)

            def iteration(i, par):
                p0, p1 = par, 1 - par
                if there(i):
                    b = i
                    pe.wait_ge(s["turned"], b + 1 + s.past["turned"])
                    if later(b, 2):
                        pe.wait_ge(s["logits"], b - 1 + s.past["logits"])
                    nc.tensor.matmul(bank[:, 2 + p0, 0:E], m_normT[p0][:, :], gate_w[:, s.layer, :],
                                     start=True, stop=True).then_inc(s["logit_ps"], 1)
                if there(i + 1):
                    b = i + 1
                    pe.wait_ge(s["normed"], b + 1 + s.past["normed"])
                    if later(b, 2):
                        pe.wait_ge(s["turned2"], b - 1 + s.past["turned2"])
                    nc.tensor.transpose(bank[:, p1, 0:P], m_normed[p1][:, :], ident[:, :]).then_inc(s["turned_ps"], 1)

            skewed(pe, iteration, *TOKENS)

            def turn(e, p, pair):
                pe.wait_ge((s["rows_in0"], s["rows_in1"])[p], 32 * (pair + 1) + s.past["rows_in0"])
                pe.wait_ge(s["rows"], 2 * e + 2 + s.past["rows"])
                for f in range(FB):
                    mm = nc.tensor.transpose(quarters(6)[:, f, :], w1_rows[p][:, f, :], ident[:, :])
                mm.then_inc(s["rows_ps"], 1)
                for f in range(FB):
                    mm = nc.tensor.transpose(quarters(7)[:, f, :], w2_rows[p][:, f * P:(f + 1) * P], ident[:, :])
                mm.then_inc(s["rows_ps"], 1)

            if s.layer == 0:
                turn(0, 0, 0)
            pe.wait_ge(s["gate_in"], 1 + s.past["gate_in"])
            nc.tensor.transpose(bank[:, 4, 0:P], gates[:, :, :].rearrange("p b e -> p (b e)"), ident[:, :]).then_inc(s["turned_gates_ps"], 1)
            pe.wait_ge(s["turned_gates"], 1 + s.past["turned_gates"])
            pe.wait_ge(s["spread"], 1 + s.past["spread"])
            for c in range(NC):
                if c >= 2:
                    pe.wait_ge(s["bias"], c - 1 + s.past["bias"])
                nc.tensor.matmul(bank[:, 4 + c % 2, :], gatesT[:, :], b2_spread[:, CH * c:CH * c + CH, :],
                                 start=True, stop=True).then_inc(s["bias_ps"], 1)
            pe.wait_ge(s["logits"], NB + s.past["logits"])
            pe.wait_ge(s["turned2"], NB + s.past["turned2"])
            pe.wait_ge(s["bias"], NC + s.past["bias"])

            def up(e, p, c):
                step = NC * e + c
                for f in range(FB):
                    pe.wait_ge(s["hidden"], FB * step + f + 1 + s.past["hidden"])
                    nc.tensor.matmul(bank[:, f, :], w1[p][:, f * P:(f + 1) * P],
                                     tokensT[:, c * CH * P:(c + 1) * CH * P], start=True, stop=True).then_inc(s["h_ps"], 1)

            def down(e, p, c):
                step = NC * e + c
                pe.wait_ge(s["hidden"], FB * step + 2 * FB + s.past["hidden"])
                pe.wait_ge(s["added"], step + 1 + s.past["added"])
                for t in range(CH):
                    for f in range(FB):
                        mm = nc.tensor.matmul(quarters(4 + c % 2)[:, t, :], hidden[c % 2][:, f, t * P:(t + 1) * P],
                                              w2[p][:, f, :], start=(f == 0), stop=(f == FB - 1))
                mm.then_inc(s["y_ps"], 1)

            def expert(e, p, pair, turn_next):
                if s.layer == 0:
                    pe.wait_ge(s["rows"], 2 * e + 4 + s.past["rows"])
                else:
                    pe.wait_ge((s["rows_in0"], s["rows_in1"])[p], 32 * (pair + 1) + s.past["rows_in0"])
                up(e, p, 0)
                for c in range(NC):
                    if c + 1 < NC:
                        up(e, p, c + 1)
                    if c == 2 and turn_next:
                        turn(e + 1, 1 - p, pair + p)
                    down(e, p, c)

            if s.layer == 0:
                with pe.Fori(0, E // 2 - 1) as pair:
                    expert(2 * pair, 0, pair, True)
                    expert(2 * pair + 1, 1, pair, True)
                expert(E - 2, 0, E // 2 - 1, True)
                expert(E - 1, 1, E // 2 - 1, False)
            else:
                with pe.Fori(0, E // 2) as pair:
                    expert(2 * pair, 0, pair, False)
                    expert(2 * pair + 1, 1, pair, False)

        def sp_mixture(sp, s):
            after_previous(sp, s.n)

            def load(e, p):
                arrived = (s["rows_in0"], s["rows_in1"])[p]
                if s.layer == 0:
                    sp.wait_ge(s["rows_ps"], 2 * e + 2 + s.past["rows_ps"])
                    sp.dma_start(w1_rows[p][:, :, :], a["L0_ffn_fc1_w"][e, :, :].rearrange("(c q) d -> q c d", q=P)).then_inc(arrived, 16)
                    sp.dma_start(w2_rows[p][:, :], a["L0_ffn_fc2_w"][e, :, :]).then_inc(arrived, 16)
                else:
                    sp.wait_ge(s["y_ps"], 4 * e + 2 + s.past["y_ps"])
                    sp.dma_start(w1[p][:, :], a["L1_ffn_W1"][e, :, :]).then_inc(arrived, 16)
                    sp.dma_start(w2[p][:, :, :], a["L1_ffn_W2"][e, :, :].rearrange("(c q) d -> q c d", q=P)).then_inc(arrived, 16)

            sp.sem_inc(s["rows_ps"], 4)
            sp.sem_inc(s["y_ps"], 6)
            with sp.Fori(0, E // 2) as pair:
                load(2 * pair, 0)
                load(2 * pair + 1, 1)

        def act_mixture(act, s):
            after_previous(act, s.n)
            act.sem_inc(s["hidden"], FB)

            def iteration(i, par):
                p1 = 1 - par
                if there(i + 1):
                    b = i + 1
                    act.wait_ge(s["turned_ps"], b + 1 + s.past["turned_ps"])
                    if later(b, 2):
                        act.wait_ge(s["logit_ps"], b - 1 + s.past["logit_ps"])
                    affine = {} if s.layer else dict(scale=cols[:, C_LN2W:C_LN2W + 1], bias=cols[:, C_LN2B:C_LN2B + 1])
                    f = ACT.Copy if s.layer else ACT.Identity
                    nc.scalar.activation(m_normT[p1][:, :], bank[:, p1, 0:P], f, **affine).then_inc(s["turned"], 1)
                    nc.scalar.activation(tokensT[:, bass.ts(b, P)], bank[:, p1, 0:P], f, **affine).then_inc(s["turned2"], 1)

            skewed(act, iteration, *TOKENS)
            if s.layer == 0:
                act.wait_ge(s["chain"], 12 + s.past["chain"])
                nc.scalar.activation(gate_col[3][:, :], gate_col[2][:, :], ACT.Exp).then_inc(s["gate_exp"], 1)
            else:
                act.wait_ge(s["chain"], 2 + s.past["chain"])
                nc.scalar.activation(gate_tmp[1][:, :, :], gate_tmp[0][:, :, :], ACT.Exp).then_inc(s["gate_exp"], 1)
            act.wait_ge(s["turned_gates_ps"], 1 + s.past["turned_gates_ps"])
            nc.scalar.activation(gatesT[:, :], bank[:, 4, 0:P], ACT.Copy).then_inc(s["turned_gates"], 1)

            with act.Fori(0, E // 2) as pair:
                for p in range(2):
                    for c in range(NC):
                        step = 2 * NC * pair + (NC * p + c)
                        for f in range(FB):
                            act.wait_ge(s["h_ps"], FB * step + f + 1 + s.past["h_ps"])
                            if f == 0:
                                act.wait_ge(s["y_ps"], step + 5 + s.past["y_ps"])
                            col = 32 * s.layer + 2 * FB * pair + (FB * p + f)
                            take(act, L["passed"])
                            nc.scalar.activation(hidden[c % 2][:, f, :], bank[:, f, :], ACT.Gelu,
                                                 bias=cols[:, bass.ds(col, 1)]).then_inc(s["hidden"], 1)

        def pool_mixture(pool, s):
            after_previous(pool, s.n)
            nc.gpsimd.tensor_tensor(b2_spread[:, :, :], b2_rep[:, s.layer, :].unsqueeze(1).to_broadcast([P, NB, P]),
                                    head_of[:, :].unsqueeze(2).to_broadcast([P, NB, P]), ALU.mult).then_inc(s["spread"], 1)
            chain = Chain(1, s.past["pool_chain"])

            def iteration(i, par):
                p0 = par
                if there(i + 2):
                    b = i + 2
                    chain.begin(b)
                    pool.wait_ge(s["stat"], b + 1 + s.past["stat"])
                    take(pool, L["passed"])
                    nc.gpsimd.tensor_scalar(m_var[:, p0, :], m_moments[:, p0, 1:2], EPS, None, ALU.add).then_inc(s["pool_chain"], 1)
                    pool.wait_ge(s["pool_chain"], chain.next())
                    nc.gpsimd.tensor_tensor(m_rstd[:, p0, :], m_var[:, p0, :], minus_half[:, 0:1], ALU.pow).then_inc(s["rstd"], 1)

            skewed(pool, iteration, *TOKENS)
            if s.layer:
                def final(b, p):
                    pool.wait_ge(s["fin_stat"], b + 1 + s.past["fin_stat"])
                    take(pool, L["passed"])
                    nc.gpsimd.tensor_scalar(m_var[:, p, :], m_moments[:, p, 1:2], EPS, None, ALU.add).then_inc(s["pool_chain"], 1)
                    pool.wait_ge(s["pool_chain"], NB + 1 + b + s.past["pool_chain"])
                    nc.gpsimd.tensor_tensor(m_rstd[:, p, :], m_var[:, p, :], minus_half[:, 0:1], ALU.pow).then_inc(s["fin_rstd"], 1)

                with pool.Fori(0, NB // 2) as pair:
                    final(2 * pair, 0)
                    final(2 * pair + 1, 1)

        def dve_mixture(dve, s):
            after_previous(dve, s.n)
            dve.sem_inc(s["added"], 2)
            dve.sem_inc(s["rows"], 2)
            stat_chain = Chain(1, s.past["stat_chain"])

            def iteration(i, par):
                p0 = par
                if there(i + 2):
                    b = i + 2
                    stat_chain.begin(b)
                    nc.vector.bn_stats(m_stats[:, p0, :], s.src[:, b, :]).then_inc(s["stat_chain"], 1)
                    dve.wait_ge(s["stat_chain"], stat_chain.next())
                    take(dve, L["passed"])
                    nc.vector.bn_aggr(m_moments[:, p0, :], m_stats[:, p0, :]).then_inc(s["stat"], 1)
                if there(i):
                    b = i
                    dve.wait_ge(s["logit_ps"], b + 1 + s.past["logit_ps"])
                    if s.layer == 0:
                        nc.vector.tensor_copy(logits[:, b, :], bank[:, 2 + p0, 0:E]).then_inc(s["logits"], 1)
                    else:
                        nc.vector.tensor_tensor(logits[:, b, :], bank[:, 2 + p0, 0:E], gate_b[:, :], ALU.add).then_inc(s["logits"], 1)
                if there(i + 2):
                    b = i + 2
                    if s.layer == 0:
                        nc.vector.tensor_tensor(x[:, b, :], x[:, b, :], y[:, b, :], ALU.add)
                    dve.wait_ge(s["rstd"], b + 1 + s.past["rstd"])
                    if later(b, 2):
                        dve.wait_ge(s["turned_ps"], b - 1 + s.past["turned_ps"])
                    nc.vector.tensor_scalar(m_normed[p0][:, :], s.src[:, b, :], m_moments[:, p0, 0:1], m_rstd[:, p0, :],
                                            ALU.subtract, ALU.mult).then_inc(s["normed"], 1)

            skewed(dve, iteration, *TOKENS)

            dve.wait_ge(s["logits"], NB + s.past["logits"])
            made = []

            def make(instruction):
                made.append(1)
                instruction.then_inc(s["chain"], 1)
                dve.wait_ge(s["chain"], len(made) + s.past["chain"])

            def over(col):
                return col[:, :].unsqueeze(2).to_broadcast([P, NB, E])

            V = nc.vector
            scores = logits
            if s.layer:
                make(V.tensor_reduce(gate_col[0][:, :], logits[:, :, :], AX.X, ALU.max))
                make(V.tensor_tensor(gate_tmp[0][:, :, :], logits[:, :, :], over(gate_col[0]), ALU.subtract))
                dve.wait_ge(s["gate_exp"], 1 + s.past["gate_exp"])
                make(V.tensor_reduce(gate_col[0][:, :], gate_tmp[1][:, :, :], AX.X, ALU.add))
                make(V.reciprocal(gate_col[1][:, :], gate_col[0][:, :]))
                make(V.tensor_tensor(logits[:, :, :], gate_tmp[1][:, :, :], over(gate_col[1]), ALU.mult))

            def pick(values, best, hot):
                make(V.tensor_reduce(best[:, :], values[:, :, :], AX.X, ALU.max))
                make(V.tensor_tensor(gate_tmp[2][:, :, :], values[:, :, :], over(best), ALU.is_equal))
                make(V.tensor_tensor(gate_tmp[3][:, :, :], gate_tmp[2][:, :, :],
                                     countdown[:, :].unsqueeze(1).to_broadcast([P, NB, E]), ALU.mult))
                make(V.tensor_reduce(gate_col[4][:, :], gate_tmp[3][:, :, :], AX.X, ALU.max))
                make(V.tensor_tensor(hot[:, :, :], gate_tmp[3][:, :, :], over(gate_col[4]), ALU.is_equal))

            pick(scores, gate_col[0], first_hot)
            make(V.scalar_tensor_tensor(out=gate_tmp[0][:, :, :], in0=first_hot[:, :, :], scalar=NEG, in1=scores[:, :, :],
                                        op0=ALU.mult, op1=ALU.add))
            pick(gate_tmp[0], gate_col[1], second_hot)
            if s.layer == 0:
                make(V.tensor_tensor(gate_col[2][:, :], gate_col[1][:, :], gate_col[0][:, :], ALU.subtract))
                dve.wait_ge(s["gate_exp"], 1 + s.past["gate_exp"])
                make(V.tensor_scalar(gate_col[4][:, :], gate_col[3][:, :], 1.0, None, ALU.add))
                make(V.reciprocal(gate_col[0][:, :], gate_col[4][:, :]))
                make(V.tensor_tensor(gate_col[1][:, :], gate_col[3][:, :], gate_col[0][:, :], ALU.mult))
            else:
                make(V.tensor_tensor(gate_col[2][:, :], gate_col[1][:, :], gate_col[0][:, :], ALU.add))
                make(V.tensor_scalar(gate_col[3][:, :], gate_col[2][:, :], 1e-8, None, ALU.add))
                make(V.reciprocal(gate_col[5][:, :], gate_col[3][:, :]))
                make(V.tensor_tensor(gate_col[0][:, :], gate_col[0][:, :], gate_col[5][:, :], ALU.mult))
                make(V.tensor_tensor(gate_col[1][:, :], gate_col[1][:, :], gate_col[5][:, :], ALU.mult))
            make(V.tensor_tensor(gate_tmp[0][:, :, :], first_hot[:, :, :], over(gate_col[0]), ALU.mult))
            make(V.tensor_tensor(gate_tmp[1][:, :, :], second_hot[:, :, :], over(gate_col[1]), ALU.mult))
            V.tensor_tensor(gates[:, :, :], gate_tmp[0][:, :, :], gate_tmp[1][:, :, :], ALU.add).then_inc(s["gate_in"], 1)

            def take_rows(e, p):
                dve.wait_ge(s["y_ps"], 4 * e + 2 + s.past["y_ps"])
                dve.wait_ge(s["rows_ps"], 2 * e + 5 + s.past["rows_ps"])
                V.tensor_copy(w1[p][:, :].rearrange("p (n c) -> p n c", c=P), quarters(6)).then_inc(s["rows"], 1)
                dve.wait_ge(s["rows_ps"], 2 * e + 6 + s.past["rows_ps"])
                V.tensor_copy(w2[p][:, :, :], quarters(7)).then_inc(s["rows"], 1)

            if s.layer == 0:
                take_rows(0, 0)
            for c in range(NC):
                dve.wait_ge(s["bias_ps"], c + 1 + s.past["bias_ps"])
                acc = s.acc[:, CH * c:CH * c + CH, :]
                if s.layer == 0:
                    V.tensor_tensor(acc, quarters(4 + c % 2), acc, ALU.add).then_inc(s["bias"], 1)
                else:
                    V.tensor_copy(acc, quarters(4 + c % 2)).then_inc(s["bias"], 1)
            dve.wait_ge(s["bias"], NC + s.past["bias"])

            def add(e, c):
                step = NC * e + c
                dve.wait_ge(s["y_ps"], step + 7 + s.past["y_ps"])
                dve.wait_ge(s["added"], step + 2 + s.past["added"])
                for t in range(CH):
                    b = CH * c + t
                    ins = V.scalar_tensor_tensor(out=s.acc[:, b, :], in0=quarters(4 + c % 2)[:, t, :],
                                                 scalar=gates[:, b, bass.ds(e, 1)], in1=s.acc[:, b, :],
                                                 op0=ALU.mult, op1=ALU.add)
                ins.then_inc(s["added"], 1)

            def expert(e, p, take_next):
                for c in range(NC):
                    if c == 2 and take_next:
                        take_rows(e + 1, 1 - p)
                    add(e, c)

            if s.layer == 0:
                with dve.Fori(0, E // 2 - 1) as pair:
                    expert(2 * pair, 0, True)
                    expert(2 * pair + 1, 1, True)
                expert(E - 2, 0, True)
                expert(E - 1, 1, False)
            else:
                with dve.Fori(0, E // 2) as pair:
                    expert(2 * pair, 0, False)
                    expert(2 * pair + 1, 1, False)

                def final(b, p):
                    V.bn_stats(m_stats[:, p, :], y[:, b, :]).then_inc(s["stat_chain"], 1)
                    dve.wait_ge(s["stat_chain"], NB + 1 + 4 * b + s.past["stat_chain"])
                    take(dve, L["passed"])
                    V.bn_aggr(m_moments[:, p, :], m_stats[:, p, :]).then_inc(s["fin_stat"], 1)
                    dve.wait_ge(s["fin_rstd"], b + 1 + s.past["fin_rstd"])
                    V.tensor_scalar(m_out[p][:, :], y[:, b, :], m_moments[:, p, 0:1], m_rstd[:, p, :],
                                    ALU.subtract, ALU.mult).then_inc(s["stat_chain"], 1)
                    dve.wait_ge(s["stat_chain"], NB + 2 + 4 * b + s.past["stat_chain"])
                    V.tensor_tensor(m_out[p][:, :], m_out[p][:, :], gamma[:, :], ALU.mult).then_inc(s["stat_chain"], 1)
                    dve.wait_ge(s["stat_chain"], NB + 3 + 4 * b + s.past["stat_chain"])
                    V.tensor_tensor(m_out[p][:, :], m_out[p][:, :], beta[:, :], ALU.add).then_inc(s["stat_chain"], 1)
                    dve.wait_ge(s["stat_chain"], NB + 4 + 4 * b + s.past["stat_chain"])
                    V.tensor_tensor(x[:, b, :], x[:, b, :], m_out[p][:, :], ALU.add).then_inc(s["done"], 1)

                dve.wait_ge(s["added"], STEPS + 2 + s.past["added"])
                with dve.Fori(0, NB // 2) as pair:
                    final(2 * pair, 0)
                    final(2 * pair + 1, 1)

        M0, M1 = mixture(3, 0), mixture(6, 1)
        all_done.append((M0["added"], 2 + STEPS))
        all_done.append((LA["done"], NB))
        all_done.append((W["done"], NB))
        all_done.append((M1["done"], NB))

        block = ctx.enter_context(nc.Block())
        D = sems("end", "stored")

        @block.sync
        def _(sp):
            sp_load(sp)
            sp_narrow(sp, X0)
            sp_narrow(sp, C0)
            sp_mixture(sp, M0)
            sp_wide(sp)
            sp_mixture(sp, M1)

            def store(b):
                sp.wait_ge(M1["done"], b + 1)
                sp.dma_start(out[b, :, :], x[:, b, :]).then_inc(D["stored"], 16)

            with sp.Fori(0, NB) as b:
                store(b)
            sp.wait_ge(D["stored"], 16 * NB)

        @block.scalar
        def _(act):
            act_load(act)
            act_phase(act)
            act_narrow(act, X0)
            act_narrow(act, C0)
            act_mixture(act, M0)
            act_linear(act)
            act_wide(act)
            act_mixture(act, M1)

        @block.gpsimd
        def _(pool):
            pool_load(pool)
            pool_phase(pool)
            pool_narrow(pool, X0)
            pool_narrow(pool, C0)
            pool_mixture(pool, M0)
            pool_linear(pool)
            pool_wide(pool)
            pool_mixture(pool, M1)

        @block.vector
        def _(dve):
            dve_load(dve)
            dve_phase(dve)
            dve_narrow(dve, X0)
            dve_narrow(dve, C0)
            dve_mixture(dve, M0)
            dve_linear(dve)
            dve_wide(dve)
            dve_mixture(dve, M1)

        @block.tensor
        def _(pe):
            pe_load(pe)
            pe_phase(pe)
            pe_narrow(pe, X0)
            pe_narrow(pe, C0)
            pe_mixture(pe, M0)
            pe_linear(pe)
            pe_wide(pe)
            pe_mixture(pe, M1)


_INS = ['x', 'ctx_1024', 'L0_attn_Wq', 'L0_attn_bq', 'L0_attn_Wk', 'L0_attn_bk', 'L0_attn_Wv', 'L0_attn_bv',
        'L0_attn_Wo', 'L0_attn_bo', 'L0_xattn_Wq', 'L0_xattn_Wk', 'L0_xattn_Wv', 'L0_xattn_Wo', 'L0_ffn_ln1_w',
        'L0_ffn_ln1_b', 'L0_ffn_ln2_w', 'L0_ffn_ln2_b', 'L0_ffn_Wqkv', 'L0_ffn_bqkv', 'L0_ffn_Wo', 'L0_ffn_bo',
        'L0_ffn_gate_W', 'L0_ffn_fc1_w', 'L0_ffn_fc1_b', 'L0_ffn_fc2_w', 'L0_ffn_fc2_b', 'L1_attn_w_qkv',
        'L1_attn_w_out', 'L1_xattn_Wq', 'L1_xattn_Wk', 'L1_xattn_Wv', 'L1_xattn_Wo', 'L1_ffn_Wg', 'L1_ffn_bg',
        'L1_ffn_W1', 'L1_ffn_b1', 'L1_ffn_W2', 'L1_ffn_b2', 'L1_ffn_gamma', 'L1_ffn_beta']
_OUTS = [((16, 128, 128), 'float32')]


def kernel(**inputs):
    import numpy as _np
    import concourse.bacc as _bacc
    from concourse import mybir as _mybir
    from concourse.bass_utils import run_bass_kernel_spmd as _run

    nc = _bacc.Bacc("TRN2", target_bir_lowering=False, num_devices=1)
    arrays, args = {}, {}
    for name in _INS:
        a = _np.ascontiguousarray(inputs[name])
        arrays[f"in_{name}"] = a
        args[name] = nc.dram_tensor(f"in_{name}", a.shape, _mybir.dt.from_np(a.dtype), kind="ExternalInput").ap()
    shape, dtype = _OUTS[0]
    out = nc.dram_tensor("out_0", shape, _mybir.dt.from_np(_np.dtype(dtype)), kind="ExternalOutput").ap()
    decoder(nc, args, out)
    r = _run(nc, [arrays], core_ids=[0])
    return r.results[0]["out_0"]
```

```python
from contextlib import ExitStack

import concourse.bass as bass
from concourse import mybir

F32 = mybir.dt.float32
BF16 = mybir.dt.bfloat16
F32R = mybir.dt.float32r
ALU = mybir.AluOpType
ACT = mybir.ActivationFunctionType
AX = mybir.AxisListType

P = 128
NB = 16
CH = 4
NC = NB // CH
CA = 2
NCA = NB // CA
H = 16
HD = P // H
WH = 64
WB = H * WH // P
E = 8
FF = 512
FB = FF // P
HG = 4
G = H // HG
EPS = 1e-5
NEG = -3.0e38
PI = 3.141592653589793
LN_B = 2.772588722239781


def skewed(eng, iteration, first, lo, hi, last, between=()):
    for i in range(first, lo):
        iteration(i, i % 2)
    with eng.Fori(0, (hi - lo) // 2) as pair:
        iteration(2 * pair + lo, lo % 2)
        iteration(2 * pair + (lo + 1), (lo + 1) % 2)
    for i in range(hi, last + 1):
        if last - i < len(between):
            between[i - last - 1]()
        iteration(i, i % 2)


def there(b, n=NB):
    return not isinstance(b, int) or 0 <= b < n


def later(b, n):
    return not isinstance(b, int) or b >= n


def take(eng, passed):
    eng.sem_inc(passed, 1)


class Stage:

    def __init__(self, sems, past):
        self.sems, self.past = dict(sems), past

    def __getitem__(self, name):
        return self.sems[name]


class Chain:

    def __init__(self, per, past=0):
        self.per, self.past, self.at = per, past, 0

    def begin(self, b):
        self.base, self.at = self.per * b + self.past, 0

    def next(self):
        self.at += 1
        return self.base + self.at

    def end(self):
        assert self.at == self.per, (self.at, self.per)


def decoder(nc, a, out):
    with ExitStack() as ctx:
        def sb(name, shape, dt=F32):
            return ctx.enter_context(nc.sbuf_tensor(name, shape, dt))

        early = ctx.enter_context(ExitStack())

        def eb(name, shape, dt=F32):
            return early.enter_context(nc.sbuf_tensor(name, shape, dt))

        def sems(prefix, names):
            return {n: ctx.enter_context(nc.semaphore(f"{prefix}_{n}")) for n in names.split()}

        bank = ctx.enter_context(nc.psum_tensor("bank", [P, 8, 512], F32))

        def quarters(k):
            return bank[:, k, :].rearrange("p (n c) -> p n c", n=4)

        NT = 28
        NCOL = 2 * E * FB + 6
        x = sb("x", [P, NB, P])
        y = sb("y", [P, NB, P])
        tokensT = sb("tokensT", [P, NB * P])

        ident = sb("ident", [P, P])
        ident16 = sb("ident16", [P, P], BF16)
        head_of = sb("head_of", [P, H])
        future = sb("future", [P, HG, P], BF16)
        expert_of = sb("expert_of", [E, P])
        countdown = sb("countdown", [P, E])
        ones_row = sb("ones_row", [1, P])
        minus_half = sb("minus_half", [P, 2 * E])
        plus_half = sb("plus_half", [P, 2 * E])

        turned = sb("turned", [P, NT, P])
        A0_V = 2
        A0_QKV, A0_O, X0_Q, X0_K, X0_V, X0_O, A1_QKV, A1_O, X1_Q, X1_K = 0, 3, 4, 5, 6, 7, 8, 11, 12, 20
        cols = sb("cols", [P, NCOL])
        C_B1, C_LN1W, C_LN1B, C_LN2W, C_LN2B, C_BQ, C_BK = (0, E * FB), 64, 65, 66, 67, 68, 69
        c0_qkv = sb("c0_qkv", [P, 3 * P])
        c0_o = sb("c0_o", [P, P])
        x1_v = sb("x1_v", [P, WB * P])
        x1_v_hi = sb("x1_v_hi", [P, WB * P], F32R)
        x1_v_lo = sb("x1_v_lo", [P, WB * P], F32R)
        x1_o = sb("x1_o", [P, WB, P])
        x1_m = sb("x1_m", [P, H, P])
        gate_w = sb("gate_w", [P, 2, E])
        b2_rows = sb("b2_rows", [E, 2, P])
        b2_rep = sb("b2_rep", [P, 2, P])
        a0_bqkv = sb("a0_bqkv", [P, 3 * P])
        a0_bo = sb("a0_bo", [P, P])
        c0_bv = sb("c0_bv", [P, P])
        c0_bo = sb("c0_bo", [P, P])
        gate_b = sb("gate_b", [P, E])
        gamma = sb("gamma", [P, P])
        beta = sb("beta", [P, P])
        m_normed = [sb(f"m_normed{c}", [P, CH, P]) for c in range(NC)]
        f_stats = sb("f_stats", [P, CH, 6])
        f_moments = sb("f_moments", [P, 2, CH, 2])
        f_var = sb("f_var", [P, 2, CH])
        f_rstd = sb("f_rstd", [P, 2, CH])

        all_done = []

        def after_previous(eng, n):
            if n:
                eng.wait_ge(*all_done[n - 1])

        rows = eb("rows", [P, NT, P])
        col_rows = eb("col_rows", [NCOL, P])
        L = sems("load", "x0 x w0 w vec0 vec const first_ps first rest_ps rest_act rest_dve passed")
        w_loads = [
            (rows[:, A0_QKV, :], a["L0_attn_Wq"]), (rows[:, A0_QKV + 1, :], a["L0_attn_Wk"]),
            (rows[:, A0_QKV + 2, :], a["L0_attn_Wv"]), (rows[:, A0_O, :], a["L0_attn_Wo"]),
            (rows[:, X0_Q, :], a["L0_xattn_Wq"]), (rows[:, X0_K, :], a["L0_xattn_Wk"]),
            (rows[:, X0_V, :], a["L0_xattn_Wv"]), (rows[:, X0_O, :], a["L0_xattn_Wo"]),
            (rows[:, A1_QKV:A1_QKV + 3, :], a["L1_attn_w_qkv"].rearrange("(c p) d -> p c d", p=P)),
            (rows[:, A1_O, :], a["L1_attn_w_out"]),
            (rows[:, X1_Q:X1_Q + WB, :], a["L1_xattn_Wq"].rearrange("p (c d) -> p c d", d=P)),
            (rows[:, X1_K:X1_K + WB, :], a["L1_xattn_Wk"].rearrange("p (c d) -> p c d", d=P)),
            (col_rows[0:32, :], a["L0_ffn_fc1_b"].rearrange("e (c p) -> (e c) p", p=P)),
            (col_rows[32:64, :], a["L1_ffn_b1"].rearrange("e (c p) -> (e c) p", p=P)),
            (col_rows[64:65, :], a["L0_ffn_ln1_w"].unsqueeze(0)), (col_rows[65:66, :], a["L0_ffn_ln1_b"].unsqueeze(0)),
            (col_rows[66:67, :], a["L0_ffn_ln2_w"].unsqueeze(0)), (col_rows[67:68, :], a["L0_ffn_ln2_b"].unsqueeze(0)),
            (col_rows[68:70, :], a["L0_ffn_bqkv"][0:2 * P].rearrange("(c p) -> c p", p=P)),
            (b2_rows[:, 0, :], a["L0_ffn_fc2_b"]), (b2_rows[:, 1, :], a["L1_ffn_b2"]),
        ]
        vec_loads = [
            (a0_bqkv[:, 0:P], a["L0_attn_bq"].partition_broadcast(P)),
            (a0_bqkv[:, P:2 * P], a["L0_attn_bk"].partition_broadcast(P)),
            (a0_bqkv[:, 2 * P:3 * P], a["L0_attn_bv"].partition_broadcast(P)),
            (a0_bo[:, :], a["L0_attn_bo"].partition_broadcast(P)),
            (c0_bv[:, :], a["L0_ffn_bqkv"][2 * P:3 * P].partition_broadcast(P)),
            (c0_bo[:, :], a["L0_ffn_bo"].partition_broadcast(P)),
            (gate_b[:, :], a["L1_ffn_bg"].partition_broadcast(P)),
            (gamma[:, :], a["L1_ffn_gamma"].partition_broadcast(P)),
            (beta[:, :], a["L1_ffn_beta"].partition_broadcast(P)),
            (c0_qkv[:, :], a["L0_ffn_Wqkv"]), (c0_o[:, :], a["L0_ffn_Wo"]),
            (x1_v[:, :], a["L1_xattn_Wv"]), (x1_o[:, :, :], a["L1_xattn_Wo"].rearrange("(c p) d -> p c d", p=P)),
            (gate_w[:, 0, :], a["L0_ffn_gate_W"]), (gate_w[:, 1, :], a["L1_ffn_Wg"]),
        ]

        def sp_load(sp):
            rows_of = a["x"].rearrange("b t d -> t b d")
            sp.dma_start(x[:, 0:CH, :], rows_of[:, 0:CH, :]).then_inc(L["x0"], 16)
            for dst, src in vec_loads[:N_FIRST]:
                sp.dma_start(dst, src).then_inc(L["vec0"], 16)
            sp.dma_start(x[:, CH:NB, :], rows_of[:, CH:NB, :]).then_inc(L["x"], 16)
            for dst, src in w_loads[N_FIRST:]:
                sp.dma_start(dst, src).then_inc(L["w"], 16)
            for dst, src in vec_loads[N_FIRST:]:
                sp.dma_start(dst, src).then_inc(L["vec"], 16)

        def act_load(act):
            for dst, src in w_loads[:N_FIRST]:
                act.dma_start(dst, src).then_inc(L["w0"], 16)

        def pool_load(pool):
            made = []

            def make(instruction):
                made.append(1)
                instruction.then_inc(L["const"], 1)
                pool.wait_ge(L["const"], len(made))

            make(nc.gpsimd.memset(minus_half[:, :], -0.5))
            make(nc.gpsimd.memset(plus_half[:, :], 0.5))
            make(nc.gpsimd.memset(ident[:, :], 0.0))
            make(nc.gpsimd.affine_select(out=ident[:, :], in_=ident[:, :], compare_op=ALU.not_equal, fill=1.0,
                                         base=0, pattern=[[-1, P]], channel_multiplier=1))
            assert len(made) == FIRST_CONSTS

        def pool_load_rest(pool):
            made = [1] * FIRST_CONSTS

            def make(instruction):
                made.append(1)
                instruction.then_inc(L["const"], 1)
                pool.wait_ge(L["const"], len(made))

            make(nc.gpsimd.tensor_copy(ident16[:, :], ident[:, :]))
            make(nc.gpsimd.memset(head_of[:, :], 1.0))
            make(nc.gpsimd.affine_select(out=head_of[:, :], in_=head_of[:, :], compare_op=ALU.is_ge, fill=0.0,
                                         base=0, pattern=[[-HD, H]], channel_multiplier=1))
            make(nc.gpsimd.affine_select(out=head_of[:, :], in_=head_of[:, :], compare_op=ALU.is_ge, fill=0.0,
                                         base=HD - 1, pattern=[[HD, H]], channel_multiplier=-1))
            make(nc.gpsimd.memset(future[:, :, :], 0.0))
            make(nc.gpsimd.affine_select(out=future[:, :, :], in_=future[:, :, :], compare_op=ALU.is_ge, fill=NEG,
                                         base=0, pattern=[[0, HG], [-1, P]], channel_multiplier=1))
            make(nc.gpsimd.memset(expert_of[:, :], 0.0))
            eo = expert_of[:, :].rearrange("p (b e) -> p b e", e=E)
            make(nc.gpsimd.affine_select(out=eo, in_=eo, compare_op=ALU.not_equal, fill=1.0,
                                         base=0, pattern=[[0, P // E], [-1, E]], channel_multiplier=1))
            make(nc.gpsimd.iota(countdown[:, :], pattern=[[-1, E]], base=E, channel_multiplier=0,
                                allow_small_or_imprecise_dtypes=True))
            make(nc.gpsimd.memset(ones_row[:, :], 1.0))
            assert len(made) == CONSTS

        N_FIRST = 4
        FIRST_CONSTS = 4
        CONSTS = 14

        def pe_load(pe):
            pe.wait_ge(L["const"], FIRST_CONSTS)
            pe.wait_ge(L["w0"], 16 * N_FIRST)
            pe.wait_ge(L["vec0"], 16 * N_FIRST)
            for j in range(4):
                src = a0_bqkv[:, 2 * P:3 * P] if j == A0_V else rows[:, A0_QKV + j, :]
                mm = nc.tensor.transpose(quarters(0)[:, j, :], src, ident[:, :])
            mm.then_inc(L["first_ps"], 1)
            pe.wait_ge(L["first"], 1)
            nc.tensor.matmul(bank[:, 1, 0:P], rows[:, A0_V, :], turned[:, A0_O, :], start=True, stop=True)
            nc.tensor.matmul(bank[:, 1, P:2 * P], turned[:, A0_V, :], turned[:, A0_O, :], start=True,
                             stop=True).then_inc(L["first_ps"], 1)
            pe.wait_ge(L["first"], 3)

        def dve_load(dve):
            dve.wait_ge(L["first_ps"], 1)
            nc.vector.tensor_copy(turned[:, A0_QKV:A0_QKV + 4, :], quarters(0)).then_inc(L["first"], 1)
            dve.wait_ge(L["first_ps"], 2)
            nc.vector.tensor_copy(turned[:, A0_V, :], bank[:, 1, 0:P]).then_inc(L["first"], 1)
            dve.wait_ge(L["vec0"], 16 * N_FIRST)
            nc.vector.tensor_tensor(a0_bo[:, :], bank[:, 1, P:2 * P], a0_bo[:, :], ALU.add).then_inc(L["first"], 1)

        def pe_load_rest(pe):
            pe.wait_ge(L["w"], 16 * (len(w_loads) - N_FIRST))
            pe.wait_ge(L["const"], CONSTS)
            pe.wait_ge(A["shift"], NCA)
            for n in range(1, NT // 4):
                for j in range(4):
                    mm = nc.tensor.transpose(quarters(n)[:, j, :], rows[:, 4 * n + j, :], ident[:, :])
                mm.then_inc(L["rest_ps"], 1)
            nc.tensor.transpose(bank[:, 7, 0:NCOL], col_rows[:, :], ident[0:NCOL, 0:NCOL]).then_inc(L["rest_ps"], 1)
            pe.wait_ge(L["rest_act"], 3)
            pe.wait_ge(L["rest_dve"], 3)
            for odd in range(2):
                for n in range(WB):
                    r = slice(WH * odd, WH * odd + WH)
                    mm = nc.tensor.matmul(quarters(4 + 2 * odd + n // 4)[:, n % 4, :], turned[r, X1_Q + n, :],
                                          turned[r, X1_K + n, :], start=True, stop=True)
                    if n == 3 and odd == 1:
                        pe.wait_ge(L["rest_dve"], 4)
            mm.then_inc(L["rest_ps"], 1)
            for l in range(2):
                mm = nc.tensor.matmul(bank[:, 3, l * P:(l + 1) * P], expert_of[:, :], b2_rows[:, l, :],
                                      start=True, stop=True)
            mm.then_inc(L["rest_ps"], 1)

        def act_load_rest(act):
            for n in range(1, NT // 4, 2):
                act.wait_ge(L["rest_ps"], n)
                nc.scalar.activation(turned[:, 4 * n:4 * n + 4, :], quarters(n), ACT.Copy).then_inc(L["rest_act"], 1)

        def dve_load_rest(dve):
            for n in range(2, NT // 4, 2):
                dve.wait_ge(L["rest_ps"], n)
                nc.vector.tensor_copy(turned[:, 4 * n:4 * n + 4, :], quarters(n)).then_inc(L["rest_dve"], 1)
            dve.wait_ge(L["rest_ps"], 7)
            nc.vector.tensor_copy(cols[:, :], bank[:, 7, 0:NCOL]).then_inc(L["rest_dve"], 1)
            dve.wait_ge(L["rest_ps"], 8)
            for n in range(4):
                odd, half = n // 2, n % 2
                nc.vector.tensor_copy(x1_m[:, odd + 8 * half:odd + 8 * half + 7:2, :], quarters(4 + n)).then_inc(L["rest_dve"], 1)
            dve.wait_ge(L["rest_ps"], 9)
            nc.vector.tensor_copy(b2_rep[:, :, :], bank[:, 3, 0:2 * P].rearrange("p (l c) -> p l c", l=2)).then_inc(L["rest_dve"], 1)
            dve.wait_ge(L["vec"], 16 * (len(vec_loads) - N_FIRST))

        A = sems("phase", """var rstd normed turned_ps turned qk_ps v_ps qk values square sums root scaled sides_ps
                             sides score_ps sine shift probs probsT_ps probsT den out_ps biased done stat_chain
                             norm_chain score_chain sum_chain""")
        FIRST_HALF = (-2, 2, 6, NCA - 1)
        SECOND_HALF = (-1, 3, 7, NCA - 1)
        a_stats = eb("a_stats", [P, 2, CA, 6])
        a_moments = eb("a_moments", [P, 2, CA, 2])
        a_var = eb("a_var", [P, 2, CA])
        a_rstd = eb("a_rstd", [P, 2, CA])
        a_normed = [eb(f"a_normed{p}", [P, CA, P]) for p in range(2)]
        a_T = [eb(f"a_T{p}", [P, CA, P]) for p in range(2)]
        a_qk = [eb(f"a_qk{p}", [P, CA, 2, P]) for p in range(2)]
        a_values = eb("a_values", [P, NB, P])
        a_squares = [eb(f"a_squares{p}", [P, 2, CA, P]) for p in range(2)]
        a_sums = eb("a_sums", [P, 2, 2, CA])
        a_norms = eb("a_norms", [P, 2, 2, CA])
        a_norms1 = eb("a_norms1", [P, 2, 2, CA])
        a_inv = eb("a_inv", [P, 2, 2, CA])
        a_unit = [eb(f"a_unit{p}", [P, CA, P]) for p in range(2)]
        a_sides = [eb(f"a_sides{p}", [P, 3, CA, P]) for p in range(2)]
        a_sine = [eb(f"a_sine{p}", [P, CA, P]) for p in range(2)]
        a_phase = [eb(f"a_phase{p}", [P, CA, P]) for p in range(2)]
        a_scores = [eb(f"a_scores{p}", [P, CA, P]) for p in range(2)]
        a_peak = eb("a_peak", [P, 2, CA])
        a_shift = eb("a_shift", [P, NB, P])
        a_probs = [eb(f"a_probs{p}", [P, CA, P]) for p in range(2)]
        a_den = eb("a_den", [P, 2, CA])
        a_rden = eb("a_rden", [P, 2, CA])
        a_probsT = [eb(f"a_probsT{p}", [P, CA, P]) for p in range(2)]
        early.close()

        heads_end = ctx.enter_context(ExitStack())

        def hb(name, shape, dt=F32):
            return heads_end.enter_context(nc.sbuf_tensor(name, shape, dt))

        stats = hb("stats", [P, 2, 6])
        moments = hb("moments", [P, 2, 2])
        var_eps = hb("var_eps", [P, 2, 1])
        rstd = hb("rstd", [P, 2, 1])
        stats2 = hb("stats2", [P, 2, 6])
        moments2 = hb("moments2", [P, 2, 2])
        rstd2 = hb("rstd2", [P, 2, 1])
        normed = [hb(f"normed{p}", [P, P]) for p in range(2)]
        ctx_rows = [hb(f"ctx_rows{p}", [P, P]) for p in range(2)]
        bothT = [hb(f"bothT{p}", [P, 2, P]) for p in range(2)]
        qT = [hb(f"qT{p}", [P, P]) for p in range(2)]
        kT = [hb(f"kT{p}", [P, P]) for p in range(2)]
        wide = [hb(f"wide{p}", [P, H, P]) for p in range(2)]
        probs = [hb(f"probs{p}", [P, H, P]) for p in range(2)]
        probsT = hb("probsT", [P, H, P])
        peak = [hb(f"peak{p}", [P, H]) for p in range(2)]
        values = [hb(f"values{p}", [P, H, 32]) for p in range(2)]
        headsT = [hb(f"headsT{p}", [P, 4, P]) for p in range(2)]
        den = [hb(f"den{p}", [P, H]) for p in range(2)]
        den1 = [hb(f"den1{p}", [P, H]) for p in range(2)]
        merged = [hb(f"merged{p}", [P, P]) for p in range(2)]
        mergedT = [hb(f"mergedT{p}", [P, P]) for p in range(2)]
        ctxT_hi = [hb(f"ctxT_hi{p}", [P, P], F32R) for p in range(2)]
        ctxT_lo = [hb(f"ctxT_lo{p}", [P, P], F32R) for p in range(2)]
        v_wide = [hb(f"v_wide{p}", [P, WB * P]) for p in range(2)]
        wideT = hb("wideT", [P, WB, P])
        lin_raw = [hb(f"lin_raw{p}", [P, 2, P]) for p in range(2)]
        lin_neg = [hb(f"lin_neg{p}", [P, 2, P]) for p in range(2)]
        lin_exp = [hb(f"lin_exp{p}", [P, 2, P]) for p in range(2)]
        lin_qk = [hb(f"lin_qk{p}", [P, 2, P]) for p in range(2)]
        lin_v = [hb(f"lin_v{p}", [P, 2, P]) for p in range(2)]
        lin_kv = [hb(f"lin_kv{p}", [P, 2 * P]) for p in range(2)]
        block_of = hb("block_of", [P, P])

        all_done.append((A["done"], NCA))

        def pe_phase(pe):
            def first_half(i, par):
                p0, p1 = par, 1 - par
                if there(i + 1, NCA):
                    c = i + 1
                    pe.wait_ge(A["turned"], c + 1)
                    if later(c, 1):
                        pe.wait_ge(A["qk"], c)
                        pe.wait_ge(A["values"], c)
                    for j in range(CA):
                        mm = nc.tensor.matmul(bank[:, 1, 2 * P * j:2 * P * (j + 1)], a_T[p1][:, j, :],
                                              turned[:, A0_QKV:A0_QKV + 2, :], start=True, stop=True)
                    mm.then_inc(A["qk_ps"], 1)
                    for j in range(CA):
                        mm = nc.tensor.matmul(quarters(2)[:, j, :], a_T[p1][:, j, :], turned[:, A0_V, :],
                                              start=True, stop=True)
                    mm.then_inc(A["v_ps"], 1)
                if there(i, NCA):
                    c = i
                    pe.wait_ge(A["qk"], c + 1)
                    if later(c, 1):
                        pe.wait_ge(A["sides"], 2 * c)
                    for side in range(2):
                        for j in range(CA):
                            mm = nc.tensor.transpose(quarters(3)[:, CA * side + j, :], a_qk[p0][:, j, side, :], ident[:, :])
                    mm.then_inc(A["sides_ps"], 1)
                    pe.wait_ge(A["scaled"], c + 1)
                    for j in range(CA):
                        mm = nc.tensor.transpose(quarters(4)[:, j, :], a_unit[p0][:, j, :], ident[:, :])
                    mm.then_inc(A["sides_ps"], 1)
                    pe.wait_ge(A["sides"], 2 * c + 2)
                    if later(c, 1):
                        pe.wait_ge(A["shift"], c)
                    for side in range(2):
                        for j in range(CA):
                            mm = nc.tensor.matmul(quarters(5 + side)[:, j, :], a_sides[p0][:, 0, j, :],
                                                  a_sides[p0][:, 2 - side, j, :], start=True, stop=True)
                        mm.then_inc(A["score_ps"], 1)

                if there(i + 2, NCA):
                    c = i + 2
                    pe.wait_ge(A["normed"], c + 1)
                    if later(c, 1):
                        pe.wait_ge(A["turned"], c)
                    for j in range(CA):
                        mm = nc.tensor.transpose(quarters(0)[:, j, :], a_normed[p0][:, j, :], ident[:, :])
                    mm.then_inc(A["turned_ps"], 1)

            def second_half(i, par):
                p0, p1 = par, 1 - par
                if there(i + 1, NCA):
                    c = i + 1
                    pe.wait_ge(A["probs"], c + 1)
                    if later(c, 2):
                        pe.wait_ge(A["probsT"], c - 1)
                    for j in range(CA):
                        mm = nc.tensor.transpose(quarters(p1)[:, j, :], a_probs[p1][:, j, :], ident[:, :])
                    mm.then_inc(A["probsT_ps"], 1)
                if there(i, NCA):
                    c = i
                    pe.wait_ge(A["probsT"], c + 1)
                    if later(c, 2):
                        pe.wait_ge(A["done"], c - 1)
                    for j in range(CA):
                        mm = nc.tensor.matmul(quarters(2 + p0)[:, j, :], a_probsT[p0][:, j, :],
                                              a_values[:, CA * c + j, :], start=True, stop=True)
                    mm.then_inc(A["out_ps"], 1)

            skewed(pe, first_half, *FIRST_HALF)
            pe_load_rest(pe)
            pe.wait_ge(L["rest_dve"], 9)
            skewed(pe, second_half, *SECOND_HALF)

        def act_phase(act):
            def first_half(i, par):
                p0, p1 = par, 1 - par
                if there(i, NCA):
                    c = i
                    act.wait_ge(A["sides_ps"], 2 * c + 1)
                    nc.scalar.activation(a_sides[p0][:, 0:2, :, :].rearrange("p s j d -> p (s j) d"), quarters(3),
                                         ACT.Copy).then_inc(A["sides"], 1)
                    act.wait_ge(A["sides_ps"], 2 * c + 2)
                    nc.scalar.activation(a_sides[p0][:, 2, :, :], quarters(4)[:, 0:CA, :], ACT.Copy).then_inc(A["sides"], 1)
                if there(i + 1, NCA):
                    c = i + 1
                    act.wait_ge(A["v_ps"], c + 1)
                    take(act, L["passed"])
                    nc.scalar.activation(a_values[:, bass.ts(c, CA), :], quarters(2)[:, 0:CA, :], ACT.Copy).then_inc(A["values"], 1)
                    act.wait_ge(A["qk"], c + 1)
                    nc.scalar.activation(a_squares[p1][:, :, :, :], a_qk[p1][:, :, :, :].rearrange("p j s d -> p s j d"),
                                         ACT.Square).then_inc(A["square"], 1)
                if there(i, NCA):
                    c = i
                    act.wait_ge(A["score_ps"], 2 * c + 1)
                    for j in range(CA):
                        ins = nc.scalar.activation(a_sine[p0][:, j, :], quarters(5)[:, j, :], ACT.Sin,
                                                   scale=a_inv[:, p0, 0, j:j + 1])
                    ins.then_inc(A["sine"], 1)

                if there(i + 2, NCA):
                    c = i + 2
                    act.wait_ge(A["turned_ps"], c + 1)
                    nc.scalar.activation(a_T[p0][:, :, :], quarters(0)[:, 0:CA, :], ACT.Copy).then_inc(A["turned"], 1)

            def second_half(i, par):
                p0, p1 = par, 1 - par
                if there(i + 1, NCA):
                    c = i + 1
                    act.wait_ge(A["shift"], c + 1)
                    if later(c, 2):
                        act.wait_ge(A["probsT_ps"], c - 1)
                        act.wait_ge(A["den"], c - 1)
                    take(act, L["passed"])
                    nc.scalar.activation(a_probs[p1][:, :, :], a_shift[:, bass.ts(c, CA), :], ACT.Exp,
                                         scale=P ** -0.5).then_inc(A["probs"], 1)
                if there(i, NCA):
                    c = i
                    act.wait_ge(A["probsT_ps"], c + 1)
                    if later(c, 2):
                        act.wait_ge(A["out_ps"], c - 1)
                    nc.scalar.activation(a_probsT[p0][:, :, :], quarters(p0)[:, 0:CA, :], ACT.Copy).then_inc(A["probsT"], 1)

            skewed(act, first_half, *FIRST_HALF)
            act_load_rest(act)
            skewed(act, second_half, *SECOND_HALF)

        def pool_phase(pool):
            def first_half(i, par):
                p0, p1 = par, 1 - par
                if there(i + 2, NCA):
                    c = i + 2
                    pool.wait_ge(A["var"], c + 1)
                    nc.gpsimd.tensor_tensor(a_rstd[:, p0, :], a_var[:, p0, :], minus_half[:, 0:CA], ALU.pow).then_inc(A["rstd"], 1)
                if there(i + 1, NCA):
                    c = i + 1
                    pool.wait_ge(A["sums"], c + 1)
                    nc.gpsimd.tensor_tensor(a_norms[:, p1, :, :].rearrange("p s j -> p (s j)"),
                                            a_sums[:, p1, :, :].rearrange("p s j -> p (s j)"),
                                            plus_half[:, 0:2 * CA], ALU.pow).then_inc(A["root"], 1)

            first_half(FIRST_HALF[0], FIRST_HALF[0] % 2)
            pool_load_rest(pool)
            skewed(pool, first_half, FIRST_HALF[0] + 1, *FIRST_HALF[1:])
            pool.wait_ge(L["first"], 3)
            pool.wait_ge(A["normed"], NCA)
            for c in range(NC):
                xc = x[:, CH * c:CH * (c + 1), :]
                nc.gpsimd.tensor_tensor(xc, xc, a0_bo[:, :].unsqueeze(1).to_broadcast([P, CH, P]), ALU.add).then_inc(A["biased"], 1)

            pool.wait_ge(L["vec"], 16 * (len(vec_loads) - N_FIRST))
            nc.gpsimd.tensor_copy(x1_v_hi[:, :], x1_v[:, :]).then_inc(L["const"], 1)
            pool.wait_ge(L["const"], CONSTS + 1)
            nc.gpsimd.tensor_tensor(x1_v_lo[:, :], x1_v[:, :], x1_v_hi[:, :], ALU.subtract).then_inc(L["const"], 1)

        def dve_phase(dve):
            stat_chain, norm_chain, score_chain, sum_chain = Chain(2), Chain(3), Chain(3), Chain(1)
            dve.wait_ge(L["x0"], 16)

            def first_half(i, par):
                p0, p1 = par, 1 - par
                if there(i + 2, NCA):
                    c = i + 2
                    stat_chain.begin(c)
                    if isinstance(c, int) and c == CH // CA:
                        dve.wait_ge(L["x"], 16)
                    for j in range(CA):
                        ins = nc.vector.bn_stats(a_stats[:, p0, j, :], x[:, CA * c + j, :])
                    ins.then_inc(A["stat_chain"], 1)
                    dve.wait_ge(A["stat_chain"], stat_chain.next())
                    take(dve, L["passed"])
                    for j in range(CA):
                        ins = nc.vector.bn_aggr(a_moments[:, p0, j, :], a_stats[:, p0, j, :])
                    ins.then_inc(A["stat_chain"], 1)
                    dve.wait_ge(A["stat_chain"], stat_chain.next())
                    nc.vector.tensor_scalar(a_var[:, p0, :], a_moments[:, p0, :, 1], EPS, None, ALU.add).then_inc(A["var"], 1)
                if there(i + 1, NCA):
                    c = i + 1
                    if isinstance(i, int) and i == -1:
                        dve.wait_ge(L["vec0"], 16 * N_FIRST)
                    dve.wait_ge(A["qk_ps"], c + 1)
                    nc.vector.tensor_tensor(a_qk[p1][:, :, :, :].rearrange("p j s d -> p j (s d)"),
                                            bank[:, 1, :].rearrange("p (j c) -> p j c", j=CA),
                                            a0_bqkv[:, 0:2 * P].unsqueeze(1).to_broadcast([P, CA, 2 * P]),
                                            ALU.add).then_inc(A["qk"], 1)
                if there(i + 2, NCA):
                    c = i + 2
                    dve.wait_ge(A["rstd"], c + 1)
                    if later(c, 2):
                        dve.wait_ge(A["turned_ps"], c - 1)
                    for j in range(CA):
                        ins = nc.vector.tensor_scalar(a_normed[p0][:, j, :], x[:, CA * c + j, :], a_moments[:, p0, j, 0:1],
                                                      a_rstd[:, p0, j:j + 1], ALU.subtract, ALU.mult)
                    ins.then_inc(A["normed"], 1)
                if there(i + 1, NCA):
                    c = i + 1
                    dve.wait_ge(A["square"], c + 1)
                    nc.vector.tensor_reduce(a_sums[:, p1, :, :], a_squares[p1][:, :, :, :], AX.X, ALU.add).then_inc(A["sums"], 1)
                if there(i, NCA):
                    c = i
                    score_chain.begin(c)
                    dve.wait_ge(A["sine"], c + 1)
                    nc.vector.scalar_tensor_tensor(out=a_phase[p0][:, :, :], in0=a_sine[p0][:, :, :], scalar=-2.0,
                                                   in1=a_sine[p0][:, :, :], op0=ALU.mult, op1=ALU.mult).then_inc(A["score_chain"], 1)
                    dve.wait_ge(A["score_chain"], score_chain.next())
                    dve.wait_ge(A["score_ps"], 2 * c + 2)
                    nc.vector.scalar_tensor_tensor(out=a_scores[p0][:, :, :], in0=a_phase[p0][:, :, :], scalar=1.0,
                                                   in1=quarters(6)[:, 0:CA, :], op0=ALU.add, op1=ALU.mult).then_inc(A["score_chain"], 1)
                    dve.wait_ge(A["score_chain"], score_chain.next())
                    nc.vector.tensor_reduce(a_peak[:, p0, :], a_scores[p0][:, :, :], AX.X, ALU.max).then_inc(A["score_chain"], 1)
                    dve.wait_ge(A["score_chain"], score_chain.next())
                    nc.vector.tensor_tensor(a_shift[:, bass.ts(c, CA), :], a_scores[p0][:, :, :],
                                            a_peak[:, p0, :].unsqueeze(2).to_broadcast([P, CA, P]),
                                            ALU.subtract).then_inc(A["shift"], 1)

                if there(i + 1, NCA):
                    c = i + 1
                    norm_chain.begin(c)
                    dve.wait_ge(A["root"], c + 1)
                    nc.vector.tensor_scalar(a_norms1[:, p1, 0, :], a_norms[:, p1, 0, :], 1e-8, 2 / PI, ALU.add,
                                            ALU.mult).then_inc(A["norm_chain"], 1)
                    nc.vector.tensor_scalar(a_norms1[:, p1, 1, :], a_norms[:, p1, 1, :], 1e-8, None,
                                            ALU.add).then_inc(A["norm_chain"], 1)
                    norm_chain.next()
                    dve.wait_ge(A["norm_chain"], norm_chain.next())
                    nc.vector.reciprocal(a_inv[:, p1, :, :], a_norms1[:, p1, :, :]).then_inc(A["norm_chain"], 1)
                    dve.wait_ge(A["norm_chain"], norm_chain.next())
                    for j in range(CA):
                        ins = nc.vector.tensor_scalar(a_unit[p1][:, j, :], a_qk[p1][:, j, 1, :], a_inv[:, p1, 1, j:j + 1],
                                                      None, ALU.mult)
                    ins.then_inc(A["scaled"], 1)

            def second_half(i, par):
                p0, p1 = par, 1 - par
                if there(i + 1, NCA):
                    c = i + 1
                    sum_chain.begin(c)
                    dve.wait_ge(A["probs"], c + 1)
                    nc.vector.tensor_reduce(a_den[:, p1, :], a_probs[p1][:, :, :], AX.X, ALU.add).then_inc(A["sum_chain"], 1)
                    dve.wait_ge(A["sum_chain"], sum_chain.next())
                    nc.vector.reciprocal(a_rden[:, p1, :], a_den[:, p1, :]).then_inc(A["den"], 1)
                if there(i, NCA):
                    c = i
                    dve.wait_ge(A["den"], c + 1)
                    dve.wait_ge(A["out_ps"], c + 1)
                    for j in range(CA):
                        ins = nc.vector.scalar_tensor_tensor(out=x[:, CA * c + j, :], in0=quarters(2 + p0)[:, j, :],
                                                             scalar=a_rden[:, p0, j:j + 1], in1=x[:, CA * c + j, :],
                                                             op0=ALU.mult, op1=ALU.add)
                    ins.then_inc(A["done"], 1)

            first_half(FIRST_HALF[0], FIRST_HALF[0] % 2)
            dve_load(dve)
            skewed(dve, first_half, FIRST_HALF[0] + 1, *FIRST_HALF[1:])
            dve_load_rest(dve)
            dve.wait_ge(A["biased"], NC)
            skewed(dve, second_half, *SECOND_HALF)

        NARROW_SEMS = sems("narrow", """ctx stat rstd zed stat2 rstd2 normed both_ps both qk_ps q k masked score_ps
            shifted probs clean turn_ps probsT av_ps headsT back_ps merged mT_ps mT out_ps done v_ps values cleared
            chain norm_chain stat_chain pool_chain""")

        def run_twice(sem_set, before, second):
            return Stage(sem_set, {k: before(k) if second else 0 for k in sem_set})

        def narrow(n, cross):
            def before(k):
                if k in ("masked", "score_ps", "shifted", "probs", "clean", "turn_ps", "probsT", "chain"):
                    return G * NB
                if k in ("zed", "stat2", "rstd2"):
                    return 0
                return {"ctx": 16 * NB, "norm_chain": 2 * NB, "cleared": 4}.get(k, NB)

            s = run_twice(NARROW_SEMS, before, not cross)
            s.n, s.cross = n, cross
            s.scale = LN_B * HD ** -0.5 if cross else HD ** -0.5
            s.wq, s.wk, s.wv, s.wo = ([turned[:, X0_Q, :], turned[:, X0_K, :], turned[:, X0_V, :], turned[:, X0_O, :]] if cross
                                      else [c0_qkv[:, 0:P], c0_qkv[:, P:2 * P], c0_qkv[:, 2 * P:3 * P], c0_o[:, :]])
            s.kv = 1 if cross else 0
            s.sems["ready"] = s["clean"] if cross else s["probs"]
            s.past["ready"] = s.past["clean"] if cross else s.past["probs"]
            all_done.append((s["done"], NB + s.past["done"]))
            return s

        X0, C0 = narrow(1, True), narrow(2, False)
        NARROW = (-3, 3, 13, 16)

        def sp_narrow(sp, s):
            after_previous(sp, s.n)
            if s.cross:
                def load(b, p):
                    if later(b, 2):
                        sp.wait_ge(s["both_ps"], b - 1 + s.past["both_ps"])
                        take(sp, L["passed"])
                    if later(b, 1):
                        sp.wait_ge(s["ctx"], 16 * b + s.past["ctx"])
                    sp.dma_start(ctx_rows[p][:, :], a["ctx_1024"][b, :, :]).then_inc(s["ctx"], 16)

                load(0, 0)
                load(1, 1)
                with sp.Fori(1, NB // 2) as pair:
                    load(2 * pair, 0)
                    load(2 * pair + 1, 1)

        def pe_narrow(pe, s):
            after_previous(pe, s.n)

            def iteration(i, par):
                p0, p1 = par, 1 - par
                if there(i + 1):
                    b = i + 1
                    pe.wait_ge(s["q"], b + 1 + s.past["q"])
                    for g in range(G):
                        pe.wait_ge(s["masked"], G * b + g + 1 + s.past["masked"])
                        if later(b, 1):
                            pe.wait_ge(s["shifted"], G * (b - 1) + g + 1 + s.past["shifted"])
                        mm = nc.tensor.matmul(bank[:, g, :], qT[p1][:, :], wide[p1][:, HG * g:HG * g + HG, :],
                                              start=True, stop=s.cross)
                        if not s.cross:
                            mm = nc.tensor.matmul(bank[:, g, :], ident16[:, :], future[:, :, :], start=False, stop=True)
                        mm.then_inc(s["score_ps"], 1)
                if there(i - 1):
                    b = i - 1
                    pe.wait_ge(s["merged"], b + 1 + s.past["merged"])
                    if later(b, 1):
                        pe.wait_ge(s["done"], b + s.past["done"])
                    nc.tensor.transpose(bank[:, 7, 0:P], merged[p1][:, :], ident[:, :]).then_inc(s["mT_ps"], 1)
                if there(i):
                    b = i
                    for g in range(G):
                        pe.wait_ge(s["ready"], G * b + g + 1 + s.past["ready"])
                        if g >= 2:
                            pe.wait_ge(s["probsT"], G * b + g - 1 + s.past["probsT"])
                        elif g == 0 and later(b, 1):
                            pe.wait_ge(s["merged"], b + s.past["merged"])
                        elif g == 1 and (not isinstance(b, int) or b + 2 < NB):
                            pe.wait_ge(s["both"], b + 3 + s.past["both"])
                        elif g == 1:
                            pe.wait_ge(s["both"], NB + s.past["both"])
                            pe.wait_ge(s["values"], min(b + 2, NB) + s.past["values"])
                        for j in range(HG):
                            mm = nc.tensor.transpose(quarters(4 + g % 2)[:, j, :], probs[p0][:, HG * g + j, :], ident[:, :])
                        mm.then_inc(s["turn_ps"], 1)
                if there(i + 2):
                    b = i + 2
                    pe.wait_ge(s["both"], b + 1 + s.past["both"])
                    if later(b, 3):
                        pe.wait_ge(s["headsT"], b - 2 + s.past["headsT"])
                    elif b >= 1:
                        pe.wait_ge(s["k"], b + s.past["k"])
                        pe.wait_ge(s["q"], b + s.past["q"])
                    nc.tensor.matmul(bank[:, 6, 0:P], s.wq, bothT[p0][:, 0, :], start=True, stop=True)
                    nc.tensor.matmul(bank[:, 6, P:2 * P], s.wk, bothT[p0][:, s.kv, :],
                                     start=True, stop=True).then_inc(s["qk_ps"], 1)
                if there(i - 1):
                    b = i - 1
                    pe.wait_ge(s["mT"], b + 1 + s.past["mT"])
                    mm = nc.tensor.matmul(bank[:, 7, 0:P], mergedT[p1][:, :], s.wo, start=True, stop=s.cross)
                    if not s.cross:
                        mm = nc.tensor.matmul(bank[:, 7, 0:P], ones_row[:, :], c0_bo[0:1, :], start=False, stop=True)
                    mm.then_inc(s["out_ps"], 1)
                if there(i):
                    b = i
                    pe.wait_ge(s["values"], b + 1 + s.past["values"])
                    if s.cross and isinstance(b, int) and b == 0:
                        pe.wait_ge(s["cleared"], 4 + s.past["cleared"])
                    pe.wait_ge(s["probsT"], G * b + G + s.past["probsT"])
                    if not isinstance(b, int) or b + 2 < NB:
                        pe.wait_ge(s["k"], b + 3 + s.past["k"])
                        pe.wait_ge(s["q"], b + 3 + s.past["q"])
                    for h in range(H):
                        j = 32 * (h % 4)
                        mm = nc.tensor.matmul(quarters(6)[j:j + 32, h // 4, :], values[p0][:, h, :], probsT[:, h, :],
                                              start=True, stop=True)
                    mm.then_inc(s["av_ps"], 1)
                if there(i + 2):
                    b = i + 2
                    pe.wait_ge(s["both"], b + 1 + s.past["both"])
                    if there(i):
                        pe.wait_ge(s["probsT"], G * i + G + s.past["probsT"])
                    mm = nc.tensor.matmul(bank[:, 5, 0:P], bothT[p0][:, s.kv, :], s.wv, start=True, stop=s.cross)
                    if not s.cross:
                        mm = nc.tensor.matmul(bank[:, 5, 0:P], ones_row[:, :], c0_bv[0:1, :], start=False, stop=True)
                    mm.then_inc(s["v_ps"], 1)
                if there(i + 3):
                    b = i + 3
                    pe.wait_ge(s["normed"], b + 1 + s.past["normed"])
                    if s.cross:
                        pe.wait_ge(s["ctx"], 16 * (b + 1) + s.past["ctx"])
                    if s.cross:
                        nc.tensor.transpose(quarters(5)[:, 2, :], ctx_rows[p1][:, :], ident[:, :])
                    nc.tensor.transpose(quarters(5)[:, 1, :], normed[p1][:, :], ident[:, :]).then_inc(s["both_ps"], 1)
                if there(i):
                    b = i
                    pe.wait_ge(s["headsT"], b + 1 + s.past["headsT"])
                    for g in range(G):
                        mm = nc.tensor.transpose(quarters(4)[:, g, :], headsT[p0][:, g, :], ident[:, :])
                    mm.then_inc(s["back_ps"], 1)

            skewed(pe, iteration, *NARROW)

        def act_narrow(act, s):
            after_previous(act, s.n)

            def iteration(i, par):
                p0, p1 = par, 1 - par
                def exps(g):
                    if there(i + 1):
                        act.wait_ge(s["shifted"], G * (i + 1) + g + 1 + s.past["shifted"])
                        pr = probs[p1][:, HG * g:HG * g + HG, :]
                        nc.scalar.activation(pr, pr, ACT.Exp, scale=s.scale).then_inc(s["probs"], 1)

                def turned_probs(g):
                    if there(i):
                        act.wait_ge(s["turn_ps"], G * i + g + 1 + s.past["turn_ps"])
                        if g == 0 and later(i, 1):
                            act.wait_ge(s["av_ps"], i + s.past["av_ps"])
                        nc.scalar.activation(probsT[:, HG * g:HG * g + HG, :], quarters(4 + g % 2),
                                             ACT.Copy).then_inc(s["probsT"], 1)

                exps(0)
                if there(i - 1):
                    b = i - 1
                    act.wait_ge(s["mT_ps"], b + 1 + s.past["mT_ps"])
                    if later(b, 2):
                        act.wait_ge(s["out_ps"], b - 1 + s.past["out_ps"])
                    nc.scalar.activation(mergedT[p1][:, :], bank[:, 7, 0:P], ACT.Copy).then_inc(s["mT"], 1)

                turned_probs(0)
                turned_probs(1)
                turned_probs(2)
                turned_probs(3)
                if there(i + 2):
                    b = i + 2
                    act.wait_ge(s["qk_ps"], b + 1 + s.past["qk_ps"])
                    if later(b, 2):
                        act.wait_ge(s["score_ps"], G * (b - 1) + s.past["score_ps"])
                    if s.cross:
                        nc.scalar.activation(kT[p0][:, :], bank[:, 6, P:2 * P], ACT.Copy).then_inc(s["k"], 1)
                        nc.scalar.activation(qT[p0][:, :], bank[:, 6, 0:P], ACT.Copy).then_inc(s["q"], 1)
                    else:
                        nc.scalar.activation(kT[p0][:, :], bank[:, 6, P:2 * P], ACT.Identity,
                                             bias=cols[:, C_BK:C_BK + 1]).then_inc(s["k"], 1)
                        nc.scalar.activation(qT[p0][:, :], bank[:, 6, 0:P], ACT.Identity,
                                             bias=cols[:, C_BQ:C_BQ + 1]).then_inc(s["q"], 1)
                exps(1)
                exps(2)
                if there(i):
                    act.wait_ge(s["av_ps"], i + 1 + s.past["av_ps"])
                    if later(i, 2):
                        act.wait_ge(s["back_ps"], i - 1 + s.past["back_ps"])
                    nc.scalar.activation(headsT[p0][:, :, :], quarters(6), ACT.Copy).then_inc(s["headsT"], 1)
                if there(i + 2):
                    b = i + 2
                    act.wait_ge(s["v_ps"], b + 1 + s.past["v_ps"])
                    if there(i + 3):
                        act.wait_ge(s["both_ps"], i + 4 + s.past["both_ps"])
                    v8 = values[p0][:, :, 0:HD]
                    src = bank[:, 5, 0:P].rearrange("p (h d) -> p h d", d=HD)
                    nc.scalar.activation(v8, src, ACT.Copy).then_inc(s["values"], 1)
                if there(i + 3):
                    b = i + 3
                    act.wait_ge(s["both_ps"], b + 1 + s.past["both_ps"])
                    if later(b, 2):
                        act.wait_ge(s["v_ps"], b - 1 + s.past["v_ps"])
                    if s.cross:
                        nc.scalar.activation(bothT[p1][:, :, :], quarters(5)[:, 1:3, :], ACT.Copy).then_inc(s["both"], 1)
                    else:
                        nc.scalar.activation(bothT[p1][:, 0, :], quarters(5)[:, 1, :], ACT.Identity,
                                             scale=cols[:, C_LN1W:C_LN1W + 1],
                                             bias=cols[:, C_LN1B:C_LN1B + 1]).then_inc(s["both"], 1)
                exps(3)

            skewed(act, iteration, *NARROW)

        def pool_narrow(pool, s):
            after_previous(pool, s.n)
            chain = Chain(1 if s.cross else 2, s.past["pool_chain"])
            if s.cross:
                for p in range(2):
                    nc.gpsimd.memset(values[p][:, :, HD:32], 0.0).then_inc(s["cleared"], 1)
                pool.wait_ge(s["cleared"], 2 + s.past["cleared"])
                for p in range(2):
                    nc.gpsimd.memset(values[p][:, :, HD:HD + 1], 1.0).then_inc(s["cleared"], 1)

            def iteration(i, par):
                p0, p1 = par, 1 - par
                if there(i + 3):
                    b = i + 3
                    chain.begin(b)
                    pool.wait_ge(s["stat"], b + 1 + s.past["stat"])
                    take(pool, L["passed"])
                    nc.gpsimd.tensor_scalar(var_eps[:, p1, :], moments[:, p1, 1:2], EPS, None, ALU.add).then_inc(s["pool_chain"], 1)
                    pool.wait_ge(s["pool_chain"], chain.next())
                    nc.gpsimd.tensor_tensor(rstd[:, p1, :], var_eps[:, p1, :], minus_half[:, 0:1], ALU.pow).then_inc(s["rstd"], 1)
                    if not s.cross:
                        pool.wait_ge(s["stat2"], b + 1 + s.past["stat2"])
                        take(pool, L["passed"])
                        nc.gpsimd.tensor_scalar(var_eps[:, p1, :], moments2[:, p1, 1:2], EPS, None, ALU.add).then_inc(s["pool_chain"], 1)
                        pool.wait_ge(s["pool_chain"], chain.next())
                        nc.gpsimd.tensor_tensor(rstd2[:, p1, :], var_eps[:, p1, :], minus_half[:, 0:1],
                                                ALU.pow).then_inc(s["rstd2"], 1)
                    chain.end()
                if there(i + 2):
                    b = i + 2
                    pool.wait_ge(s["k"], b + 1 + s.past["k"])
                    for g in range(G):
                        if later(b, 2):
                            pool.wait_ge(s["score_ps"], G * (b - 2) + g + 1 + s.past["score_ps"])
                        nc.gpsimd.tensor_tensor(
                            wide[p0][:, HG * g:HG * g + HG, :], kT[p0][:, :].unsqueeze(1).to_broadcast([P, HG, P]),
                            head_of[:, HG * g:HG * g + HG].unsqueeze(2).to_broadcast([P, HG, P]),
                            ALU.mult).then_inc(s["masked"], 1)
                if s.cross and there(i + 1):
                    b = i + 1
                    for g in range(G):
                        pool.wait_ge(s["probs"], G * b + g + 1 + s.past["probs"])
                        pr = probs[p1][:, HG * g:HG * g + HG, :]
                        take(pool, L["passed"])
                        nc.gpsimd.affine_select(out=pr, in_=pr, compare_op=ALU.is_ge, fill=0.0, base=0,
                                                pattern=[[0, HG], [-1, P]], channel_multiplier=1).then_inc(s["clean"], 1)

            skewed(pool, iteration, *NARROW)

        def dve_narrow(dve, s):
            after_previous(dve, s.n)
            stat_chain = Chain(1 if s.cross else 2, s.past["stat_chain"])
            norm_chain = Chain(2 if s.cross else 1, s.past["norm_chain"])
            soft_chain = Chain(G, s.past["chain"])

            def iteration(i, par):
                p0, p1 = par, 1 - par
                def soften(g):
                    b = i + 1
                    if there(b):
                        if g == 0:
                            soft_chain.begin(b)
                        hs = slice(HG * g, HG * g + HG)
                        dve.wait_ge(s["score_ps"], G * b + g + 1 + s.past["score_ps"])
                        nc.vector.tensor_reduce(peak[p1][:, hs], quarters(g), AX.X, ALU.max).then_inc(s["chain"], 1)
                        dve.wait_ge(s["chain"], soft_chain.next())
                        if later(b, 2):
                            dve.wait_ge(s["turn_ps"], G * (b - 2) + g + 1 + s.past["turn_ps"])
                        nc.vector.tensor_tensor(probs[p1][:, hs, :], quarters(g),
                                                peak[p1][:, hs].unsqueeze(2).to_broadcast([P, HG, P]),
                                                ALU.subtract).then_inc(s["shifted"], 1)

                def normalise(mom, r, src, dst):
                    return nc.vector.tensor_scalar(dst, src, mom[:, p1, 0:1], r[:, p1, :], ALU.subtract, ALU.mult)

                if there(i + 3):
                    b = i + 3
                    stat_chain.begin(b)
                    nc.vector.bn_stats(stats[:, p1, :], x[:, b, :]).then_inc(s["stat_chain"], 1)
                    dve.wait_ge(s["stat_chain"], stat_chain.next())
                    take(dve, L["passed"])
                    nc.vector.bn_aggr(moments[:, p1, :], stats[:, p1, :]).then_inc(s["stat"], 1)
                soften(0)
                if there(i - 1):
                    b = i - 1
                    norm_chain.begin(b)
                    dve.wait_ge(s["back_ps"], b + 1 + s.past["back_ps"])
                    heads = bank[:, 4, :].rearrange("p (h w) -> p h w", w=32)
                    src = heads[:, :, HD]
                    if s.cross:
                        nc.vector.tensor_scalar(den1[p1][:, :], src, 1.0, None, ALU.add).then_inc(s["norm_chain"], 1)
                        dve.wait_ge(s["norm_chain"], norm_chain.next())
                        src = den1[p1][:, :]
                    nc.vector.reciprocal(den[p1][:, :], src).then_inc(s["norm_chain"], 1)
                    dve.wait_ge(s["norm_chain"], norm_chain.next())
                    norm_chain.end()
                    if later(b, 2):
                        dve.wait_ge(s["mT_ps"], b - 1 + s.past["mT_ps"])
                    nc.vector.tensor_tensor(merged[p1][:, :].rearrange("p (h d) -> p h d", d=HD), heads[:, :, 0:HD],
                                            den[p1][:, :].unsqueeze(2).to_broadcast([P, H, HD]),
                                            ALU.mult).then_inc(s["merged"], 1)

                if not s.cross and there(i + 3):
                    b = i + 3
                    dve.wait_ge(s["rstd"], b + 1 + s.past["rstd"])
                    normalise(moments, rstd, x[:, b, :], y[:, b, :]).then_inc(s["zed"], 1)
                    dve.wait_ge(s["zed"], b + 1 + s.past["zed"])
                    take(dve, L["passed"])
                    nc.vector.bn_stats(stats2[:, p1, :], y[:, b, :]).then_inc(s["stat_chain"], 1)
                    dve.wait_ge(s["stat_chain"], stat_chain.next())
                    take(dve, L["passed"])
                    nc.vector.bn_aggr(moments2[:, p1, :], stats2[:, p1, :]).then_inc(s["stat2"], 1)
                soften(1)
                soften(2)
                if there(i - 1):
                    b = i - 1
                    dve.wait_ge(s["out_ps"], b + 1 + s.past["out_ps"])
                    if s.cross:
                        nc.vector.tensor_tensor(x[:, b, :], bank[:, 7, 0:P], x[:, b, :], ALU.add).then_inc(s["done"], 1)
                    else:
                        nc.vector.tensor_tensor(y[:, b, :], bank[:, 7, 0:P], y[:, b, :], ALU.add).then_inc(s["done"], 1)

                if there(i + 3):
                    b = i + 3
                    if later(b, 2):
                        dve.wait_ge(s["both_ps"], b - 1 + s.past["both_ps"])
                    if s.cross:
                        dve.wait_ge(s["rstd"], b + 1 + s.past["rstd"])
                        normalise(moments, rstd, x[:, b, :], normed[p1][:, :]).then_inc(s["normed"], 1)
                    else:
                        dve.wait_ge(s["rstd2"], b + 1 + s.past["rstd2"])
                        normalise(moments2, rstd2, y[:, b, :], normed[p1][:, :]).then_inc(s["normed"], 1)
                soften(3)

            skewed(dve, iteration, *NARROW, between=() if s.cross else ahead(dve, M0, s["done"], s.past["done"]))

        LA = sems("linear", """stat rstd normed turned_ps turned qkv_ps raw v negative exps mapped kv_ps kv qT_ps qT att_ps
                               merged mT_ps mT out_ps done chain pool_chain map_chain""")
        LINEAR = (-3, 4, 12, 17)
        N_LINEAR = 4

        def pe_linear(pe):
            after_previous(pe, N_LINEAR)

            def iteration(i, par):
                p0, p1 = par, 1 - par
                if there(i + 2):
                    b = i + 2
                    pe.wait_ge(LA["turned"], b + 1)
                    if later(b, 1):
                        pe.wait_ge(LA["v"], b)
                    nc.tensor.matmul(bank[:, 1, 0:3 * P], bothT[p0][:, 0, :], turned[:, A1_QKV:A1_QKV + 3, :],
                                     start=True, stop=True).then_inc(LA["qkv_ps"], 1)
                if there(i + 1):
                    b = i + 1
                    pe.wait_ge(LA["mapped"], b + 1)
                    pe.wait_ge(LA["v"], b + 1)
                    if later(b, 1):
                        pe.wait_ge(LA["kv"], b)
                        pe.wait_ge(LA["qT"], b)
                    nc.tensor.matmul(bank[:, 2, 0:2 * P], lin_qk[p1][:, 1, :], lin_v[p1][:, :, :],
                                     start=True, stop=True).then_inc(LA["kv_ps"], 1)
                    nc.tensor.transpose(bank[:, 3, 0:P], lin_qk[p1][:, 0, :], ident[:, :]).then_inc(LA["qT_ps"], 1)
                if there(i):
                    b = i
                    pe.wait_ge(LA["kv"], b + 1)
                    pe.wait_ge(LA["qT"], b + 1)
                    if later(b, 1):
                        pe.wait_ge(LA["merged"], b)
                    nc.tensor.matmul(bank[:, 4, 0:2 * P], qT[p0][:, :], lin_kv[p0][:, :], start=True,
                                     stop=True).then_inc(LA["att_ps"], 1)
                if there(i - 1):
                    b = i - 1
                    pe.wait_ge(LA["merged"], b + 1)
                    if later(b, 1):
                        pe.wait_ge(LA["mT"], b)
                    nc.tensor.transpose(bank[:, 5, 0:P], merged[p1][:, :], ident[:, :]).then_inc(LA["mT_ps"], 1)
                if there(i - 2):
                    b = i - 2
                    pe.wait_ge(LA["mT"], b + 1)
                    if later(b, 1):
                        pe.wait_ge(LA["done"], b)
                    nc.tensor.matmul(bank[:, 6, 0:P], mergedT[p0][:, :], turned[:, A1_O, :], start=True,
                                     stop=True).then_inc(LA["out_ps"], 1)
                if there(i + 3):
                    b = i + 3
                    pe.wait_ge(LA["normed"], b + 1)
                    if later(b, 1):
                        pe.wait_ge(LA["turned"], b)
                    nc.tensor.transpose(bank[:, 0, 0:P], normed[p1][:, :], ident[:, :]).then_inc(LA["turned_ps"], 1)

            skewed(pe, iteration, *LINEAR)

        def act_linear(act):
            after_previous(act, N_LINEAR)

            def iteration(i, par):
                p0, p1 = par, 1 - par
                if there(i + 2):
                    b = i + 2
                    act.wait_ge(LA["qkv_ps"], b + 1)
                    if later(b, 2):
                        act.wait_ge(LA["mapped"], b - 1)
                        act.wait_ge(LA["kv_ps"], b - 1)
                    nc.scalar.activation(lin_raw[p0][:, :, :], bank[:, 1, 0:2 * P].rearrange("p (s d) -> p s d", s=2),
                                         ACT.Copy).then_inc(LA["raw"], 1)
                    nc.scalar.activation(lin_v[p0][:, 0, :], bank[:, 1, 2 * P:3 * P], ACT.Copy).then_inc(LA["v"], 1)
                if there(i + 1):
                    b = i + 1
                    act.wait_ge(LA["qT_ps"], b + 1)
                    if later(b, 2):
                        act.wait_ge(LA["att_ps"], b - 1)
                    nc.scalar.activation(qT[p1][:, :], bank[:, 3, 0:P], ACT.Copy).then_inc(LA["qT"], 1)
                if there(i + 2):
                    b = i + 2
                    act.wait_ge(LA["negative"], b + 1)
                    nc.scalar.activation(lin_exp[p0][:, :, :], lin_neg[p0][:, :, :], ACT.Exp).then_inc(LA["exps"], 1)
                if there(i + 3):
                    b = i + 3
                    act.wait_ge(LA["turned_ps"], b + 1)
                    if later(b, 2):
                        act.wait_ge(LA["qkv_ps"], b - 1)
                    nc.scalar.activation(bothT[p1][:, 0, :], bank[:, 0, 0:P], ACT.Copy).then_inc(LA["turned"], 1)

                if there(i - 1):
                    b = i - 1
                    act.wait_ge(LA["mT_ps"], b + 1)
                    if later(b, 2):
                        act.wait_ge(LA["out_ps"], b - 1)
                    nc.scalar.activation(mergedT[p1][:, :], bank[:, 5, 0:P], ACT.Copy).then_inc(LA["mT"], 1)

            skewed(act, iteration, *LINEAR)

        def pool_linear(pool):
            after_previous(pool, N_LINEAR)
            chain = Chain(1)
            nc.gpsimd.memset(lin_v[0][:, 1, :], 1.0)
            nc.gpsimd.memset(lin_v[1][:, 1, :], 1.0)
            nc.gpsimd.tensor_copy(block_of[:, :].rearrange("p (h d) -> p h d", d=HD),
                                  head_of[:, :].unsqueeze(2).to_broadcast([P, H, HD])).then_inc(LA["map_chain"], 1)

            def iteration(i, par):
                p1 = 1 - par
                if there(i + 3):
                    b = i + 3
                    chain.begin(b)
                    pool.wait_ge(LA["stat"], b + 1)
                    take(pool, L["passed"])
                    nc.gpsimd.tensor_scalar(var_eps[:, p1, :], moments[:, p1, 1:2], EPS, None, ALU.add).then_inc(LA["pool_chain"], 1)
                    pool.wait_ge(LA["pool_chain"], chain.next())
                    nc.gpsimd.tensor_tensor(rstd[:, p1, :], var_eps[:, p1, :], minus_half[:, 0:1], ALU.pow).then_inc(LA["rstd"], 1)

            skewed(pool, iteration, *LINEAR)

        def dve_linear(dve):
            after_previous(dve, N_LINEAR)
            dve.wait_ge(LA["map_chain"], 1)
            chain = Chain(2)

            def iteration(i, par):
                p0, p1 = par, 1 - par
                if there(i + 3):
                    b = i + 3
                    nc.vector.bn_stats(stats[:, p1, :], x[:, b, :]).then_inc(LA["map_chain"], 1)
                    dve.wait_ge(LA["map_chain"], b + 2)
                    take(dve, L["passed"])
                    nc.vector.bn_aggr(moments[:, p1, :], stats[:, p1, :]).then_inc(LA["stat"], 1)
                if there(i + 2):
                    b = i + 2
                    dve.wait_ge(LA["raw"], b + 1)
                    if later(b, 2):
                        dve.wait_ge(LA["exps"], b - 1)
                    nc.vector.tensor_scalar(lin_neg[p0][:, :, :], lin_raw[p0][:, :, :], 0.0, None, ALU.min).then_inc(LA["negative"], 1)
                if there(i + 1):
                    b = i + 1
                    dve.wait_ge(LA["kv_ps"], b + 1)
                    if later(b, 2):
                        dve.wait_ge(LA["att_ps"], b - 1)
                    nc.vector.tensor_tensor(lin_kv[p1][:, :].rearrange("p (s d) -> p s d", s=2),
                                            bank[:, 2, 0:2 * P].rearrange("p (s d) -> p s d", s=2),
                                            block_of[:, :].unsqueeze(1).to_broadcast([P, 2, P]), ALU.mult).then_inc(LA["kv"], 1)
                if there(i + 3):
                    b = i + 3
                    dve.wait_ge(LA["rstd"], b + 1)
                    if later(b, 2):
                        dve.wait_ge(LA["turned_ps"], b - 1)
                    nc.vector.tensor_scalar(normed[p1][:, :], x[:, b, :], moments[:, p1, 0:1], rstd[:, p1, :],
                                            ALU.subtract, ALU.mult).then_inc(LA["normed"], 1)

                if there(i):
                    b = i
                    chain.begin(b)
                    dve.wait_ge(LA["att_ps"], b + 1)
                    nc.vector.tensor_scalar(den1[p0][:, :], bank[:, 4, P:2 * P:HD], 1e-6, None, ALU.add).then_inc(LA["chain"], 1)
                    dve.wait_ge(LA["chain"], chain.next())
                    nc.vector.reciprocal(den[p0][:, :], den1[p0][:, :]).then_inc(LA["chain"], 1)
                    dve.wait_ge(LA["chain"], chain.next())
                    if later(b, 2):
                        dve.wait_ge(LA["mT_ps"], b - 1)
                    nc.vector.tensor_tensor(merged[p0][:, :].rearrange("p (h d) -> p h d", d=HD),
                                            bank[:, 4, 0:P].rearrange("p (h d) -> p h d", d=HD),
                                            den[p0][:, :].unsqueeze(2).to_broadcast([P, H, HD]),
                                            ALU.mult).then_inc(LA["merged"], 1)
                if there(i + 2):
                    b = i + 2
                    dve.wait_ge(LA["exps"], b + 1)
                    if later(b, 2):
                        dve.wait_ge(LA["kv_ps"], b - 1)
                        dve.wait_ge(LA["qT_ps"], b - 1)
                    nc.vector.scalar_tensor_tensor(out=lin_qk[p0][:, :, :], in0=lin_raw[p0][:, :, :], scalar=0.0,
                                                   in1=lin_exp[p0][:, :, :], op0=ALU.max, op1=ALU.add).then_inc(LA["mapped"], 1)
                if there(i - 2):
                    b = i - 2
                    dve.wait_ge(LA["out_ps"], b + 1)
                    nc.vector.tensor_tensor(x[:, b, :], bank[:, 6, 0:P], x[:, b, :], ALU.add).then_inc(LA["done"], 1)

            skewed(dve, iteration, *LINEAR)

        W = sems("wide", """ctx ctx_low stat rstd normed both_ps both through_ps through score_ps shifted probs sums clean
                            turn_ps probsT av_ps wideT v_ps v out_ps done chain sum_chain stat_chain pool_chain""")
        WIDE = (-3, 3, 13, 15)
        N_WIDE = 5

        def sp_wide(sp):
            after_previous(sp, N_WIDE)

            def load(b, p):
                if later(b, 2):
                    sp.wait_ge(W["both_ps"], b - 1)
                    take(sp, L["passed"])
                if later(b, 1):
                    sp.wait_ge(W["ctx"], 16 * b)
                sp.dma_start(ctx_rows[p][:, :], a["ctx_1024"][b, :, :]).then_inc(W["ctx"], 16)

            load(0, 0)
            load(1, 1)
            with sp.Fori(1, NB // 2) as pair:
                load(2 * pair, 0)
                load(2 * pair + 1, 1)

        def pe_wide(pe):
            after_previous(pe, N_WIDE)
            pe.wait_ge(L["const"], CONSTS + 2)

            def iteration(i, par):
                p0, p1 = par, 1 - par
                if there(i + 1):
                    b = i + 1
                    pe.wait_ge(W["both"], b + 1)
                    for g in range(G):
                        pe.wait_ge(W["through"], G * b + g + 1)
                        if later(b, 1):
                            pe.wait_ge(W["shifted"], G * (b - 1) + g + 1)
                        for j in range(HG):
                            mm = nc.tensor.matmul(quarters(g)[:, j, :], wide[p1][:, HG * g + j, :], bothT[p1][:, 1, :],
                                                  start=True, stop=True)
                        mm.then_inc(W["score_ps"], 1)
                if there(i):
                    b = i
                    for g in range(G):
                        pe.wait_ge(W["clean"], G * b + g + 1)
                        if g >= 2:
                            pe.wait_ge(W["probsT"], G * b + g - 1)
                        elif not isinstance(b, int) or b + 1 < NB:
                            pe.wait_ge(W["v"], 2 * (b + 1) + g + 1)
                        for j in range(HG):
                            mm = nc.tensor.transpose(quarters(4 + g % 2)[:, j, :], probs[p0][:, HG * g + j, :], ident[:, :])
                        mm.then_inc(W["turn_ps"], 1)
                if there(i):
                    b = i
                    for half in range(2):
                        pe.wait_ge(W["v"], 2 * b + half + 1)
                        pe.wait_ge(W["probsT"], G * b + 2 * half + 2)
                        if half == 0 and (not isinstance(b, int) or b + 2 < NB):
                            pe.wait_ge(W["both"], b + 3)
                        if half == 1 and later(b, 1):
                            pe.wait_ge(W["done"], b)
                        for h in range(8 * half, 8 * half + 8):
                            r = WH * (h % 2)
                            mm = nc.tensor.matmul(quarters(6 + half)[r:r + WH, (h // 2) % 4, :],
                                                  v_wide[p0][:, WH * h:WH * h + WH], probsT[:, h, :], start=True, stop=True)
                        mm.then_inc(W["av_ps"], 1)
                if there(i + 2):
                    b = i + 2
                    pe.wait_ge(W["both"], b + 1)
                    for g in range(G):
                        if g >= 2:
                            pe.wait_ge(W["through"], G * b + g - 1)
                        elif there(i):
                            pe.wait_ge(W["probsT"], G * i + g + 3)
                        elif b >= 1:
                            pe.wait_ge(W["v"], 2 * (b - 1) + g + 1)
                        for j in range(HG):
                            mm = nc.tensor.matmul(quarters(4 + g % 2)[:, j, :], x1_m[:, HG * g + j, :], bothT[p0][:, 0, :],
                                                  start=True, stop=True)
                        mm.then_inc(W["through_ps"], 1)
                if there(i + 3):
                    b = i + 3
                    pe.wait_ge(W["normed"], b + 1)
                    pe.wait_ge(W["ctx"], 16 * (b + 1))
                    if there(i):
                        pe.wait_ge(W["wideT"], 2 * i + 1)
                    elif b >= 1:
                        pe.wait_ge(W["both"], b)
                    nc.tensor.transpose(quarters(6)[:, 0, :], normed[p1][:, :], ident[:, :])
                    nc.tensor.transpose(quarters(6)[:, 1, :], ctx_rows[p1][:, :], ident[:, :]).then_inc(W["both_ps"], 1)
                if there(i):
                    b = i
                    pe.wait_ge(W["wideT"], 2 * b + 2)
                    for c in range(WB):
                        mm = nc.tensor.matmul(bank[:, 7, 0:P], wideT[:, c, :], x1_o[:, c, :], start=(c == 0),
                                              stop=(c == WB - 1))
                    mm.then_inc(W["out_ps"], 1)

                if there(i + 2):
                    b = i + 2
                    pe.wait_ge(W["ctx_low"], b + 1)
                    for half in range(2):
                        pe.wait_ge(W["through"], G * b + half + 3)
                        cols_v = slice(512 * half, 512 * half + 512)
                        nc.tensor.matmul(bank[:, 4 + half, :], ctxT_hi[p0][:, :], x1_v_hi[:, cols_v], start=True, stop=False)
                        nc.tensor.matmul(bank[:, 4 + half, :], ctxT_hi[p0][:, :], x1_v_lo[:, cols_v], start=False, stop=False)
                        nc.tensor.matmul(bank[:, 4 + half, :], ctxT_lo[p0][:, :], x1_v_hi[:, cols_v], start=False,
                                         stop=True).then_inc(W["v_ps"], 1)

            skewed(pe, iteration, *WIDE)

        def act_wide(act):
            after_previous(act, N_WIDE)

            def iteration(i, par):
                p0, p1 = par, 1 - par

                def exps(g):
                    if there(i + 1):
                        act.wait_ge(W["shifted"], G * (i + 1) + g + 1)
                        pr = probs[p1][:, HG * g:HG * g + HG, :]
                        nc.scalar.activation(pr, pr, ACT.Exp, scale=WH ** -0.5).then_inc(W["probs"], 1)

                def turned_probs(g):
                    if there(i):
                        act.wait_ge(W["turn_ps"], G * i + g + 1)
                        if g == 0 and later(i, 1):
                            act.wait_ge(W["av_ps"], 2 * i)
                        nc.scalar.activation(probsT[:, HG * g:HG * g + HG, :], quarters(4 + g % 2),
                                             ACT.Copy).then_inc(W["probsT"], 1)

                def through(g):
                    if there(i + 2):
                        b = i + 2
                        act.wait_ge(W["through_ps"], G * b + g + 1)
                        if g == 0 and later(b, 2):
                            act.wait_ge(W["score_ps"], G * (b - 1))
                        nc.scalar.activation(wide[p0][:, HG * g:HG * g + HG, :], quarters(4 + g % 2),
                                             ACT.Copy).then_inc(W["through"], 1)

                exps(0)
                turned_probs(0)
                turned_probs(1)
                exps(1)
                turned_probs(2)
                turned_probs(3)
                if there(i):
                    for half in range(2):
                        act.wait_ge(W["av_ps"], 2 * i + half + 1)
                        if half == 0 and later(i, 1):
                            act.wait_ge(W["out_ps"], i)
                        nc.scalar.activation(wideT[:, 4 * half:4 * half + 4, :], quarters(6 + half),
                                             ACT.Copy).then_inc(W["wideT"], 1)
                through(0)
                through(1)
                exps(2)
                through(2)
                through(3)
                exps(3)
                if there(i + 3):
                    b = i + 3
                    act.wait_ge(W["both_ps"], b + 1)
                    if later(b, 2):
                        act.wait_ge(W["score_ps"], G * (b - 1))
                        act.wait_ge(W["v_ps"], 2 * (b - 1))
                    nc.scalar.activation(ctxT_hi[p1][:, :], quarters(6)[:, 1, :], ACT.Copy)
                    nc.scalar.activation(bothT[p1][:, :, :], quarters(6)[:, 0:2, :], ACT.Copy).then_inc(W["both"], 1)

                if there(i + 2):
                    b = i + 2
                    for half in range(2):
                        act.wait_ge(W["v_ps"], 2 * b + half + 1)
                        nc.scalar.activation(v_wide[p0][:, 512 * half:512 * half + 512], bank[:, 4 + half, :],
                                             ACT.Copy).then_inc(W["v"], 1)

            skewed(act, iteration, *WIDE)

        def pool_wide(pool):
            after_previous(pool, N_WIDE)
            chain = Chain(1)

            def iteration(i, par):
                p1 = 1 - par
                if there(i + 3):
                    b = i + 3
                    chain.begin(b)
                    pool.wait_ge(W["stat"], b + 1)
                    take(pool, L["passed"])
                    nc.gpsimd.tensor_scalar(var_eps[:, p1, :], moments[:, p1, 1:2], EPS, None, ALU.add).then_inc(W["pool_chain"], 1)
                    pool.wait_ge(W["pool_chain"], chain.next())
                    nc.gpsimd.tensor_tensor(rstd[:, p1, :], var_eps[:, p1, :], minus_half[:, 0:1], ALU.pow).then_inc(W["rstd"], 1)
                if there(i + 1):
                    b = i + 1
                    for g in range(G):
                        pool.wait_ge(W["sums"], G * b + g + 1)
                        hs = slice(HG * g, HG * g + HG)
                        nc.gpsimd.tensor_tensor(probs[p1][:, hs, :], probs[p1][:, hs, :],
                                                den[p1][:, hs].unsqueeze(2).to_broadcast([P, HG, P]),
                                                ALU.mult).then_inc(W["clean"], 1)

            skewed(pool, iteration, *WIDE)

        def dve_wide(dve):
            after_previous(dve, N_WIDE)
            stat_chain = Chain(1)
            soft_chain = Chain(G)
            sum_chain = Chain(G)

            def iteration(i, par):
                p0, p1 = par, 1 - par
                def soften(g):
                    b = i + 1
                    if there(b):
                        if g == 0:
                            soft_chain.begin(b)
                            sum_chain.begin(b)
                        hs = slice(HG * g, HG * g + HG)
                        dve.wait_ge(W["score_ps"], G * b + g + 1)
                        nc.vector.tensor_reduce(peak[p1][:, hs], quarters(g), AX.X, ALU.max).then_inc(W["chain"], 1)
                        dve.wait_ge(W["chain"], soft_chain.next())
                        if later(b, 2):
                            dve.wait_ge(W["turn_ps"], G * (b - 2) + g + 1)
                        nc.vector.tensor_tensor(probs[p1][:, hs, :], quarters(g),
                                                peak[p1][:, hs].unsqueeze(2).to_broadcast([P, HG, P]),
                                                ALU.subtract).then_inc(W["shifted"], 1)

                def total(g):
                    b = i + 1
                    if there(b):
                        hs = slice(HG * g, HG * g + HG)
                        dve.wait_ge(W["probs"], G * b + g + 1)
                        nc.vector.tensor_reduce(den1[p1][:, hs], probs[p1][:, hs, :], AX.X, ALU.add).then_inc(W["sum_chain"], 1)
                        dve.wait_ge(W["sum_chain"], sum_chain.next())
                        nc.vector.reciprocal(den[p1][:, hs], den1[p1][:, hs]).then_inc(W["sums"], 1)

                if there(i + 3):
                    b = i + 3
                    stat_chain.begin(b)
                    nc.vector.bn_stats(stats[:, p1, :], x[:, b, :]).then_inc(W["stat_chain"], 1)
                    dve.wait_ge(W["stat_chain"], stat_chain.next())
                    take(dve, L["passed"])
                    nc.vector.bn_aggr(moments[:, p1, :], stats[:, p1, :]).then_inc(W["stat"], 1)

                soften(0)
                soften(1)
                soften(2)
                if there(i + 2):
                    b = i + 2
                    dve.wait_ge(W["both"], b + 1)
                    nc.vector.tensor_tensor(ctxT_lo[p0][:, :], bothT[p0][:, 1, :], ctxT_hi[p0][:, :], ALU.subtract).then_inc(W["ctx_low"], 1)
                soften(3)
                total(0)
                total(1)
                if there(i + 3):
                    b = i + 3
                    dve.wait_ge(W["rstd"], b + 1)
                    if later(b, 2):
                        dve.wait_ge(W["both_ps"], b - 1)
                    nc.vector.tensor_scalar(normed[p1][:, :], x[:, b, :], moments[:, p1, 0:1], rstd[:, p1, :],
                                            ALU.subtract, ALU.mult).then_inc(W["normed"], 1)
                total(2)
                total(3)
                if there(i):
                    b = i
                    dve.wait_ge(W["out_ps"], b + 1)
                    nc.vector.tensor_tensor(x[:, b, :], bank[:, 7, 0:P], x[:, b, :], ALU.add).then_inc(W["done"], 1)

            skewed(dve, iteration, *WIDE, between=ahead(dve, M1, W["done"], 0))

        heads_end.close()
        logits = sb("logits", [P, NB, E])
        gate_tmp = [sb(f"gate_tmp{n}", [P, NB, E]) for n in range(4)]
        gate_col = [sb(f"gate_col{n}", [P, NB]) for n in range(6)]
        first_hot = sb("first_hot", [P, NB, E])
        second_hot = sb("second_hot", [P, NB, E])
        gates = sb("gates", [P, NB, E])
        gatesT = sb("gatesT", [P, P])
        b2_spread = sb("b2_spread", [P, NB, P])
        w1_rows = [sb(f"w1_rows{p}", [P, FB, P]) for p in range(2)]
        w2_rows = [sb(f"w2_rows{p}", [P, FF]) for p in range(2)]
        w1 = [sb(f"w1_{p}", [P, FF]) for p in range(2)]
        w2 = [sb(f"w2_{p}", [P, FB, P]) for p in range(2)]
        hidden = [sb(f"hidden{p}", [P, FB, CH * P]) for p in range(2)]
        tokensT_hi = sb("tokensT_hi", [P, NB * P], F32R)
        tokensT_lo = sb("tokensT_lo", [P, NB * P], F32R)
        w1_hi = [sb(f"w1_hi{p}", [P, FF], F32R) for p in range(2)]
        w1_lo = [sb(f"w1_lo{p}", [P, FF], F32R) for p in range(2)]
        m_out = sb("m_out", [P, CH, P])
        STEPS = E * NC

        EXPERT_SEMS = sems("experts", """stat rstd normed turned_ps turned logit_ps logits chain joined
            gate_exp gate_in turned_gates_ps turned_gates spread bias_ps bias rows_in0 rows_in1 rows_ps rows h_ps
            hidden low w_split y_ps added stat_chain fin_beta done""")

        def mixture(n, layer):
            def before(k):
                return {"chain": 17, "gate_exp": 1, "gate_in": 1, "turned_gates_ps": 1, "turned_gates": 1, "spread": 1,
                        "rows_in0": 16 * E, "rows_in1": 16 * E, "rows_ps": 4 + 2 * E, "rows": 2 + 2 * E,
                        "h_ps": FB * STEPS, "hidden": FB + FB * STEPS, "turned": 2 * NC,
                        "w_split": 2 * E, "y_ps": 6 + STEPS, "added": 2 + STEPS,
                        "stat_chain": 2 * NC, "fin_beta": 0, "done": 0}.get(k, NC)

            s = run_twice(EXPERT_SEMS, before, layer == 1)
            s.n, s.layer = n, layer
            s.src = x if layer else y
            s.acc = y if layer else x
            return s

        def pe_mixture(pe, s):
            after_previous(pe, s.n)

            def transpose_tokens(c):
                pe.wait_ge(s["normed"], c + 1 + s.past["normed"])
                for t in range(CH):
                    mm = nc.tensor.transpose(quarters(c)[:, t, :], m_normed[c][:, t, :], ident[:, :])
                mm.then_inc(s["turned_ps"], 1)

            def gate_logits(c):
                pe.wait_ge(s["turned"], 2 * c + 1 + s.past["turned"])
                if c >= 2 and s.layer == 0:
                    pe.wait_ge(s["rows"], 4 + s.past["rows"])
                for t in range(CH):
                    b = CH * c + t
                    mm = nc.tensor.matmul(bank[:, 4 + c, E * t:E * (t + 1)], tokensT[:, b * P:(b + 1) * P],
                                          gate_w[:, s.layer, :], start=True, stop=True)
                mm.then_inc(s["logit_ps"], 1)

            def turn(e, p, pair):
                pe.wait_ge((s["rows_in0"], s["rows_in1"])[p], 32 * (pair + 1) + s.past["rows_in0"])
                pe.wait_ge(s["rows"], 2 * e + 2 + s.past["rows"])
                for f in range(FB):
                    mm = nc.tensor.transpose(quarters(6)[:, f, :], w1_rows[p][:, f, :], ident[:, :])
                mm.then_inc(s["rows_ps"], 1)
                for f in range(FB):
                    mm = nc.tensor.transpose(quarters(7)[:, f, :], w2_rows[p][:, f * P:(f + 1) * P], ident[:, :])
                mm.then_inc(s["rows_ps"], 1)

            for c in range(NC - 1):
                transpose_tokens(c)
            if s.layer == 0:
                turn(0, 0, 0)
            for c in range(NC - 2):
                gate_logits(c)
            transpose_tokens(NC - 1)
            for c in range(NC - 2, NC):
                gate_logits(c)

            def up(e, p, pair, c):
                step = NC * e + c
                if c == 0:
                    pe.wait_ge(s["w_split"], 2 * e + 2 + s.past["w_split"])
                chunk = slice(c * CH * P, (c + 1) * CH * P)
                for f in range(FB):
                    cols_f = slice(f * P, (f + 1) * P)
                    pe.wait_ge(s["hidden"], FB * step + f + 1 + s.past["hidden"])
                    nc.tensor.matmul(bank[:, f, :], w1_hi[p][:, cols_f], tokensT_hi[:, chunk], start=True, stop=False)
                    nc.tensor.matmul(bank[:, f, :], w1_hi[p][:, cols_f], tokensT_lo[:, chunk], start=False, stop=False)
                    nc.tensor.matmul(bank[:, f, :], w1_lo[p][:, cols_f], tokensT_hi[:, chunk], start=False,
                                     stop=True).then_inc(s["h_ps"], 1)

            def down(e, p, c):
                step = NC * e + c
                pe.wait_ge(s["hidden"], FB * step + 2 * FB + s.past["hidden"])
                pe.wait_ge(s["added"], step + 1 + s.past["added"])
                for t in range(CH):
                    for f in range(FB):
                        mm = nc.tensor.matmul(quarters(4 + c % 2)[:, t, :], hidden[c % 2][:, f, t * P:(t + 1) * P],
                                              w2[p][:, f, :], start=(f == 0), stop=(f == FB - 1))
                mm.then_inc(s["y_ps"], 1)

            def gate_biases():
                pe.wait_ge(s["gate_in"], 1 + s.past["gate_in"])
                nc.tensor.transpose(bank[:, 6, 0:P], gates[:, :, :].rearrange("p b e -> p (b e)"),
                                    ident[:, :]).then_inc(s["turned_gates_ps"], 1)
                pe.wait_ge(s["turned_gates"], 1 + s.past["turned_gates"])
                pe.wait_ge(s["spread"], 1 + s.past["spread"])
                for c in range(NC):
                    if c >= 2:
                        pe.wait_ge(s["bias"], c - 1 + s.past["bias"])
                    nc.tensor.matmul(bank[:, 6 + c % 2, :], gatesT[:, :], b2_spread[:, CH * c:CH * c + CH, :],
                                     start=True, stop=True).then_inc(s["bias_ps"], 1)

            def expert(e, p, pair, more, first=False):
                for c in range(NC):
                    if c == 1 and more and s.layer == 0:
                        if first:
                            pe.wait_ge(s["bias"], NC + s.past["bias"])
                        turn(e + 1, 1 - p, pair + p)
                    down(e, p, c)
                    if c == 0 and first:
                        gate_biases()
                    if c + 2 < NC:
                        up(e, p, pair, c + 2)
                    elif more:
                        up(e + 1, 1 - p, pair + p, c + 2 - NC)

            pe.wait_ge(s["logits"], NC + s.past["logits"])
            pe.wait_ge(s["low"], NC + s.past["low"])
            up(0, 0, 0, 0)
            up(0, 0, 0, 1)
            expert(0, 0, 0, True, True)
            expert(1, 1, 0, True)
            with pe.Fori(1, E // 2 - 1) as pair:
                expert(2 * pair, 0, pair, True)
                expert(2 * pair + 1, 1, pair, True)
            expert(E - 2, 0, E // 2 - 1, True)
            expert(E - 1, 1, E // 2 - 1, False)

        def sp_mixture(sp, s):
            after_previous(sp, s.n)

            def load(e, p):
                arrived = (s["rows_in0"], s["rows_in1"])[p]
                if s.layer == 0:
                    sp.wait_ge(s["rows_ps"], 2 * e + 2 + s.past["rows_ps"])
                    sp.dma_start(w1_rows[p][:, :, :], a["L0_ffn_fc1_w"][e, :, :].rearrange("(c q) d -> q c d", q=P)).then_inc(arrived, 16)
                    sp.dma_start(w2_rows[p][:, :], a["L0_ffn_fc2_w"][e, :, :]).then_inc(arrived, 16)
                else:
                    sp.wait_ge(s["y_ps"], 4 * e + 2 + s.past["y_ps"])
                    sp.dma_start(w1[p][:, :], a["L1_ffn_W1"][e, :, :]).then_inc(arrived, 16)
                    sp.dma_start(w2[p][:, :, :], a["L1_ffn_W2"][e, :, :].rearrange("(c q) d -> q c d", q=P)).then_inc(arrived, 16)

            sp.sem_inc(s["rows_ps"], 4)
            sp.sem_inc(s["y_ps"], 6)
            with sp.Fori(0, E // 2) as pair:
                load(2 * pair, 0)
                load(2 * pair + 1, 1)

        def act_mixture(act, s):
            after_previous(act, s.n)
            act.sem_inc(s["hidden"], FB)

            affine = {} if s.layer else dict(scale=cols[:, C_LN2W:C_LN2W + 1], bias=cols[:, C_LN2B:C_LN2B + 1])
            for c in range(NC):
                act.wait_ge(s["turned_ps"], c + 1 + s.past["turned_ps"])
                nc.scalar.activation(tokensT[:, c * CH * P:(c + 1) * CH * P], bank[:, c, :],
                                     ACT.Copy if s.layer else ACT.Identity, **affine).then_inc(s["turned"], 1)
                nc.scalar.activation(tokensT_hi[:, c * CH * P:(c + 1) * CH * P], bank[:, c, :],
                                     ACT.Copy if s.layer else ACT.Identity, **affine).then_inc(s["turned"], 1)
            if s.layer == 0:
                act.wait_ge(s["chain"], 12 + s.past["chain"])
                nc.scalar.activation(gate_col[3][:, :], gate_col[2][:, :], ACT.Exp).then_inc(s["gate_exp"], 1)
            else:
                act.wait_ge(s["chain"], 2 + s.past["chain"])
                nc.scalar.activation(gate_tmp[1][:, :, :], gate_tmp[0][:, :, :], ACT.Exp).then_inc(s["gate_exp"], 1)

            def gelus(step, col0, c, first=False):
                for f in range(FB):
                    act.wait_ge(s["h_ps"], FB * step + f + 1 + s.past["h_ps"])
                    if f == 0 and not first:
                        act.wait_ge(s["y_ps"], step + 5 + s.past["y_ps"])
                    take(act, L["passed"])
                    nc.scalar.activation(hidden[c % 2][:, f, :], bank[:, f, :], ACT.Gelu,
                                         bias=cols[:, bass.ds(col0 + f, 1)]).then_inc(s["hidden"], 1)

            for c in range(2):
                gelus(c, 32 * s.layer, c, True)
            act.wait_ge(s["turned_gates_ps"], 1 + s.past["turned_gates_ps"])
            nc.scalar.activation(gatesT[:, :], bank[:, 6, 0:P], ACT.Copy).then_inc(s["turned_gates"], 1)
            for c in range(2, NC):
                gelus(c, 32 * s.layer, c)
            for c in range(NC):
                gelus(NC + c, 32 * s.layer + FB, c)
            with act.Fori(1, E // 2) as pair:
                for p in range(2):
                    for c in range(NC):
                        gelus(2 * NC * pair + (NC * p + c), 2 * FB * pair + (32 * s.layer + FB * p), c)

        def pool_mixture(pool, s):
            for c in range(NC):
                pool.wait_ge(s["stat"], c + 1 + s.past["stat"])
                nc.gpsimd.tensor_tensor(f_rstd[:, c % 2, :], f_var[:, c % 2, :], minus_half[:, 0:CH],
                                        ALU.pow).then_inc(s["rstd"], 1)
            after_previous(pool, s.n)

            def split(e, p, pair):
                if s.layer == 0:
                    pool.wait_ge(s["rows"], 2 * e + 4 + s.past["rows"])
                else:
                    pool.wait_ge((s["rows_in0"], s["rows_in1"])[p], 32 * (pair + 1) + s.past["rows_in0"])
                take(pool, L["passed"])
                nc.gpsimd.tensor_copy(w1_hi[p][:, :], w1[p][:, :]).then_inc(s["w_split"], 1)
                pool.wait_ge(s["w_split"], 2 * e + 1 + s.past["w_split"])
                nc.gpsimd.tensor_tensor(w1_lo[p][:, :], w1[p][:, :], w1_hi[p][:, :], ALU.subtract).then_inc(s["w_split"], 1)

            split(0, 0, 0)
            nc.gpsimd.tensor_tensor(b2_spread[:, :, :], b2_rep[:, s.layer, :].unsqueeze(1).to_broadcast([P, NB, P]),
                                    head_of[:, :].unsqueeze(2).to_broadcast([P, NB, P]), ALU.mult).then_inc(s["spread"], 1)
            if s.layer == 0:
                for c in range(NC):
                    xc = x[:, CH * c:CH * (c + 1), :]
                    nc.gpsimd.tensor_tensor(xc, xc, y[:, CH * c:CH * (c + 1), :], ALU.add).then_inc(s["joined"], 1)
            if s.layer:
                pool.wait_ge(s["normed"], NC + s.past["normed"])
                for c in range(NC):
                    xc = x[:, CH * c:CH * (c + 1), :]
                    nc.gpsimd.tensor_tensor(xc, xc, beta[:, :].unsqueeze(1).to_broadcast([P, CH, P]), ALU.add).then_inc(s["fin_beta"], 1)
            split(1, 1, 0)
            with pool.Fori(1, E // 2) as pair:
                split(2 * pair, 0, pair)
                split(2 * pair + 1, 1, pair)
            if s.layer:
                for c in range(NC):
                    pool.wait_ge(s["stat"], NC + c + 1 + s.past["stat"])
                    nc.gpsimd.tensor_tensor(f_rstd[:, c % 2, :], f_var[:, c % 2, :], minus_half[:, 0:CH],
                                            ALU.pow).then_inc(s["rstd"], 1)

        def expert_tokens(dve, s, written, past):
            def stats(c):
                p = c % 2
                dve.wait_ge(written, CH * (c + 1) + past)
                for t in range(CH):
                    ins = nc.vector.bn_stats(f_stats[:, t, :], s.src[:, CH * c + t, :])
                ins.then_inc(s["stat_chain"], 1)
                dve.wait_ge(s["stat_chain"], 2 * c + 1 + s.past["stat_chain"])
                for t in range(CH):
                    ins = nc.vector.bn_aggr(f_moments[:, p, t, :], f_stats[:, t, :])
                ins.then_inc(s["stat_chain"], 1)
                dve.wait_ge(s["stat_chain"], 2 * c + 2 + s.past["stat_chain"])
                nc.vector.tensor_scalar(f_var[:, p, :], f_moments[:, p, :, 1], EPS, None, ALU.add).then_inc(s["stat"], 1)

            def normalise(c):
                p = c % 2
                dve.wait_ge(s["rstd"], c + 1 + s.past["rstd"])
                for t in range(CH):
                    ins = nc.vector.tensor_scalar(m_normed[c][:, t, :], s.src[:, CH * c + t, :], f_moments[:, p, t, 0:1],
                                                  f_rstd[:, p, t:t + 1], ALU.subtract, ALU.mult)
                ins.then_inc(s["normed"], 1)

            return stats, normalise

        def ahead(dve, s, written, past):
            stats, normalise = expert_tokens(dve, s, written, past)

            def second():
                normalise(0)
                stats(1)

            def third():
                normalise(1)
                stats(2)

            return [lambda: stats(0), second] + ([] if s.layer else [third])

        def dve_mixture(dve, s):
            stats, normalise = expert_tokens(dve, s, *((W["done"], 0) if s.layer else (C0["done"], C0.past["done"])))
            if s.layer:
                normalise(1)
                stats(2)
            normalise(2)
            stats(3)
            normalise(3)
            after_previous(dve, s.n)
            dve.sem_inc(s["added"], 2)
            dve.sem_inc(s["rows"], 2)

            def take_logits(c):
                dve.wait_ge(s["logit_ps"], c + 1 + s.past["logit_ps"])
                src = bank[:, 4 + c, 0:CH * E].rearrange("p (t e) -> p t e", e=E)
                dst = logits[:, CH * c:CH * (c + 1), :]
                if s.layer == 0:
                    nc.vector.tensor_copy(dst, src).then_inc(s["logits"], 1)
                else:
                    nc.vector.tensor_tensor(dst, src, gate_b[:, :].unsqueeze(1).to_broadcast([P, CH, E]),
                                            ALU.add).then_inc(s["logits"], 1)

            def low_tokens(c):
                dve.wait_ge(s["turned"], 2 * c + 2 + s.past["turned"])
                chunk = slice(c * CH * P, (c + 1) * CH * P)
                nc.vector.tensor_tensor(tokensT_lo[:, chunk], tokensT[:, chunk], tokensT_hi[:, chunk],
                                        ALU.subtract).then_inc(s["low"], 1)

            def take_rows(e, p):
                dve.wait_ge(s["y_ps"], 4 * e + 2 + s.past["y_ps"])
                dve.wait_ge(s["rows_ps"], 2 * e + 5 + s.past["rows_ps"])
                nc.vector.tensor_copy(w1[p][:, :].rearrange("p (n c) -> p n c", c=P), quarters(6)).then_inc(s["rows"], 1)
                dve.wait_ge(s["rows_ps"], 2 * e + 6 + s.past["rows_ps"])
                nc.vector.tensor_copy(w2[p][:, :, :], quarters(7)).then_inc(s["rows"], 1)

            if s.layer == 0:
                take_rows(0, 0)
            for c in range(NC):
                low_tokens(c)
                take_logits(c)

            dve.wait_ge(s["logits"], NC + s.past["logits"])
            made = []

            def make(instruction):
                made.append(1)
                instruction.then_inc(s["chain"], 1)
                dve.wait_ge(s["chain"], len(made) + s.past["chain"])

            def over(col):
                return col[:, :].unsqueeze(2).to_broadcast([P, NB, E])

            V = nc.vector
            scores = logits
            if s.layer:
                make(V.tensor_reduce(gate_col[0][:, :], logits[:, :, :], AX.X, ALU.max))
                make(V.tensor_tensor(gate_tmp[0][:, :, :], logits[:, :, :], over(gate_col[0]), ALU.subtract))
                dve.wait_ge(s["gate_exp"], 1 + s.past["gate_exp"])
                make(V.tensor_reduce(gate_col[0][:, :], gate_tmp[1][:, :, :], AX.X, ALU.add))
                make(V.reciprocal(gate_col[1][:, :], gate_col[0][:, :]))
                make(V.tensor_tensor(logits[:, :, :], gate_tmp[1][:, :, :], over(gate_col[1]), ALU.mult))

            def pick(values, best, hot):
                make(V.tensor_reduce(best[:, :], values[:, :, :], AX.X, ALU.max))
                make(V.tensor_tensor(gate_tmp[2][:, :, :], values[:, :, :], over(best), ALU.is_equal))
                make(V.tensor_tensor(gate_tmp[3][:, :, :], gate_tmp[2][:, :, :],
                                     countdown[:, :].unsqueeze(1).to_broadcast([P, NB, E]), ALU.mult))
                make(V.tensor_reduce(gate_col[4][:, :], gate_tmp[3][:, :, :], AX.X, ALU.max))
                make(V.tensor_tensor(hot[:, :, :], gate_tmp[3][:, :, :], over(gate_col[4]), ALU.is_equal))

            pick(scores, gate_col[0], first_hot)
            make(V.scalar_tensor_tensor(out=gate_tmp[0][:, :, :], in0=first_hot[:, :, :], scalar=NEG, in1=scores[:, :, :],
                                        op0=ALU.mult, op1=ALU.add))
            pick(gate_tmp[0], gate_col[1], second_hot)
            if s.layer == 0:
                make(V.tensor_tensor(gate_col[2][:, :], gate_col[1][:, :], gate_col[0][:, :], ALU.subtract))
                dve.wait_ge(s["gate_exp"], 1 + s.past["gate_exp"])
                make(V.tensor_scalar(gate_col[4][:, :], gate_col[3][:, :], 1.0, None, ALU.add))
                make(V.reciprocal(gate_col[0][:, :], gate_col[4][:, :]))
                make(V.tensor_tensor(gate_col[1][:, :], gate_col[3][:, :], gate_col[0][:, :], ALU.mult))
            else:
                make(V.tensor_tensor(gate_col[2][:, :], gate_col[1][:, :], gate_col[0][:, :], ALU.add))
                make(V.tensor_scalar(gate_col[3][:, :], gate_col[2][:, :], 1e-8, None, ALU.add))
                make(V.reciprocal(gate_col[5][:, :], gate_col[3][:, :]))
                make(V.tensor_tensor(gate_col[0][:, :], gate_col[0][:, :], gate_col[5][:, :], ALU.mult))
                make(V.tensor_tensor(gate_col[1][:, :], gate_col[1][:, :], gate_col[5][:, :], ALU.mult))
            make(V.tensor_tensor(gate_tmp[0][:, :, :], first_hot[:, :, :], over(gate_col[0]), ALU.mult))
            make(V.tensor_tensor(gate_tmp[1][:, :, :], second_hot[:, :, :], over(gate_col[1]), ALU.mult))
            V.tensor_tensor(gates[:, :, :], gate_tmp[0][:, :, :], gate_tmp[1][:, :, :], ALU.add).then_inc(s["gate_in"], 1)

            if s.layer == 0:
                dve.wait_ge(s["joined"], NC)
            for c in range(NC):
                dve.wait_ge(s["bias_ps"], c + 1 + s.past["bias_ps"])
                acc = s.acc[:, CH * c:CH * c + CH, :]
                if s.layer == 0:
                    V.tensor_tensor(acc, quarters(6 + c % 2), acc, ALU.add).then_inc(s["bias"], 1)
                else:
                    V.tensor_copy(acc, quarters(6 + c % 2)).then_inc(s["bias"], 1)
            dve.wait_ge(s["bias"], NC + s.past["bias"])

            def add(e, c):
                step = NC * e + c
                dve.wait_ge(s["y_ps"], step + 7 + s.past["y_ps"])
                dve.wait_ge(s["added"], step + 2 + s.past["added"])
                for t in range(CH):
                    b = CH * c + t
                    ins = V.scalar_tensor_tensor(out=s.acc[:, b, :], in0=quarters(4 + c % 2)[:, t, :],
                                                 scalar=gates[:, b, bass.ds(e, 1)], in1=s.acc[:, b, :],
                                                 op0=ALU.mult, op1=ALU.add)
                ins.then_inc(s["added"], 1)

            def expert(e, p, take_next):
                for c in range(NC):
                    if c == 1 and take_next:
                        take_rows(e + 1, 1 - p)
                    add(e, c)

            with dve.Fori(0, E // 2 - 1) as pair:
                expert(2 * pair, 0, s.layer == 0)
                expert(2 * pair + 1, 1, s.layer == 0)
            expert(E - 2, 0, s.layer == 0)
            if s.layer == 0:
                expert(E - 1, 1, False)
                return

            def sum_stats(c):
                p = c % 2
                dve.wait_ge(s["added"], STEPS - NC + c + 3 + s.past["added"])
                for t in range(CH):
                    ins = V.bn_stats(f_stats[:, t, :], y[:, CH * c + t, :])
                ins.then_inc(s["stat_chain"], 1)
                dve.wait_ge(s["stat_chain"], 2 * NC + 2 * c + 1 + s.past["stat_chain"])
                for t in range(CH):
                    ins = V.bn_aggr(f_moments[:, p, t, :], f_stats[:, t, :])
                ins.then_inc(s["stat_chain"], 1)
                dve.wait_ge(s["stat_chain"], 2 * NC + 2 * c + 2 + s.past["stat_chain"])
                V.tensor_scalar(f_var[:, p, :], f_moments[:, p, :, 1], EPS, None, ALU.add).then_inc(s["stat"], 1)

            def finish(c):
                p = c % 2
                dve.wait_ge(s["rstd"], NC + c + 1 + s.past["rstd"])
                if c:
                    dve.wait_ge(s["done"], c)
                for t in range(CH):
                    ins = V.tensor_scalar(m_out[:, t, :], y[:, CH * c + t, :], f_moments[:, p, t, 0:1], f_rstd[:, p, t:t + 1],
                                          ALU.subtract, ALU.mult)
                make(ins)
                make(V.tensor_tensor(m_out[:, :, :], m_out[:, :, :], gamma[:, :].unsqueeze(1).to_broadcast([P, CH, P]), ALU.mult))
                dve.wait_ge(s["fin_beta"], NC)
                xc = x[:, CH * c:CH * (c + 1), :]
                V.tensor_tensor(xc, xc, m_out[:, :, :], ALU.add).then_inc(s["done"], 1)

            for c in range(NC):
                add(E - 1, c)
                sum_stats(c)
                if c:
                    finish(c - 1)
            finish(NC - 1)

        M0, M1 = mixture(3, 0), mixture(6, 1)
        all_done.append((M0["added"], 2 + STEPS))
        all_done.append((LA["done"], NB))
        all_done.append((W["done"], NB))
        all_done.append((M1["done"], NC))

        block = ctx.enter_context(nc.Block())
        D = sems("end", "stored")

        @block.sync
        def _(sp):
            sp_load(sp)
            sp_narrow(sp, X0)
            sp_narrow(sp, C0)
            sp_mixture(sp, M0)
            sp_wide(sp)
            sp_mixture(sp, M1)

            for c in range(NC):
                sp.wait_ge(M1["done"], c + 1)
                chunk = slice(CH * c, CH * (c + 1))
                sp.dma_start(out[chunk, :, :].rearrange("b t d -> t b d"), x[:, chunk, :]).then_inc(D["stored"], 16)
            sp.wait_ge(D["stored"], 16 * NC)

        @block.scalar
        def _(act):
            act_load(act)
            act_phase(act)
            act_narrow(act, X0)
            act_narrow(act, C0)
            act_mixture(act, M0)
            act_linear(act)
            act_wide(act)
            act_mixture(act, M1)

        @block.gpsimd
        def _(pool):
            pool_load(pool)
            pool_phase(pool)
            pool_narrow(pool, X0)
            pool_narrow(pool, C0)
            pool_mixture(pool, M0)
            pool_linear(pool)
            pool_wide(pool)
            pool_mixture(pool, M1)

        @block.vector
        def _(dve):
            dve_phase(dve)
            dve_narrow(dve, X0)
            dve_narrow(dve, C0)
            dve_mixture(dve, M0)
            dve_linear(dve)
            dve_wide(dve)
            dve_mixture(dve, M1)

        @block.tensor
        def _(pe):
            pe_load(pe)
            pe_phase(pe)
            pe_narrow(pe, X0)
            pe_narrow(pe, C0)
            pe_mixture(pe, M0)
            pe_linear(pe)
            pe_wide(pe)
            pe_mixture(pe, M1)


_INS = ['x', 'ctx_1024', 'L0_attn_Wq', 'L0_attn_bq', 'L0_attn_Wk', 'L0_attn_bk', 'L0_attn_Wv', 'L0_attn_bv',
        'L0_attn_Wo', 'L0_attn_bo', 'L0_xattn_Wq', 'L0_xattn_Wk', 'L0_xattn_Wv', 'L0_xattn_Wo', 'L0_ffn_ln1_w',
        'L0_ffn_ln1_b', 'L0_ffn_ln2_w', 'L0_ffn_ln2_b', 'L0_ffn_Wqkv', 'L0_ffn_bqkv', 'L0_ffn_Wo', 'L0_ffn_bo',
        'L0_ffn_gate_W', 'L0_ffn_fc1_w', 'L0_ffn_fc1_b', 'L0_ffn_fc2_w', 'L0_ffn_fc2_b', 'L1_attn_w_qkv',
        'L1_attn_w_out', 'L1_xattn_Wq', 'L1_xattn_Wk', 'L1_xattn_Wv', 'L1_xattn_Wo', 'L1_ffn_Wg', 'L1_ffn_bg',
        'L1_ffn_W1', 'L1_ffn_b1', 'L1_ffn_W2', 'L1_ffn_b2', 'L1_ffn_gamma', 'L1_ffn_beta']
_OUTS = [((16, 128, 128), 'float32')]


def kernel(**inputs):
    import numpy as _np
    import concourse.bacc as _bacc
    from concourse import mybir as _mybir
    from concourse.bass_utils import run_bass_kernel_spmd as _run

    nc = _bacc.Bacc("TRN2", target_bir_lowering=False, num_devices=1)
    arrays, args = {}, {}
    for name in _INS:
        a = _np.ascontiguousarray(inputs[name])
        arrays[f"in_{name}"] = a
        args[name] = nc.dram_tensor(f"in_{name}", a.shape, _mybir.dt.from_np(a.dtype), kind="ExternalInput").ap()
    shape, dtype = _OUTS[0]
    out = nc.dram_tensor("out_0", shape, _mybir.dt.from_np(_np.dtype(dtype)), kind="ExternalOutput").ap()
    decoder(nc, args, out)
    r = _run(nc, [arrays], core_ids=[0])
    return r.results[0]["out_0"]
```
